# Optimizing a Trainium2 kernel written in Bass

```python
import numpy as np
import jax
import jax.numpy as jnp

def _softmax(x, axis=-1):
    return jax.nn.softmax(x, axis=axis)

def _gelu(x):
    return jax.nn.gelu(x, approximate=True)

def _silu(x):
    return jax.nn.silu(x)

def _sigmoid(x):
    return jax.nn.sigmoid(x)

def _layernorm(x, axis=-1, eps=1e-05):
    m = jnp.mean(x, axis=axis, keepdims=True)
    v = jnp.var(x, axis=axis, keepdims=True)
    return (x - m) / jnp.sqrt(v + eps)

def _scatter_add(tgt, idx, src, axis=0):
    return tgt.at[idx].add(src)

def _segment_sum(src, seg, n):
    return jax.ops.segment_sum(src, seg, n)
kernel_name = 'mk_gps_d2_gnn_r8_9a125d'

def setup_inputs(seed: int=0):
    np.random.seed(seed)
    _w = jnp.asarray

    def _rec_inputs():
        import jax
        import jax.numpy as jnp
        _gk = jax.random.key(seed)
        x = -0.0005963 + 1.001 * jax.random.normal(jax.random.fold_in(_gk, 1), (384, 1024), jnp.float32)
        src = jax.random.randint(jax.random.fold_in(_gk, 2), (6144,), 0, 384, jnp.int32)
        dst = jnp.minimum((384 * jax.random.uniform(jax.random.fold_in(_gk, 3), (6144,)) ** 2.0).astype(jnp.int32), 3071)
        _o = jnp.argsort(dst, stable=True)
        src = src[_o]
        dst = dst[_o]
        edge_type_5 = jax.random.randint(jax.random.fold_in(_gk, 13), (6144,), 0, 5, jnp.int32)
        return (x, src, dst, edge_type_5)
    x, src, dst, edge_type_5 = _rec_inputs()

    def _L0_gnn_setup():
        import jax, jax.numpy as jnp
        import numpy as np
        N = 384
        E = 12288
        IN_F = 1024
        OUT_F = 1024
        H = 16
        D = OUT_F // H
        NUM_ETYPES = 4

        def _build_mask(edge_index, edge_type, edge_type_weights, dtype):
            src, dst = (edge_index[0], edge_index[1])
            w = jax.nn.softplus(edge_type_weights)
            mask = jnp.full((N, N), -jnp.inf, dtype=dtype)
            mask = mask.at[src, dst].set(w[edge_type - 1])
            diag = jnp.diagonal(mask)
            idx = jnp.arange(N)
            mask = mask.at[idx, idx].set(jnp.where(jnp.isneginf(diag), w[3], diag))
            return mask
        key = jax.random.key(seed)
        ks = jax.random.split(key, 20)
        p = lambda k, shape: jax.random.normal(k, shape, dtype=jnp.float32) * 0.02
        return {'x': jax.random.normal(ks[0], (N, IN_F), dtype=jnp.float32), 'edge_index': jax.random.randint(ks[1], (2, E), 0, N), 'edge_type': jax.random.randint(ks[2], (E,), 1, NUM_ETYPES + 1), 'edge_type_weights': jnp.ones((NUM_ETYPES,), jnp.float32) + 0.1 * jax.random.normal(ks[3], (NUM_ETYPES,), dtype=jnp.float32), 'wq': p(ks[4], (OUT_F, IN_F)), 'bq': p(ks[5], (OUT_F,)), 'wk': p(ks[6], (OUT_F, IN_F)), 'bk': p(ks[7], (OUT_F,)), 'wv': p(ks[8], (OUT_F, IN_F)), 'bv': p(ks[9], (OUT_F,)), 'wiq': p(ks[10], (OUT_F, OUT_F)), 'biq': p(ks[11], (OUT_F,)), 'wik': p(ks[12], (OUT_F, OUT_F)), 'bik': p(ks[13], (OUT_F,)), 'wiv': p(ks[14], (OUT_F, OUT_F)), 'biv': p(ks[15], (OUT_F,)), 'wo': p(ks[16], (OUT_F, OUT_F)), 'bo': p(ks[17], (OUT_F,))}
    _L0_gnn_all = _L0_gnn_setup()
    _L0_gnn_in = {k: v for k, v in _L0_gnn_all.items() if k in ('edge_type_weights', 'wq', 'bq', 'wk', 'bk', 'wv', 'bv', 'wiq', 'biq', 'wik', 'bik', 'wiv', 'biv', 'wo', 'bo')}
    del _L0_gnn_all

    def _L0_mix_setup():
        import jax, jax.numpy as jnp
        import numpy as np
        B, N, QD = (4, 512, 1024)
        HEADS, DIM_HEAD = (8, 64)
        HID = HEADS * DIM_HEAD
        SCALE = DIM_HEAD ** (-0.5)
        key = jax.random.key(seed)
        ks = jax.random.split(key, 6)
        s_in = 1.0 / np.sqrt(QD)
        s_h = 1.0 / np.sqrt(HID)
        return {'x': jax.random.normal(ks[0], (B, N, QD), dtype=jnp.float32), 'Wq': jax.random.uniform(ks[1], (QD, HID), jnp.float32, -s_in, s_in), 'Wk': jax.random.uniform(ks[2], (QD, HID), jnp.float32, -s_in, s_in), 'Wv': jax.random.uniform(ks[3], (QD, HID), jnp.float32, -s_in, s_in), 'Wo': jax.random.uniform(ks[4], (HID, QD), jnp.float32, -s_h, s_h), 'bo': jax.random.uniform(ks[5], (QD,), jnp.float32, -s_h, s_h)}
    _L0_mix_all = _L0_mix_setup()
    _L0_mix_in = {k: v for k, v in _L0_mix_all.items() if k in ('Wq', 'Wk', 'Wv', 'Wo', 'bo')}
    del _L0_mix_all

    def _L0_ffn_setup():
        import jax, jax.numpy as jnp
        import numpy as np
        EPS = 1e-05

        def rmsnorm(x):
            return x * jax.lax.rsqrt(jnp.mean(x * x, axis=-1, keepdims=True) + EPS)

        def act_quant(x):
            scale = 127.0 / jnp.clip(jnp.max(jnp.abs(x), axis=-1, keepdims=True), 1e-05)
            q = jnp.clip(jnp.round(x * scale), -128.0, 127.0) / scale
            return x + jax.lax.stop_gradient(q - x)

        def weight_quant(w):
            scale = 1.0 / jnp.clip(jnp.mean(jnp.abs(w)), 1e-05)
            q = jnp.clip(jnp.round(w * scale), -1.0, 1.0) / scale
            return w + jax.lax.stop_gradient(q - w)

        def bitlinear(x, w, b):
            xq = act_quant(rmsnorm(x))
            wq = weight_quant(w)
            return jnp.einsum('bsd,fd->bsf', xq, wq) + b
        key = jax.random.key(seed)
        k0, k1, k2 = jax.random.split(key, 3)
        B, S, D, F = (2, 1024, 1024, 512)
        x = jax.random.normal(k0, (B, S, D), dtype=jnp.float32)
        w1 = jax.random.normal(k1, (F, D), dtype=jnp.float32) * (1.0 / np.sqrt(D))
        b1 = jnp.zeros((F,), dtype=jnp.float32)
        w2 = jax.random.normal(k2, (D, F), dtype=jnp.float32) * (1.0 / np.sqrt(F))
        b2 = jnp.zeros((D,), dtype=jnp.float32)
        return {'x': x, 'w1': w1, 'b1': b1, 'w2': w2, 'b2': b2}
    _L0_ffn_all = _L0_ffn_setup()
    _L0_ffn_in = {k: v for k, v in _L0_ffn_all.items() if k in ('w1', 'b1', 'w2', 'b2')}
    del _L0_ffn_all

    def _L1_gnn_setup():
        import jax, jax.numpy as jnp
        import numpy as np
        N_DIAS = 64
        L = 60
        N = N_DIAS * L
        E = N_DIAS * L * (L - 1)
        D = 1024
        H = 512
        K = 4

        def _build_edges():
            idx = np.arange(L)
            src = np.repeat(idx, L)
            dst = np.tile(idx, L)
            m = src != dst
            src, dst = (src[m], dst[m])
            offs = (np.arange(N_DIAS) * L)[:, None]
            row = (src[None, :] + offs).reshape(-1)
            col = (dst[None, :] + offs).reshape(-1)
            return (row.astype(np.int32), col.astype(np.int32))
        key = jax.random.key(seed)
        k0, k1, k2 = jax.random.split(key, 3)
        row, col = _build_edges()
        return {'emotions_feat': jax.random.normal(k0, (N, D), jnp.float32), 'W1': jax.random.normal(k1, (D, H), jnp.float32) * 0.02, 'b1': jnp.zeros((H,), jnp.float32), 'Wg': jax.random.normal(k2, (K, 2 * H, 1), jnp.float32) * 0.02, 'bg': jnp.zeros((K, 1), jnp.float32), 'row': jnp.asarray(row), 'col': jnp.asarray(col)}
    _L1_gnn_all = _L1_gnn_setup()
    _L1_gnn_in = {k: v for k, v in _L1_gnn_all.items() if k in ('W1', 'b1', 'Wg', 'bg')}
    del _L1_gnn_all

    def _L1_mix_setup():
        import jax, jax.numpy as jnp
        import numpy as np
        DIM = 1024
        HEADS = 16
        DIM_HEAD = 64
        key = jax.random.key(seed)
        ks = jax.random.split(key, 9)
        B, T = (4, 512)
        s = 1.0 / np.sqrt(DIM)
        x = jax.random.normal(ks[0], (B, T, DIM), dtype=jnp.float32)
        Wq = jax.random.normal(ks[1], (DIM, DIM), dtype=jnp.float32) * s
        bq = jax.random.normal(ks[2], (DIM,), dtype=jnp.float32) * 0.01
        Wk = jax.random.normal(ks[3], (DIM, DIM), dtype=jnp.float32) * s
        bk = jax.random.normal(ks[4], (DIM,), dtype=jnp.float32) * 0.01
        Wv = jax.random.normal(ks[5], (DIM, DIM), dtype=jnp.float32) * s
        bv = jax.random.normal(ks[6], (DIM,), dtype=jnp.float32) * 0.01
        Wp = jax.random.normal(ks[7], (DIM, DIM), dtype=jnp.float32) * s
        bp = jax.random.normal(ks[8], (DIM,), dtype=jnp.float32) * 0.01
        return {'x': x, 'Wq': Wq, 'bq': bq, 'Wk': Wk, 'bk': bk, 'Wv': Wv, 'bv': bv, 'Wp': Wp, 'bp': bp}
    _L1_mix_all = _L1_mix_setup()
    _L1_mix_in = {k: v for k, v in _L1_mix_all.items() if k in ('Wq', 'bq', 'Wk', 'bk', 'Wv', 'bv', 'Wp', 'bp')}
    del _L1_mix_all

    def _L1_ffn_setup():
        import jax, jax.numpy as jnp
        import numpy as np
        TOP_K = 2
        N_EXPERTS = 8
        key = jax.random.key(seed)
        k_x, k_g, k_w1, k_w2 = jax.random.split(key, 4)
        B, S, d_in, d_hid, d_out, E = (8, 256, 1024, 256, 1024, N_EXPERTS)
        s_gate = float(np.sqrt(6.0 / (d_in + E)))
        s_w1 = float(np.sqrt(6.0 / (d_in + d_hid)))
        s_w2 = float(np.sqrt(6.0 / (d_hid + d_out)))
        x = jax.random.normal(k_x, (B, S, d_in), dtype=jnp.float32)
        gate_W = jax.random.uniform(k_g, (d_in, E), jnp.float32, -s_gate, s_gate)
        W1 = jax.random.uniform(k_w1, (E, d_in, d_hid), jnp.float32, -s_w1, s_w1)
        b1 = jnp.zeros((E, d_hid), jnp.float32)
        W2 = jax.random.uniform(k_w2, (E, d_hid, d_out), jnp.float32, -s_w2, s_w2)
        b2 = jnp.zeros((E, d_out), jnp.float32)
        return {'x': x, 'gate_W': gate_W, 'W1': W1, 'b1': b1, 'W2': W2, 'b2': b2}
    _L1_ffn_all = _L1_ffn_setup()
    _L1_ffn_in = {k: v for k, v in _L1_ffn_all.items() if k in ('gate_W', 'W1', 'b1', 'W2', 'b2')}
    del _L1_ffn_all
    return {'x': x, 'src': src, 'dst': dst, 'edge_type_5': edge_type_5, 'L0_gnn_edge_type_weights': _L0_gnn_in['edge_type_weights'], 'L0_gnn_wq': _L0_gnn_in['wq'], 'L0_gnn_bq': _L0_gnn_in['bq'], 'L0_gnn_wk': _L0_gnn_in['wk'], 'L0_gnn_bk': _L0_gnn_in['bk'], 'L0_gnn_wv': _L0_gnn_in['wv'], 'L0_gnn_bv': _L0_gnn_in['bv'], 'L0_gnn_wiq': _L0_gnn_in['wiq'], 'L0_gnn_biq': _L0_gnn_in['biq'], 'L0_gnn_wik': _L0_gnn_in['wik'], 'L0_gnn_bik': _L0_gnn_in['bik'], 'L0_gnn_wiv': _L0_gnn_in['wiv'], 'L0_gnn_biv': _L0_gnn_in['biv'], 'L0_gnn_wo': _L0_gnn_in['wo'], 'L0_gnn_bo': _L0_gnn_in['bo'], 'L0_mix_Wq': _L0_mix_in['Wq'], 'L0_mix_Wk': _L0_mix_in['Wk'], 'L0_mix_Wv': _L0_mix_in['Wv'], 'L0_mix_Wo': _L0_mix_in['Wo'], 'L0_mix_bo': _L0_mix_in['bo'], 'L0_ffn_w1': _L0_ffn_in['w1'], 'L0_ffn_b1': _L0_ffn_in['b1'], 'L0_ffn_w2': _L0_ffn_in['w2'], 'L0_ffn_b2': _L0_ffn_in['b2'], 'L1_gnn_W1': _L1_gnn_in['W1'], 'L1_gnn_b1': _L1_gnn_in['b1'], 'L1_gnn_Wg': _L1_gnn_in['Wg'], 'L1_gnn_bg': _L1_gnn_in['bg'], 'L1_mix_Wq': _L1_mix_in['Wq'], 'L1_mix_bq': _L1_mix_in['bq'], 'L1_mix_Wk': _L1_mix_in['Wk'], 'L1_mix_bk': _L1_mix_in['bk'], 'L1_mix_Wv': _L1_mix_in['Wv'], 'L1_mix_bv': _L1_mix_in['bv'], 'L1_mix_Wp': _L1_mix_in['Wp'], 'L1_mix_bp': _L1_mix_in['bp'], 'L1_ffn_gate_W': _L1_ffn_in['gate_W'], 'L1_ffn_W1': _L1_ffn_in['W1'], 'L1_ffn_b1': _L1_ffn_in['b1'], 'L1_ffn_W2': _L1_ffn_in['W2'], 'L1_ffn_b2': _L1_ffn_in['b2']}

def reference(x, src, dst, edge_type_5, L0_gnn_edge_type_weights, L0_gnn_wq, L0_gnn_bq, L0_gnn_wk, L0_gnn_bk, L0_gnn_wv, L0_gnn_bv, L0_gnn_wiq, L0_gnn_biq, L0_gnn_wik, L0_gnn_bik, L0_gnn_wiv, L0_gnn_biv, L0_gnn_wo, L0_gnn_bo, L0_mix_Wq, L0_mix_Wk, L0_mix_Wv, L0_mix_Wo, L0_mix_bo, L0_ffn_w1, L0_ffn_b1, L0_ffn_w2, L0_ffn_b2, L1_gnn_W1, L1_gnn_b1, L1_gnn_Wg, L1_gnn_bg, L1_mix_Wq, L1_mix_bq, L1_mix_Wk, L1_mix_bk, L1_mix_Wv, L1_mix_bv, L1_mix_Wp, L1_mix_bp, L1_ffn_gate_W, L1_ffn_W1, L1_ffn_b1, L1_ffn_W2, L1_ffn_b2):
    import jax
    import jax.numpy as jnp

    def _L0_gnn_ref(x, edge_index, edge_type, edge_type_weights, wq, bq, wk, bk, wv, bv, wiq, biq, wik, bik, wiv, biv, wo, bo):
        import jax, jax.numpy as jnp
        import numpy as np
        N = 384
        E = 12288
        IN_F = 1024
        OUT_F = 1024
        H = 16
        D = OUT_F // H
        NUM_ETYPES = 4

        def _build_mask(edge_index, edge_type, edge_type_weights, dtype):
            src, dst = (edge_index[0], edge_index[1])
            w = jax.nn.softplus(edge_type_weights)
            mask = jnp.full((N, N), -jnp.inf, dtype=dtype)
            mask = mask.at[src, dst].set(w[edge_type - 1])
            diag = jnp.diagonal(mask)
            idx = jnp.arange(N)
            mask = mask.at[idx, idx].set(jnp.where(jnp.isneginf(diag), w[3], diag))
            return mask
        q = x @ wq.T + bq
        k = x @ wk.T + bk
        v = x @ wv.T + bv
        q2 = (q @ wiq.T + biq).reshape(N, H, D).transpose(1, 0, 2)
        k2 = (k @ wik.T + bik).reshape(N, H, D).transpose(1, 0, 2)
        v2 = (v @ wiv.T + biv).reshape(N, H, D).transpose(1, 0, 2)
        mask = _build_mask(edge_index, edge_type, edge_type_weights, x.dtype)
        scale = 1.0 / np.sqrt(D).astype(np.float32)
        scores = jnp.einsum('hnd,hmd->hnm', q2, k2) * scale + mask[None]
        attn = jax.nn.softmax(scores, axis=-1)
        out = jnp.einsum('hnm,hmd->hnd', attn, v2)
        out = out.transpose(1, 0, 2).reshape(N, OUT_F)
        return out @ wo.T + bo

    def _L0_mix_ref(x, Wq, Wk, Wv, Wo, bo):
        import jax, jax.numpy as jnp
        import numpy as np
        B, N, QD = (4, 512, 1024)
        HEADS, DIM_HEAD = (8, 64)
        HID = HEADS * DIM_HEAD
        SCALE = DIM_HEAD ** (-0.5)
        b, n, _ = x.shape
        q = x @ Wq
        k = x @ Wk
        v = x @ Wv

        def split_heads(t):
            return t.reshape(b, n, HEADS, DIM_HEAD).transpose(0, 2, 3, 1)
        q = split_heads(q)
        k = split_heads(k)
        v = split_heads(v)
        q = jax.nn.softmax(q, axis=-2) * SCALE
        k = jax.nn.softmax(k, axis=-1)
        context = jnp.einsum('bhdn,bhen->bhde', k, v)
        out = jnp.einsum('bhde,bhdn->bhen', context, q)
        out = out.transpose(0, 3, 1, 2).reshape(b, n, HID)
        return out @ Wo + bo

    def _L0_ffn_ref(x, w1, b1, w2, b2):
        import jax, jax.numpy as jnp
        import numpy as np
        EPS = 1e-05

        def rmsnorm(x):
            return x * jax.lax.rsqrt(jnp.mean(x * x, axis=-1, keepdims=True) + EPS)

        def act_quant(x):
            scale = 127.0 / jnp.clip(jnp.max(jnp.abs(x), axis=-1, keepdims=True), 1e-05)
            q = jnp.clip(jnp.round(x * scale), -128.0, 127.0) / scale
            return x + jax.lax.stop_gradient(q - x)

        def weight_quant(w):
            scale = 1.0 / jnp.clip(jnp.mean(jnp.abs(w)), 1e-05)
            q = jnp.clip(jnp.round(w * scale), -1.0, 1.0) / scale
            return w + jax.lax.stop_gradient(q - w)

        def bitlinear(x, w, b):
            xq = act_quant(rmsnorm(x))
            wq = weight_quant(w)
            return jnp.einsum('bsd,fd->bsf', xq, wq) + b
        h = bitlinear(x, w1, b1)
        h = jax.nn.gelu(h, approximate=False)
        return bitlinear(h, w2, b2)

    def _L1_gnn_ref(emotions_feat, W1, b1, Wg, bg, row, col):
        import jax, jax.numpy as jnp
        import numpy as np
        N_DIAS = 64
        L = 60
        N = N_DIAS * L
        E = N_DIAS * L * (L - 1)
        D = 1024
        H = 512
        K = 4

        def _build_edges():
            idx = np.arange(L)
            src = np.repeat(idx, L)
            dst = np.tile(idx, L)
            m = src != dst
            src, dst = (src[m], dst[m])
            offs = (np.arange(N_DIAS) * L)[:, None]
            row = (src[None, :] + offs).reshape(-1)
            col = (dst[None, :] + offs).reshape(-1)
            return (row.astype(np.int32), col.astype(np.int32))
        n = emotions_feat.shape[0]
        x1 = emotions_feat @ W1 + b1
        h = x1.shape[1]
        deg = jax.ops.segment_sum(jnp.ones_like(col, x1.dtype), col, num_segments=n)
        dis = jnp.clip(deg, 1.0) ** (-0.5)
        norm = dis[row] * dis[col]
        gnn = x1
        for k in range(Wg.shape[0]):
            Wi, Wj = (Wg[k, :h], Wg[k, h:])
            x_i = gnn[col]
            x_j = gnn[row]
            alpha = jnp.tanh(x_i @ Wi + x_j @ Wj + bg[k])
            msg = norm[:, None] * alpha * x_j
            agg = jax.ops.segment_sum(msg, col, num_segments=n)
            gnn = gnn + agg
        return jnp.concatenate([x1, gnn], axis=1)

    def _L1_mix_ref(x, Wq, bq, Wk, bk, Wv, bv, Wp, bp):
        import jax, jax.numpy as jnp
        import numpy as np
        DIM = 1024
        HEADS = 16
        DIM_HEAD = 64
        B, T, C = x.shape
        H, D = (HEADS, DIM_HEAD)

        def split_heads(t):
            return t.reshape(B, T, H, D).transpose(0, 2, 1, 3)
        q = split_heads(x @ Wq + bq)
        k = split_heads(x @ Wk + bk)
        v = split_heads(x @ Wv + bv)
        q = jax.nn.softmax(q, axis=-1)
        k = jax.nn.softmax(k, axis=-1)
        k_cumsum = k.sum(axis=-2, keepdims=True)
        D_inv = 1.0 / (q * k_cumsum).sum(axis=-1, keepdims=True)
        context = jnp.einsum('bhtd,bhte->bhde', k, v)
        y = jnp.einsum('bhtd,bhde->bhte', q, context) * D_inv + q
        y = y.transpose(0, 2, 1, 3).reshape(B, T, H * D)
        return y @ Wp + bp

    def _L1_ffn_ref(x, gate_W, W1, b1, W2, b2):
        import jax, jax.numpy as jnp
        import numpy as np
        TOP_K = 2
        N_EXPERTS = 8
        E = W1.shape[0]
        d_in = x.shape[-1]
        d_out = W2.shape[-1]
        x_flat = x.reshape(-1, d_in)
        logits = x_flat @ gate_W
        gates = jax.nn.softmax(logits, axis=-1)
        tk_g, tk_i = jax.lax.top_k(gates, TOP_K)
        tk_g = tk_g / (jnp.sum(tk_g, axis=-1, keepdims=True) + 1e-08)
        cw = jnp.sum(jax.nn.one_hot(tk_i, E, dtype=x.dtype) * tk_g[..., None], axis=1)
        out = x_flat
        for e in range(E):
            h = jax.nn.relu(x_flat @ W1[e] + b1[e])
            out = out + cw[:, e:e + 1] * (h @ W2[e] + b2[e])
        return out.reshape(x.shape[:-1] + (d_out,))
    edge_index = jnp.stack([src, dst])
    xn = _layernorm(x, axis=-1)
    x = x + _L0_gnn_ref(xn, edge_index, edge_type_5, L0_gnn_edge_type_weights, L0_gnn_wq, L0_gnn_bq, L0_gnn_wk, L0_gnn_bk, L0_gnn_wv, L0_gnn_bv, L0_gnn_wiq, L0_gnn_biq, L0_gnn_wik, L0_gnn_bik, L0_gnn_wiv, L0_gnn_biv, L0_gnn_wo, L0_gnn_bo) + _L0_mix_ref(xn[None], L0_mix_Wq, L0_mix_Wk, L0_mix_Wv, L0_mix_Wo, L0_mix_bo)[0]
    x = x + _L0_ffn_ref(_layernorm(x, axis=-1)[None], L0_ffn_w1, L0_ffn_b1, L0_ffn_w2, L0_ffn_b2)[0]
    xn = _layernorm(x, axis=-1)
    x = x + _L1_gnn_ref(xn, L1_gnn_W1, L1_gnn_b1, L1_gnn_Wg, L1_gnn_bg, src, dst) + _L1_mix_ref(xn[None], L1_mix_Wq, L1_mix_bq, L1_mix_Wk, L1_mix_bk, L1_mix_Wv, L1_mix_bv, L1_mix_Wp, L1_mix_bp)[0]
    x = x + _L1_ffn_ref(_layernorm(x, axis=-1)[None], L1_ffn_gate_W, L1_ffn_W1, L1_ffn_b1, L1_ffn_W2, L1_ffn_b2)[0]
    return x

_drawn_inputs = setup_inputs


def setup_inputs(seed=0):
    import zlib

    import numpy as np

    out = dict(_drawn_inputs(seed))
    spreads = {'L0_ffn_b1': (0.0, 0.1),
     'L0_ffn_b2': (0.0, 0.1),
     'L1_gnn_b1': (0.0, 0.1),
     'L1_gnn_bg': (0.0, 0.1),
     'L1_ffn_b1': (0.0, 0.552),
     'L1_ffn_b2': (0.0, 0.1)}
    factors = {'L0_gnn_edge_type_weights': 3.205,
     'L0_gnn_wq': 2.94,
     'L0_gnn_bq': 78.108,
     'L0_gnn_bk': 200.0,
     'L0_gnn_bv': 2.815,
     'L0_gnn_biq': 50.023,
     'L0_gnn_bik': 200.0,
     'L0_mix_Wq': 8.0,
     'L0_mix_Wk': 6.169,
     'L0_mix_Wv': 3.885,
     'L0_mix_Wo': 4.957,
     'L1_mix_bq': 60.919,
     'L1_mix_Wk': 4.664,
     'L1_mix_bk': 200.0,
     'L1_mix_bv': 4.932,
     'L1_mix_bp': 4.643}
    for name, (base, spread) in spreads.items():
        noise = np.random.default_rng([zlib.crc32(name.encode()), seed]).standard_normal(out[name].shape)
        drawn = base * np.exp(spread * noise) if base else spread * noise
        out[name] = jnp.asarray(drawn.astype(out[name].dtype))
    for name, factor in factors.items():
        out[name] = (out[name] * factor).astype(out[name].dtype)
    return out
```

```python
import concourse.bass as bass
from concourse import mybir
from contextlib import ExitStack

F32 = mybir.dt.float32
F32R = mybir.dt.float32r
BF16 = mybir.dt.bfloat16
F16 = mybir.dt.float16
I32 = mybir.dt.int32
U32 = mybir.dt.uint32
ALU = mybir.AluOpType
ACT = mybir.ActivationFunctionType
X = mybir.AxisListType.X

P = 128
N = 384
NT = N // P
D = 1024
KD = D // P
H0, DH = 16, 64
HID = 512
KH = HID // P
E = 6144
EC = E // P
NTYPE = 4
HOPS = 4
EXPERTS, EHID = 8, 256
HALF = 512
EPS = 1e-5
ROUND = 12582912.0
NO_EDGE = -1.0e30

RAW, RING, AHEAD = 3, 4, 3

ROWS = {}
_at = 0
for _n, _l in (("biv", D), ("bo", D), ("mix_bo", D), ("ffn_b1", HID), ("ffn_b2", D), ("gnn_b1", HID),
               ("wg0", D), ("bk", D), ("wg1", D), ("bv", D), ("wg2", D), ("bq", D), ("wg3", D), ("bp", D)):
    ROWS[_n] = (_at, _l)
    _at += _l
ROW_ORDER = list(ROWS)
ROW_SLOTS = 3
COLS = {"v1": 0, "q1": 8, "k1": 16, "q2": 24, "k2": 32, "e1": 40}


def schedule():
    steps, units = [], []

    def unit(name, i):
        steps.append(("unit", len(units), name, i))
        units.append((name, i))

    def run(name, a, b):
        for i in range(a, b):
            unit(name, i)

    steps.append(("graph",))
    steps.append(("transpose", "xn1"))
    run("v1", 0, 8)
    steps.append(("degree",))
    run("v2", 0, 1)
    steps.append(("norm",))
    run("v2", 1, 8)
    run("mk", 0, 4)
    run("mv", 0, 4)
    run("mq", 0, 4)
    run("q1", 0, 2)
    steps.append(("mix0_kT",))
    run("q1", 2, 4)
    steps.append(("mix0_context",))
    run("q1", 4, 6)
    steps.append(("mix0_qT",))
    run("q1", 6, 8)
    steps.append(("mix0_out",))
    run("k1", 0, 8)
    unit("q2", 0)
    unit("k2", 0)
    unit("q2", 1)
    steps.append(("scores", 0))
    unit("k2", 1)
    steps.append(("scores", 1))
    for h in range(H0):
        steps.append(("probs", h))
        if h + 2 < H0:
            steps.append(("scores", h + 2))
        if h // 2 + 2 < KD:
            unit(("q2", "k2")[h % 2], h // 2 + 2)
        steps.append(("attend", h))
    run("wo", 0, 6)
    steps.append(("ffn_mean",))
    run("wo", 6, 12)
    steps.append(("ffn",))
    steps.append(("transpose", "xn3"))
    run("g1", 0, 4)
    hops = {2: ("hop_row", 0), 4: ("hop_sum", 0), 7: ("hop_row", 1), 9: ("hop_sum", 1),
            12: ("hop_row", 2), 14: ("hop_sum", 2), 19: ("hop_row", 3), 21: ("hop_sum", 3)}
    n = 0
    for name in ("k", "v", "q"):
        for i in range(8):
            unit(name, i)
            n += 1
            if n in hops:
                steps.append(hops[n])
            if name == "q" and i == 2:
                steps.append(("context",))
            if name == "q" and i == 7:
                steps.append(("queries",))
    steps.append(("transpose", "y"))
    run("wp", 0, 8)
    steps.append(("transpose", "xn4"))
    steps.append(("gate",))
    run("e1", 0, 4)
    steps.append(("gate_rows",))
    run("e1", 4, 16)
    run("e2", 0, 16)
    return steps, units


STEPS, UNITS = schedule()
UNIT_OF = {u: n for n, u in enumerate(UNITS)}
FEATURE_MAJOR = {"v1": "xn1", "mk": "xn1", "q1": "xn1", "k1": "xn1", "q2": "q1", "k2": "k1", "e1": "xn4"}
NODE_MAJOR = {"v2": ("v1", 4), "mv": ("xn1", 4), "mq": ("xn1", 4), "wo": ("o", 6), "g1": ("xn3", 4), "k": ("xn3", 4),
              "v": ("xn3", 4), "q": ("xn3", 4), "wp": ("y", 4), "e2": ("h", 8)}


def plan_banks():
    uses, fulls, where = [0] * 8, [0] * 8, {}

    def product(name, bank, unit=None):
        uses[bank] += 1
        if unit is None:
            fulls[bank] += 1
            where[name] = (bank, uses[bank], None, fulls[bank])
        else:
            where[name] = (bank, uses[bank], "unit", unit + 1)

    single = group = 0
    for s in STEPS:
        kind = s[0]
        if kind == "unit":
            _, u, name, i = s
            if name in FEATURE_MAJOR:
                if name in ("q2", "k2"):
                    product(f"{name}.{i}", {"q2": 0, "k2": 1}[name], u)
                else:
                    product(f"{name}.{i}", single % 6, u)
                    single += 1
            else:
                per = NODE_MAJOR[name][1]
                if i % per == 0:
                    for t in range(NT):
                        product(f"{name}.{i // per}.{t}", 3 * (group % 2) + t, u + per - 1 if t == NT - 1 else None)
                    group += 1
        elif kind == "graph":
            for c in range(0, EC, 4):
                product(f"keys.{c // 4}", 6 + c // 4 % 2)
            for t in range(NT):
                product(f"last_edge.{t}", t)
                product(f"count.{t}", 3 + t)
        elif kind == "transpose":
            for k in range(KD):
                product(f"{s[1]}.{k}", 6 + k % 2)
        elif kind == "degree":
            product("degree", 7)
        elif kind == "norm":
            product("norm", 7)
        elif kind == "mix0_kT":
            for t in range(NT):
                product(f"kn.{t}", 6 + t % 2)
        elif kind == "mix0_context":
            product("mix_context", 7)
        elif kind == "mix0_qT":
            for j in range(KH):
                product(f"qT.{j}", 6 + j % 2)
        elif kind == "mix0_out":
            for j in range(KH):
                product(f"mixo.{j}", 6 + j % 2)
        elif kind == "scores":
            for t in range(NT):
                product(f"scores.{s[1]}.{t}", 2 + (3 * s[1] + t) % 2)
        elif kind == "probs":
            for m in range(NT):
                product(f"pT.{s[1]}.{m}", 4 + (3 * s[1] + m) % 2)
        elif kind == "attend":
            product(f"attend.{s[1]}", 6 + s[1] % 2)
        elif kind == "ffn_mean":
            product("w_sum", 7)
        elif kind == "ffn":
            for k in range(KD // 2):
                product(f"xqT.{k}", 6 + k % 2)
            for t in range(NT):
                product(f"ffn_h.{t}", t)
            for k in range(KH // 2):
                product(f"hqT.{k}", 6 + k % 2)
            for t in range(NT):
                for c in range(2):
                    product(f"ffn_o.{t}.{c}", 3 * c + t)
        elif kind == "hop_row":
            product(f"ai.{s[1]}", 6)
        elif kind == "hop_sum":
            for t in range(NT):
                product(f"hop.{s[1]}.{t}", 7 if t % 2 == 0 else 6)
        elif kind == "context":
            for b in range(3):
                product(f"context.{b}", 6 + b % 2)
        elif kind == "queries":
            for j in range(KD):
                product(f"q1T.{j}", 6 + j % 2)
            for t in range(NT):
                for b in range(3):
                    product(f"y.{t}.{b}", 6 + (3 * t + b) % 2)
        elif kind == "gate":
            for t in range(NT):
                product(f"logits.{t}", 6 + t % 2)
        elif kind == "gate_rows":
            product("cwT", 7)
            for e in range(EXPERTS):
                product(f"cw.{e}", 6 + e % 2)
    return where


WHERE = plan_banks()


def sub_no(name, c, t):
    return {"mq": 0, "k": NT, "q": 3 * NT}[name] + NT * c + t + 1


def gps_kernel(nc, weights, x_in, edges, rows, cols, tiny, w1_in, w2_in, gate_in, eb2_in, out):
    with ExitStack() as ctx:
        def sem(name):
            return ctx.enter_context(nc.semaphore(name))

        base = (nc.sbuf_base + 63) // 64 * 64
        fence = ctx.enter_context(nc.sbuf_tensor("fence", [P, (nc.sbuf_usable_end - nc.sbuf_base) // 4 - 16], F32))
        del fence

        def at(name, shape, dt, kib):
            return nc.alloc_sbuf_tensor_at(name, shape, dt, offset=base + int(kib * 1024))

        XA, R0, R1, R2, R3, AT, MASK, CNT, RAWS, HIS, LOS, ROWS_AT, SMALL = (
            0, 12, 36, 60, 84, 108, 138, 142.5, 147, 159, 175, 191, 203)
        x_sb = at("x_sb", [P, NT, D], F32, XA)
        raw = at("raw", [P, RAW, D], F32, RAWS)
        w_hi = at("w_hi", [P, RING, D], F32R, HIS)
        w_lo = at("w_lo", [P, RING, D], F32R, LOS)
        row_sb = at("row_sb", [P, ROW_SLOTS, D], F32, ROWS_AT)
        mask = at("mask", [P, NT, N], F32, MASK)
        count = at("count", [P, NT, N], F32, CNT)

        def pair(name, chunks, width, kib):
            return at(name, [P, 2, chunks, width], F32R, kib)

        TT = {"xn1": pair("xn1T", KD, N, R0), "v1": pair("v1T", KD, N, R1), "q1": pair("q1T", KD, N, R1),
              "k1": pair("k1T", KD, N, R3), "o": pair("oT", KD, N, R0), "mixo": pair("mixoT", KH, N, XA),
              "xn3": pair("xn3T", KD, N, R0), "q1T": pair("qT_l1", KD, N, R3), "y": pair("yT", KD, N, R1),
              "xn4": pair("xn4T", KD, N, R0), "h_a": pair("hT_a", KD, N, R1), "h_b": pair("hT_b", KD, N, R3)}
        xn1 = at("xn1_nat", [P, NT, D], F32, R3)
        onehot = at("onehot", [P, 4, 3, N], BF16, R3 + 12)
        edge_i = at("edge_i", [P, 3, EC], I32, R2)
        edge_f = at("edge_f", [P, 3, EC], F32, R2 + 1)
        key = at("key", [P, EC], F32, R2 + 2)
        four0 = at("four0", [P, EC], F32, R2 + 2.25)
        cls = at("cls", [P, EC], F32, R2 + 2.5)
        power = at("power", [P, EC], I32, R2 + 2.75)
        dead = at("dead", [P, EC], F32, R2 + 3)
        value = at("value", [P, EC], F32, R2 + 3.25)
        chunk_no = at("chunk_no", [P, EC], I32, R2 + 3.5)
        same = at("same", [P, 2, P], F32, R2 + 4)
        later = at("later", [P, P], F32, R2 + 5)
        node_i = at("node_i", [P, N], I32, R2 + 5.5)
        node = at("node", [P, N], F16, R2 + 7)
        diag = at("diag", [P, 5 * P], BF16, R2 + 8)
        edge_cls = at("edge_cls", [P, NT, N], I32, AT)
        no_edge = at("no_edge", [P, NT, N], F32, AT + 4.5)
        picked = at("picked", [P, 2, NT, N], F32, AT + 9)
        v2f = at("v2f", [P, NT, D], F32, AT)
        v2 = at("v2", [P, 2, NT, D], F32R, R2)
        qk = at("qk", [P, 2, 2, 2, N], F32R, AT)
        prob = at("prob", [P, 2, NT, N], F32, AT + 12)
        probT = at("probT", [P, 2, NT, N], F32R, AT + 21)
        ekT = at("ekT", [P, KH, N], F32, AT)
        mqn = at("mqn", [P, NT, HID], F32, AT + 6)
        mqT = at("mqT", [P, 2, KH, N], F32R, AT + 12)
        mctx = at("mctx", [P, KH, P], F32, AT + 24)
        mctx2 = at("mctx2", [P, 2, KH, P], F32R, AT + 26)
        mkn = at("mkn", [P, 2, NT, HID], F32R, R3)
        mvn = at("mvn", [P, 2, NT, HID], F32R, R3 + 12)
        base1 = at("base1", [P, NT, D], F32, R1)
        base2 = at("base2", [P, NT, D], F32, R1 + 12)
        w1r = at("w1r", [P, KD * HID], F32, R2)
        w2r = at("w2r", [P, KH * D], F32, R3)
        w1q = at("w1q", [P, KD, HID], BF16, R2 + 16)
        w2q = at("w2q", [P, KH, D], BF16, R3 + 16)
        xn2 = at("xn2_nat", [P, NT, D], F32, R0)
        xq = at("xq", [P, NT, D], BF16, R0 + 12)
        xqT = at("xqT", [P, KD, N], BF16, R0 + 18)
        hn = at("hn", [P, NT, HID], F32, AT)
        hq = at("hq", [P, NT, HID], BF16, AT + 6)
        hqT = at("hqT", [P, KH, N], BF16, AT + 9)
        junk = at("junk", [P, D], F32, AT + 12)
        xn3 = at("xn3_nat", [P, NT, D], F32, R2)
        g = at("g", [P, NT, HID], F32, AT)
        g2 = at("g2", [P, 2, NT, HID], F32R, AT + 6)
        msg = at("msg", [P, NT, N], F32, MASK)
        msg2 = at("msg2", [P, 2, NT, N], F32R, AT + 18)
        gjunk = at("gjunk", [P, HID], F32, AT + 27)
        kf = at("kf", [P, NT, D], F32, R1)
        k2n = at("k2n", [P, 2, NT, D], F32R, R3)
        v2n = at("v2n", [P, 2, NT, D], F32R, R2)
        qf = at("qf", [P, NT, D], F32, R2)
        ctx1 = at("ctx1", [P, 2, KD, P + 2], F32R, R1 + 12)
        ytmp = at("ytmp", [P, 3 * P], F32, R1 + 21)
        xn4 = at("xn4_nat", [P, NT, D], F32, R2)
        cw_row = at("cw_row", [P, EXPERTS, N], F32, AT)
        hf = at("hf", [P, 2, N], F32, AT + 12)
        gate = at("gate", [P, KD * EXPERTS], F32, AT + 15)
        gate2 = at("gate2", [P, 2, KD, EXPERTS], F32R, AT + 15.5)
        eb2 = at("eb2", [EXPERTS, D], F32, AT + 16)
        lg = at("lg", [P, NT, EXPERTS], F32, AT + 20)
        top = at("top", [P, NT, 8], F32, AT + 20.25)
        top_at = at("top_at", [P, NT, 8], U32, AT + 20.5)
        top_f = at("top_f", [P, NT, 8], F32, AT + 20.75)
        gsum = at("gsum", [P, 4, NT], F32, AT + 21)
        pick = at("pick", [P, 2, EXPERTS], F32, AT + 21.25)
        expert = at("expert", [P, EXPERTS], F32, AT + 21.5)
        expert_i = at("expert_i", [P, EXPERTS], I32, AT + 21.75)
        cw = at("cw", [P, NT, P], F32, AT + 22)
        cwT = at("cwT", [P, N], F32, AT + 24)
        ident = at("ident", [P, P], F32, SMALL)
        ident_b = at("ident_b", [P, P], BF16, SMALL + 0.5)
        ones = at("ones", [P, P], F32, SMALL + 0.75)
        ones_r = at("ones_r", [P, 2], F32R, SMALL + 1.25)
        bias = at("bias", [P, 56], F32, SMALL + 1.3125)
        tiny_sb = at("tiny_sb", [P, 8], F32, SMALL + 1.5625)
        w8 = at("w8", [P, 3, 4], F32, SMALL + 1.625)
        stats = at("stats", [P, NT, 2, 6], F32, SMALL + 1.6875)
        mv = at("mv", [P, NT, 2], F32, SMALL + 1.875)
        rstd = at("rstd", [P, NT], F32, SMALL + 1.9375)
        minus_half = at("minus_half", [P, NT], F32, SMALL + 2)
        dis = at("dis", [P, 2, NT], F32, SMALL + 2.0625)
        top1 = at("top1", [P, 2, NT], F32, SMALL + 2.125)
        rsum = at("rsum", [P, 2, NT], F32, SMALL + 2.1875)
        nmax = at("nmax", [P, 2, NT], F32, SMALL + 2.25)
        mk_s = at("mk_s", [P, 3, KH], F32, SMALL + 2.3125)
        h8 = at("h8", [P, 2, 16], F32, SMALL + 2.375)
        q_s = at("q_s", [P, 8, NT], F32, SMALL + 2.5)
        w_s = at("w_s", [P, 2, 2], F32, SMALL + 2.625)
        aij = at("aij", [P, 2, NT], F32, SMALL + 2.6875)
        den = at("den", [P, 6], F32, SMALL + 2.75)
        k8 = at("k8", [P, 2, 16], F32, SMALL + 2.8125)

        bank = [ctx.enter_context(nc.psum_tensor(f"bank{b}", [P, 512], F32)) for b in range(8)]

        bank_full = [sem(f"bank_full{b}") for b in range(8)]
        bank_emptied = [sem(f"bank_emptied{b}") for b in range(8)]
        raw_landed = [sem(f"raw_landed{r}") for r in range(RAW)]
        hi_split = sem("hi_split")
        unit_split = sem("unit_split")
        unit_done = sem("unit_done")
        act_hi = sem("act_hi")
        row_landed = [sem(f"row_landed{r}") for r in range(ROW_SLOTS)]
        x_landed = sem("x_landed")
        small_landed = sem("small_landed")
        edges_landed = sem("edges_landed")
        consts = sem("consts")
        onehots = sem("onehots")
        onehots_used = sem("onehots_used")
        key_ready = sem("key_ready")
        w8_exp, w8_ln, w8_neg, w8_one, w8_ready = (sem(n) for n in ("w8_exp", "w8_ln", "w8_neg", "w8_one", "w8_ready"))
        mask_ready = sem("mask_ready")
        ln_stats, ln_rstd, nat_ready = sem("ln_stats"), sem("ln_rstd"), sem("nat_ready")
        dis_ready = sem("dis_ready")
        node_split = sem("node_split")
        mk_max, mk_exp = sem("mk_max"), sem("mk_exp")
        q_sub, q_exp, q_ready = sem("q_sub"), sem("q_exp"), sem("q_ready")
        mctx_f, mctx_ready = sem("mctx_f"), sem("mctx_ready")
        s_max, s_exp, p_ready = sem("s_max"), sem("s_exp"), sem("p_ready")
        base1_ready, base2_ready = sem("base1_ready"), sem("base2_ready")
        ffn_landed, w_abs, w_unit, w_quant = sem("ffn_landed"), sem("w_abs"), sem("w_unit"), sem("w_quant")
        sq_ready, rms_ready, quant_ready = sem("sq_ready"), sem("rms_ready"), sem("quant_ready")
        h_gelu = sem("h_gelu")
        aij_ready, tanh_done, msg_f, msg_ready = sem("aij_ready"), sem("tanh_done"), sem("msg_f"), sem("msg_ready")
        g_ready = sem("g_ready")
        base3_ready, base4_ready = sem("base3_ready"), sem("base4_ready")
        ctx_f, ctx_ready, y_ready = sem("ctx_f"), sem("ctx_ready"), sem("y_ready")
        gate_landed, eb2_landed, gate_hi, gate_ready = sem("gate_landed"), sem("eb2_landed"), sem("gate_hi"), sem("gate_ready")
        lg_exp, cw_ready = sem("lg_exp"), sem("cw_ready")
        h_relu, h_scaled = sem("h_relu"), sem("h_scaled")
        out_ready, out_stored = sem("out_ready"), sem("out_stored")
        v_chain, a_chain, p_chain = sem("v_chain"), sem("a_chain"), sem("p_chain")
        block = ctx.enter_context(nc.Block())

        def f(ap):
            return ap.bitcast(F32)

        def out_of(name):
            return bank[WHERE[name][0]]

        def wait_bank(pe, name):
            b, n, _, _ = WHERE[name]
            if n > 1:
                pe.wait_ge(bank_emptied[b], n - 1)

        def wait_full(eng, name):
            b, _, by, n = WHERE[name]
            eng.wait_ge(unit_done if by else bank_full[b], n)

        def full(ins, name):
            ins.then_inc(bank_full[WHERE[name][0]], 1)

        def wait_emptied(eng, name):
            b, n, _, _ = WHERE[name]
            eng.wait_ge(bank_emptied[b], n)

        def emptied(ins, name):
            ins.then_inc(bank_emptied[WHERE[name][0]], 1)

        def wait_unit(eng, name, i):
            eng.wait_ge(unit_done, UNIT_OF[(name, i)] + 1)

        def row_slot(name):
            i = ROW_ORDER.index(name)
            return i % ROW_SLOTS, 16 * (i // ROW_SLOTS + 1)

        def wait_row(eng, name):
            slot, n = row_slot(name)
            eng.wait_ge(row_landed[slot], n)

        def row(name, a=0, b=None):
            return row_sb[:, row_slot(name)[0], a:ROWS[name][1] if b is None else b]

        def bcast(ap, shape):
            return ap.unsqueeze(len(shape) - 1).to_broadcast(shape)

        def heads(ap):
            return ap.rearrange("p (h d) -> p h d", d=DH)

        @block.sync
        def _(sp):
            sp.dma_start(edge_i[:], edges).then_inc(edges_landed, 16)
            sp.dma_start(x_sb[:], x_in.rearrange("(t p) d -> p t d", p=P)).then_inc(x_landed, 16)
            sp.dma_start(bias[:], cols).then_inc(small_landed, 16)
            sp.dma_start(tiny_sb[:], tiny.partition_broadcast(P)).then_inc(small_landed, 16)

            def load_row(name, free=None):
                if free:
                    free()
                o, n = ROWS[name]
                sp.dma_start(row(name), rows[o:o + n].partition_broadcast(P)).then_inc(row_landed[row_slot(name)[0]], 16)

            for name in ROW_ORDER[:ROW_SLOTS]:
                load_row(name)
            for s in STEPS:
                if s[0] == "unit":
                    _, u, name, i = s
                    if u >= RAW:
                        sp.wait_ge(unit_split, u - RAW + 1)
                    sp.dma_start(raw[:, u % RAW, :], weights[u]).then_inc(raw_landed[u % RAW], 16)
                    if (name, i) == ("wo", 1):
                        wait_unit(sp, "q2", 7)
                        sp.dma_start(base1[:], x_in.rearrange("(t p) d -> p t d", p=P)).then_inc(x_landed, 16)
                        load_row("ffn_b1", lambda: wait_emptied(sp, "v2.1.2"))
                    if (name, i) == ("wo", 3):
                        wait_full(sp, "attend.15")
                        sp.dma_start(w1r[:], w1_in).then_inc(ffn_landed, 16)
                    if (name, i) == ("wo", 5):
                        sp.dma_start(w2r[:], w2_in).then_inc(ffn_landed, 16)
                    if (name, i) == ("wo", 11):
                        load_row("ffn_b2", lambda: sp.wait_ge(base1_ready, NT))
                        load_row("gnn_b1")
                    if (name, i) == ("g1", 3):
                        load_row("wg0", lambda: wait_emptied(sp, "ffn_h.2"))
                        load_row("bk", lambda: sp.wait_ge(base2_ready, NT))
                    if (name, i) == ("k", 2):
                        load_row("wg1", lambda: wait_emptied(sp, "g1.0.2"))
                    if (name, i) == ("k", 6):
                        load_row("bv", lambda: sp.wait_ge(aij_ready, 1))
                    if (name, i) == ("v", 2):
                        load_row("wg2", lambda: wait_emptied(sp, "k.1.2"))
                    if (name, i) == ("v", 5):
                        load_row("bq", lambda: sp.wait_ge(aij_ready, 2))
                    if (name, i) == ("q", 2):
                        load_row("wg3", lambda: wait_emptied(sp, "v.1.2"))
                    if (name, i) == ("q", 4):
                        load_row("bp", lambda: sp.wait_ge(aij_ready, 3))
                    if (name, i) == ("wp", 1):
                        sp.wait_ge(base3_ready, NT)
                        sp.dma_start(gate[:], gate_in).then_inc(gate_landed, 16)
                        sp.dma_start(eb2[:], eb2_in).then_inc(eb2_landed, 16)
            n = 0
            for c in range(2):
                for t in range(NT):
                    n += 1
                    sp.wait_ge(out_ready, n)
                    sp.dma_start(out[t * P:(t + 1) * P, c * HALF:(c + 1) * HALF],
                                 x_sb[:, t, c * HALF:(c + 1) * HALF]).then_inc(out_stored, 16)
            sp.wait_ge(out_stored, 16 * n)

        @block.gpsimd
        def _(pool):
            pn = [0]

            def link(ins):
                pn[0] += 1
                ins.then_inc(p_chain, 1)
                pool.wait_ge(p_chain, pn[0])

            pool.memset(minus_half[:], -0.5).then_inc(consts, 1)
            link(pool.memset(ident[:], 0.0))
            link(pool.affine_select(out=ident[:], in_=ident[:], compare_op=ALU.not_equal, fill=1.0, base=0,
                                    pattern=[[-1, P]], channel_multiplier=1))
            pool.tensor_copy(ident_b[:], ident[:]).then_inc(consts, 1)
            link(pool.memset(ones[:], 1.0))
            pool.tensor_copy(ones_r[:], ones[:, 0:2]).then_inc(consts, 1)
            pool.affine_select(out=later[:], in_=ones[:], compare_op=ALU.is_gt, fill=0.0, base=0,
                               pattern=[[1, P]], channel_multiplier=-1).then_inc(consts, 1)
            link(pool.iota(node_i[:], pattern=[[1, N]], base=0, channel_multiplier=0))
            pool.tensor_copy(node[:], node_i[:]).then_inc(consts, 1)
            pool.iota(chunk_no[:], pattern=[[4, EC]], base=32, channel_multiplier=0).then_inc(consts, 1)
            link(pool.memset(diag[:], 0.0))
            pool.tensor_scalar(diag[:, 2 * P:3 * P], ident[:], 2.0 ** -96, None, ALU.mult).then_inc(consts, 1)

            def power(dst, src, scale, n):
                link(pool.tensor_scalar(dst, src, scale, EPS, ALU.mult, ALU.add))
                return pool.tensor_tensor(dst, dst, minus_half[:, 0:n], ALU.pow)

            lns = 0
            for s in STEPS:
                if s[0] in ("graph", "ffn") or s[:2] in (("transpose", "xn3"), ("transpose", "xn4")):
                    lns += 1
                    pool.wait_ge(ln_stats, NT * lns)
                    power(rstd[:], mv[:, :, 1], 1.0, NT).then_inc(ln_rstd, 1)
                if s[0] == "graph":
                    for t in range(NT):
                        wait_emptied(pool, f"last_edge.{t}")
                    pool.wait_ge(w8_ready, 1)
                    link(pool.tensor_scalar(picked[:, 0], edge_cls[:], 0.0, w8[:, 2, 0:1], ALU.is_equal, ALU.mult))
                    link(pool.tensor_tensor(mask[:], no_edge[:], picked[:, 0], ALU.add))
                    for k in range(1, NTYPE):
                        link(pool.tensor_scalar(picked[:, k % 2], edge_cls[:], float(k), w8[:, 2, k:k + 1],
                                                ALU.is_equal, ALU.mult))
                        ins = pool.tensor_tensor(mask[:], mask[:], picked[:, k % 2], ALU.add)
                        if k < NTYPE - 1:
                            link(ins)
                    ins.then_inc(mask_ready, 1)
                if s[0] == "degree":
                    wait_emptied(pool, "degree")
                    pool.tensor_tensor(dis[:, 1], dis[:, 0], minus_half[:], ALU.pow).then_inc(dis_ready, 1)
                if s[0] == "attend" and s[1] == H0 - 1:
                    pool.wait_ge(x_landed, 32)
                    wait_row(pool, "bo")
                    wait_row(pool, "mix_bo")
                    link(pool.tensor_tensor(row("bo"), row("bo"), row("mix_bo"), ALU.add))
                    for t in range(NT):
                        pool.tensor_tensor(base1[:, t], base1[:, t], row("bo"), ALU.add).then_inc(base1_ready, 1)
                if s[0] == "ffn_mean":
                    for w in range(2):
                        pool.wait_ge(w_unit, w + 1)
                        src, dst = ((w1r, w1q), (w2r, w2q))[w]
                        pool.tensor_scalar(dst[:].rearrange("p a b -> p (a b)"), src[:], ROUND, None,
                                           ALU.subtract).then_inc(w_quant, 1)
                if s[0] == "ffn":
                    wait_row(pool, "ffn_b2")
                    for t in range(NT):
                        wait_emptied(pool, f"wo.0.{t}")
                        wait_emptied(pool, f"wo.1.{t}")
                        pool.tensor_tensor(base2[:, t], base1[:, t], row("ffn_b2"), ALU.add).then_inc(base2_ready, 1)
                    for n, width in ((1, D), (2, HID)):
                        pool.wait_ge(sq_ready, NT * n)
                        power(q_s[:, 1], q_s[:, 0], 1.0 / width, NT).then_inc(rms_ready, 1)
                if s[0] == "hop_sum" and s[1] == 0:
                    pool.wait_ge(g_ready, NT)
                    for t in range(NT):
                        pool.tensor_tensor(x_sb[:, t, 0:HID], x_sb[:, t, 0:HID], f(g2[:, 0, t]), ALU.add).then_inc(p_chain, 1)
                        pn[0] += 1
                    pool.wait_ge(p_chain, pn[0])
                    for t in range(NT):
                        pool.tensor_tensor(x_sb[:, t, 0:HID], x_sb[:, t, 0:HID], f(g2[:, 1, t]), ALU.add).then_inc(base4_ready, 1)
                if s[0] == "hop_sum" and s[1] == HOPS - 1:
                    wait_row(pool, "bp")
                    for t in range(NT):
                        wait_emptied(pool, f"hop.{HOPS - 1}.{t}")
                    pool.wait_ge(base4_ready, NT)
                    for t in range(NT):
                        pool.tensor_tensor(x_sb[:, t, HID:D], x_sb[:, t, HID:D], g[:, t], ALU.add).then_inc(p_chain, 1)
                        pn[0] += 1
                    pool.wait_ge(p_chain, pn[0])
                    for t in range(NT):
                        pool.tensor_tensor(x_sb[:, t], x_sb[:, t], row("bp"), ALU.add).then_inc(base3_ready, 1)
                if s[0] == "gate":
                    pool.wait_ge(nat_ready, 4 * NT)
                    link(pool.iota(expert_i[:], pattern=[[1, EXPERTS]], base=0, channel_multiplier=0))
                    pool.tensor_copy(expert[:], expert_i[:]).then_inc(consts, 1)
                    for t in range(NT):
                        pool.tensor_tensor(x_sb[:, t], x_sb[:, t], xn4[:, t], ALU.add).then_inc(base4_ready, 1)

        @block.scalar
        def _(act):
            hi = [0]

            def hi_part(dst, src, name=None, bias=0.0):
                if name:
                    wait_full(act, name)
                act.activation(dst, src, ACT.Identity, bias=bias).then_inc(act_hi, 1)
                hi[0] += 1

            def split_unit(u):
                act.wait_ge(raw_landed[u % RAW], 16 * (u // RAW + 1))
                if u >= RING:
                    act.wait_ge(unit_done, u - RING + 1)
                act.activation(w_hi[:, u % RING], raw[:, u % RAW], ACT.Copy).then_inc(hi_split, 1)

            def chunk_hi(tname, k, name, col=None):
                b = 0.0 if col is None else bias[:, col:col + 1]
                hi_part(TT[tname][:, 0, k], out_of(name)[:, 0:N], name, b)

            def expert(i):
                wait_full(act, f"e1.{i}")
                if i >= 2:
                    act.wait_ge(h_scaled, 2 * (i - 2) + 2)
                emptied(act.activation(hf[:, i % 2], out_of(f"e1.{i}")[:, 0:N], ACT.Relu,
                                       bias=bias[:, COLS["e1"] + i:COLS["e1"] + i + 1]), f"e1.{i}")
                act.wait_ge(h_scaled, 2 * i + 1)
                hi_part(TT["h_a" if i < KD else "h_b"][:, 0, i % KD], hf[:, i % 2])

            act.wait_ge(small_landed, 32)
            for u in range(AHEAD):
                split_unit(u)
            for s in STEPS:
                kind = s[0]
                if kind == "graph":
                    act.wait_ge(w8_neg, 1)
                    act.activation(w8[:, 1], w8[:, 0], ACT.Exp).then_inc(w8_exp, 1)
                    act.wait_ge(w8_one, 1)
                    act.activation(w8[:, 2], w8[:, 1], ACT.Ln).then_inc(w8_ln, 1)
                    for t in range(NT):
                        wait_full(act, f"count.{t}")
                        emptied(act.activation(count[:, t], out_of(f"count.{t}")[:, 0:N], ACT.Copy), f"count.{t}")
                if kind == "transpose":
                    if s[1] == "y":
                        wait_full(act, "y.2.2")
                    if s[1] == "xn4":
                        wait_unit(act, "q", 7)
                    for k in range(KD):
                        chunk_hi(s[1], k, f"{s[1]}.{k}")
                if kind == "unit":
                    _, u, name, i = s
                    if u + AHEAD < len(UNITS):
                        split_unit(u + AHEAD)
                    if name in ("v1", "q1", "k1"):
                        if (name, i) == ("q1", 0):
                            wait_unit(act, "v2", 7)
                        if (name, i) == ("k1", 0):
                            wait_full(act, "mixo.3")
                        chunk_hi(name, i, f"{name}.{i}", COLS[name] + i)
                    if name in ("q2", "k2"):
                        n = "qk".index(name[0])
                        if i >= 2:
                            wait_full(act, f"scores.{2 * i - 3}.2")
                        hi_part(qk[:, i % 2, n, 0], out_of(f"{name}.{i}")[:, 0:N], f"{name}.{i}",
                                bias[:, COLS[name] + i:COLS[name] + i + 1])
                    if name == "mk":
                        act.wait_ge(mk_max, i + 1)
                        emptied(act.activation(ekT[:, i], out_of(f"mk.{i}")[:, 0:N], ACT.Exp, bias=mk_s[:, 0, i:i + 1],
                                               accum_out=mk_s[:, 1, i:i + 1]), f"mk.{i}")
                    if name in NODE_MAJOR and i % NODE_MAJOR[name][1] == NODE_MAJOR[name][1] - 1:
                        c = i // NODE_MAJOR[name][1]
                        for t in range(NT):
                            pr = f"{name}.{c}.{t}"
                            sl = slice(c * HALF, (c + 1) * HALF)
                            if name == "v2":
                                wait_emptied(act, pr)
                                hi_part(v2[:, 0, t, sl], v2f[:, t, sl])
                            if name == "v":
                                wait_emptied(act, pr)
                                hi_part(v2n[:, 0, t, sl], kf[:, t, sl])
                            if name == "mv":
                                hi_part(mvn[:, 0, t], out_of(pr)[:], pr)
                            if name in ("mq", "k", "q"):
                                src = {"mq": mqn[:, t], "k": kf[:, t, sl], "q": qf[:, t, sl]}[name]
                                if name == "mq":
                                    wait_emptied(act, pr)
                                else:
                                    act.wait_ge(q_sub, sub_no(name, c, t) - NT)
                                act.activation(src, src, ACT.Exp).then_inc(q_exp, 1)
                        if name == "k":
                            for t in range(NT):
                                act.wait_ge(q_ready, sub_no(name, c, t))
                                hi_part(k2n[:, 0, t, c * HALF:(c + 1) * HALF], kf[:, t, c * HALF:(c + 1) * HALF])
                        if name == "g1":
                            for t in range(NT):
                                wait_emptied(act, f"g1.0.{t}")
                                hi_part(g2[:, 0, t], g[:, t])
                    if name == "e1" and i >= 4:
                        expert(i)
                if kind == "gate_rows":
                    for e in range(EXPERTS):
                        wait_full(act, f"cw.{e}")
                        emptied(act.activation(cw_row[:, e], out_of(f"cw.{e}")[:, 0:N], ACT.Copy), f"cw.{e}")
                    for i in range(4):
                        expert(i)
                if kind == "mix0_kT":
                    for t in range(NT):
                        hi_part(mkn[:, 0, t], out_of(f"kn.{t}")[:], f"kn.{t}")
                if kind == "mix0_context":
                    act.wait_ge(mctx_f, 1)
                    for r in range(2):
                        hs = slice(64 * r, 64 * r + 64)
                        hi_part(mctx2[hs, 0, :, hs], mctx[hs, :, hs])
                if kind == "mix0_qT":
                    for j in range(KH):
                        hi_part(mqT[:, 0, j], out_of(f"qT.{j}")[:, 0:N], f"qT.{j}")
                if kind == "mix0_out":
                    for j in range(KH):
                        hi_part(TT["mixo"][:, 0, j], out_of(f"mixo.{j}")[:, 0:N], f"mixo.{j}")
                if kind == "scores":
                    h = s[1]
                    act.wait_ge(s_max, h + 1)
                    for t in range(NT):
                        act.activation(prob[:, h % 2, t], prob[:, h % 2, t], ACT.Exp, scale=0.125,
                                       bias=nmax[:, h % 2, t:t + 1], accum_out=rsum[:, h % 2, t:t + 1]).then_inc(s_exp, 1)
                if kind == "probs":
                    h = s[1]
                    if h:
                        wait_full(act, f"attend.{h - 1}")
                    for m in range(NT):
                        hi_part(probT[:, 0, m], out_of(f"pT.{h}.{m}")[:, 0:N], f"pT.{h}.{m}")
                if kind == "attend":
                    h = s[1]
                    hs = slice(64 * (h % 2), 64 * (h % 2) + 64)
                    if h == 0:
                        wait_unit(act, "k1", 7)
                    hi_part(TT["o"][hs, 0, h // 2], out_of(f"attend.{h}")[hs, 0:N], f"attend.{h}")
                if kind == "ffn_mean":
                    act.wait_ge(ffn_landed, 32)
                    for w in range(2):
                        src, dst = ((w1r, w1q), (w2r, w2q))[w]
                        act.activation(dst[:].rearrange("p a b -> p (a b)"), src[:], ACT.Abs,
                                       accum_out=w_s[:, 0, w:w + 1]).then_inc(w_abs, 1)
                if kind == "ffn":
                    for n, (src, width) in enumerate(((xn2, D), (hn, HID))):
                        if n == 1:
                            for t in range(NT):
                                wait_emptied(act, f"ffn_h.{t}")
                                act.activation(hn[:, t], hn[:, t], ACT.Gelu).then_inc(h_gelu, 1)
                        for t in range(NT):
                            if n == 0:
                                act.wait_ge(nat_ready, NT + t + 1)
                            else:
                                act.wait_ge(h_gelu, t + 1)
                            if n or t:
                                act.wait_ge(sq_ready, NT * n + t)
                            act.activation(junk[:, 0:width], src[:, t], ACT.Square,
                                           accum_out=q_s[:, 0, t:t + 1]).then_inc(sq_ready, 1)
                if kind == "hop_row":
                    n = s[1]
                    wait_full(act, f"ai.{n}")
                    act.wait_ge(aij_ready, n + 1)
                    for t in range(NT):
                        ins = act.activation(msg[:, t], out_of(f"ai.{n}")[:, 0:N], ACT.Tanh, bias=aij[:, 1, t:t + 1])
                        if t < NT - 1:
                            ins.then_inc(tanh_done, 1)
                        else:
                            emptied(ins, f"ai.{n}")
                    act.wait_ge(msg_f, n + 1)
                    if n:
                        wait_full(act, f"hop.{n - 1}.2")
                    hi_part(msg2[:, 0], msg[:])
                if kind == "hop_sum" and s[1] < HOPS - 1:
                    wait_full(act, f"hop.{s[1]}.{NT - 1}")
                    for t in range(NT):
                        wait_emptied(act, f"hop.{s[1]}.{t}")
                        if s[1] == 0:
                            act.wait_ge(base4_ready, t + 1)
                        hi_part(g2[:, 0, t], g[:, t])
                if kind == "context":
                    for b in range(3):
                        wait_full(act, f"context.{b}")
                        act.wait_ge(ctx_f, 1)
                        np_ = min(3, KD - 3 * b)
                        src = out_of(f"context.{b}")[:, 0:130 * np_].rearrange("p (j c) -> p j c", c=130)
                        for r in range(2):
                            hs = slice(64 * r, 64 * r + 64)
                            hi_part(ctx1[hs, 0, 3 * b:3 * b + np_, hs], src[hs, :, hs])
                            hi_part(ctx1[hs, 0, 3 * b:3 * b + np_, P + r], src[hs, :, P])
                if kind == "queries":
                    wait_full(act, "context.2")
                    for j in range(KD):
                        hi_part(TT["q1T"][:, 0, j], out_of(f"q1T.{j}")[:, 0:N], f"q1T.{j}")
                if kind == "gate":
                    act.wait_ge(gate_landed, 16)
                    act.activation(gate2[:, 0].rearrange("p a b -> p (a b)"), gate[:], ACT.Copy).then_inc(gate_hi, 1)
                    for t in range(NT):
                        wait_emptied(act, f"logits.{t}")
                        act.activation(lg[:, t], lg[:, t], ACT.Exp).then_inc(lg_exp, 1)

        @block.vector
        def _(dve):
            vn, hi = [0], [0]

            def link(ins):
                vn[0] += 1
                ins.then_inc(v_chain, 1)
                dve.wait_ge(v_chain, vn[0])

            def note(ins):
                vn[0] += 1
                ins.then_inc(v_chain, 1)

            def noted():
                dve.wait_ge(v_chain, vn[0])

            def lo_part(dst, src, hi_ap, name=None, col=None):
                hi[0] += 1
                dve.wait_ge(act_hi, hi[0])
                if col is None:
                    ins = dve.tensor_tensor(dst, src, f(hi_ap), ALU.subtract)
                else:
                    ins = dve.scalar_tensor_tensor(dst, src, bias[:, col:col + 1], f(hi_ap), ALU.add, ALU.subtract)
                if name:
                    emptied(ins, name)
                return ins

            def split_unit(u):
                dve.wait_ge(hi_split, u + 1)
                dve.tensor_tensor(w_lo[:, u % RING], raw[:, u % RAW], f(w_hi[:, u % RING]),
                                  ALU.subtract).then_inc(unit_split, 1)

            def chunk_lo(tname, k, name, col=None):
                t = TT[tname]
                lo_part(t[:, 1, k], out_of(name)[:, 0:N], t[:, 0, k], name, col)

            lns = [0]

            def layer_norm(src, dst):
                for t in range(NT):
                    for c in range(2):
                        note(dve.bn_stats(stats[:, t, c], src[:, t, c * HALF:(c + 1) * HALF]))
                noted()
                for t in range(NT):
                    dve.bn_aggr(mv[:, t], stats[:, t]).then_inc(ln_stats, 1)
                lns[0] += 1
                dve.wait_ge(ln_rstd, lns[0])
                dve.wait_ge(ln_stats, NT * lns[0])
                for t in range(NT):
                    dve.tensor_scalar(dst[:, t], src[:, t], mv[:, t, 0:1], rstd[:, t:t + 1], ALU.subtract,
                                      ALU.mult).then_inc(nat_ready, 1)

            def softmax_heads(name, c, t, scale=None):
                pr = f"{name}.{c}.{t}"
                sl = slice(c * HALF, (c + 1) * HALF)
                nh = HALF // DH
                tile = {"mq": mqn, "k": kf, "q": qf}[name]
                tile = tile[:, t] if name == "mq" else tile[:, t, sl]
                wait_full(dve, pr)
                n = sub_no(name, c, t)
                m = h8[:, n % 2, 0:nh]
                if name == "mq":
                    link(dve.tensor_reduce(m, heads(out_of(pr)[:]), X, ALU.max, negate=True))
                    emptied(dve.tensor_tensor(heads(tile), heads(out_of(pr)[:]), bcast(m, [P, nh, DH]), ALU.add), pr)
                else:
                    wait_row(dve, "b" + name)
                    emptied(dve.tensor_tensor(tile, out_of(pr)[:], row("b" + name, c * HALF, (c + 1) * HALF), ALU.add), pr)
                    wait_emptied(dve, pr)
                    link(dve.tensor_reduce(m, heads(tile), X, ALU.max, negate=True))
                    dve.tensor_tensor(heads(tile), heads(tile), bcast(m, [P, nh, DH]), ALU.add).then_inc(q_sub, 1)

            def softmax_heads_end(name, c, t, scale=None):
                sl = slice(c * HALF, (c + 1) * HALF)
                nh = HALF // DH
                tile = {"mq": mqn, "k": kf, "q": qf}[name]
                tile = tile[:, t] if name == "mq" else tile[:, t, sl]
                n = sub_no(name, c, t)
                dve.wait_ge(q_exp, n)
                sm, rc = k8[:, 0, 0:nh], k8[:, 1, 0:nh]
                link(dve.tensor_reduce(sm, heads(tile), X, ALU.add))
                link(dve.reciprocal(rc, sm))
                if scale is not None:
                    link(dve.tensor_scalar(rc, rc, scale, None, ALU.mult))
                dve.tensor_tensor(heads(tile), heads(tile), bcast(rc, [P, nh, DH]), ALU.mult).then_inc(q_ready, 1)

            def abs_quant(src, width, dst, n):
                for t in range(NT):
                    note(dve.tensor_reduce(q_s[:, 2, t:t + 1], src[:, t], X, ALU.max, apply_absolute_value=True))
                noted()
                dve.wait_ge(rms_ready, n)
                link(dve.tensor_tensor(q_s[:, 3], q_s[:, 2], q_s[:, 1], ALU.mult))
                link(dve.tensor_scalar(q_s[:, 3], q_s[:, 3], EPS, None, ALU.max))
                link(dve.reciprocal(q_s[:, 4], q_s[:, 3]))
                link(dve.scalar_tensor_tensor(q_s[:, 5], q_s[:, 4], 127.0, q_s[:, 1], ALU.mult, ALU.mult))
                link(dve.tensor_scalar(q_s[:, 5 + n], q_s[:, 3], 1.0 / 127.0, w_s[:, 1, n - 1:n], ALU.mult, ALU.mult))
                for t in range(NT):
                    note(dve.tensor_scalar(src[:, t], src[:, t], q_s[:, 5, t:t + 1], ROUND, ALU.mult, ALU.add))
                noted()
                for t in range(NT):
                    dve.tensor_scalar(dst[:, t], src[:, t], ROUND, 127.0, ALU.subtract, ALU.min).then_inc(quant_ready, 1)

            def expert_split(i):
                e = i // 2
                tile = TT["h_a"] if i < KD else TT["h_b"]
                wait_emptied(dve, f"e1.{i}")
                wait_emptied(dve, f"cw.{e}")
                dve.tensor_tensor(hf[:, i % 2], hf[:, i % 2], cw_row[:, e], ALU.mult).then_inc(h_scaled, 1)
                dve.wait_ge(h_scaled, 2 * i + 1)
                hi[0] += 1
                dve.wait_ge(act_hi, hi[0])
                dve.tensor_tensor(tile[:, 1, i % KD], hf[:, i % 2], f(tile[:, 0, i % KD]), ALU.subtract).then_inc(h_scaled, 1)

            dve.wait_ge(edges_landed, 16)
            link(dve.tensor_copy(edge_f[:], edge_i[:]))
            dve.scalar_tensor_tensor(key[:], edge_f[:, 0], float(N), edge_f[:, 1], ALU.mult, ALU.add).then_inc(key_ready, 1)
            link(dve.tensor_scalar(four0[:], edge_f[:, 2], 0.0, 4.0, ALU.is_equal, ALU.mult))
            link(dve.scalar_tensor_tensor(cls[:], edge_f[:, 2], -1.0, four0[:], ALU.add, ALU.add))
            dve.wait_ge(consts, 7)
            link(dve.tensor_tensor(cls[:], cls[:], chunk_no[:], ALU.add))
            link(dve.tensor_scalar(power[:], cls[:], 8388608.0, None, ALU.mult))
            dve.wait_ge(small_landed, 32)
            link(dve.tensor_scalar(w8[:, 2], tiny_sb[:, 0:4], -1.0, None, ALU.mult))
            dve.tensor_tensor(w8[:, 0], tiny_sb[:, 0:4], w8[:, 2], ALU.min).then_inc(w8_neg, 1)
            dve.wait_ge(w8_exp, 1)
            dve.tensor_scalar(w8[:, 1], w8[:, 1], 1.0, None, ALU.add).then_inc(w8_one, 1)
            for u in range(AHEAD):
                split_unit(u)
            dve.wait_ge(w8_ln, 1)
            link(dve.tensor_scalar(w8[:, 0], tiny_sb[:, 0:4], 0.0, None, ALU.max))
            link(dve.tensor_tensor(w8[:, 2], w8[:, 2], w8[:, 0], ALU.add))
            dve.tensor_scalar(w8[:, 2], w8[:, 2], 8.0, None, ALU.mult).then_inc(w8_ready, 1)

            for s in STEPS:
                kind = s[0]
                if kind == "graph":
                    dve.wait_ge(key_ready, 1)
                    for q in range(EC // 4):
                        pr = f"keys.{q}"
                        wait_full(dve, pr)
                        for j in range(4):
                            c = 4 * q + j
                            ins = dve.scalar_tensor_tensor(same[:, c % 2], out_of(pr)[:, j * P:(j + 1) * P], key[:, c:c + 1],
                                                           later[:], ALU.is_equal, ALU.mult, accum_out=dead[:, c:c + 1])
                            if j == 3:
                                emptied(ins, pr)
                                wait_emptied(dve, pr)
                            else:
                                link(ins)
                        sl = slice(4 * q, 4 * q + 4)
                        link(dve.scalar_tensor_tensor(value[:, sl], dead[:, sl], 0.0, power[:, sl].bitcast(F32),
                                                      ALU.is_equal, ALU.mult))
                        for j in range(4):
                            c = 4 * q + j
                            if c >= 4:
                                dve.wait_ge(onehots_used, c - 3)
                            dve.tensor_scalar(onehot[:, c % 4, 0], node[:], edge_f[:, 0, c:c + 1], None, ALU.is_equal)
                            dve.tensor_scalar(onehot[:, c % 4, 1], node[:], edge_f[:, 1, c:c + 1], None, ALU.is_equal)
                            dve.tensor_scalar(onehot[:, c % 4, 2], node[:], edge_f[:, 1, c:c + 1], value[:, c:c + 1],
                                              ALU.is_equal, ALU.mult).then_inc(onehots, 1)
                        if q == 5:
                            dve.wait_ge(x_landed, 16)
                            layer_norm(x_sb, xn1)
                    for t in range(NT):
                        pr = f"last_edge.{t}"
                        wait_full(dve, pr)
                        dve.tensor_scalar(no_edge[:, t], out_of(pr)[:, 0:N], 0.0, 8 * NO_EDGE, ALU.is_equal, ALU.mult)
                        emptied(dve.tensor_scalar(edge_cls[:, t], out_of(pr)[:, 0:N].bitcast(I32), 23, 3,
                                                  ALU.logical_shift_right, ALU.bitwise_and), pr)
                if kind == "transpose":
                    if s[1] == "xn3":
                        layer_norm(x_sb, xn3)
                    if s[1] == "xn4":
                        for t in range(NT):
                            wait_emptied(dve, f"wp.1.{t}")
                        layer_norm(x_sb, xn4)
                    for k in range(KD):
                        chunk_lo(s[1], k, f"{s[1]}.{k}")
                if kind == "degree":
                    wait_full(dve, "degree")
                    emptied(dve.tensor_scalar(dis[:, 0], out_of("degree")[:, 0:2 * NT:2], 1.0, None, ALU.max), "degree")
                if kind == "norm":
                    wait_full(dve, "norm")
                    for t in range(NT):
                        ins = dve.scalar_tensor_tensor(count[:, t], count[:, t], dis[:, 1, t:t + 1], out_of("norm")[:, 0:N],
                                                       ALU.mult, ALU.mult)
                        if t == NT - 1:
                            emptied(ins, "norm")
                if kind == "unit":
                    _, u, name, i = s
                    if u + AHEAD < len(UNITS):
                        split_unit(u + AHEAD)
                    if name in ("v1", "q1", "k1"):
                        chunk_lo(name, i, f"{name}.{i}", COLS[name] + i)
                    if name in ("q2", "k2"):
                        n = "qk".index(name[0])
                        lo_part(qk[:, i % 2, n, 1], out_of(f"{name}.{i}")[:, 0:N], qk[:, i % 2, n, 0], f"{name}.{i}",
                                COLS[name] + i)
                    if name == "mk":
                        if i == 0:
                            dve.wait_ge(node_split, 2 * NT)
                        wait_full(dve, f"mk.{i}")
                        dve.tensor_reduce(mk_s[:, 0, i:i + 1], out_of(f"mk.{i}")[:, 0:N], X, ALU.max,
                                          negate=True).then_inc(mk_max, 1)
                    if name in NODE_MAJOR and i % NODE_MAJOR[name][1] == NODE_MAJOR[name][1] - 1:
                        c = i // NODE_MAJOR[name][1]
                        sl = slice(c * HALF, (c + 1) * HALF)
                        if name in ("v2", "v"):
                            full_t, part, rw = (v2f, v2, "biv") if name == "v2" else (kf, v2n, "bv")
                            wait_row(dve, rw)
                            if (name, c) == ("v2", 0):
                                dve.wait_ge(mask_ready, 1)
                            if (name, c) == ("v", 0):
                                dve.wait_ge(node_split, 4 * NT)
                            for t in range(NT):
                                pr = f"{name}.{c}.{t}"
                                wait_full(dve, pr)
                                emptied(dve.tensor_tensor(full_t[:, t, sl], out_of(pr)[:], row(rw, c * HALF, (c + 1) * HALF),
                                                          ALU.add), pr)
                            for t in range(NT):
                                wait_emptied(dve, f"{name}.{c}.{t}")
                                lo_part(part[:, 1, t, sl], full_t[:, t, sl], part[:, 0, t, sl]).then_inc(node_split, 1)
                        if name == "mv":
                            for t in range(NT):
                                lo_part(mvn[:, 1, t], out_of(f"mv.0.{t}")[:], mvn[:, 0, t], f"mv.0.{t}")
                        if name in ("mq", "k", "q"):
                            for t in range(NT):
                                softmax_heads(name, c, t)
                            for t in range(NT):
                                softmax_heads_end(name, c, t, 0.125 if name == "mq" else None)
                            if name == "k":
                                for t in range(NT):
                                    dve.wait_ge(q_ready, sub_no(name, c, t))
                                    lo_part(k2n[:, 1, t, sl], kf[:, t, sl], k2n[:, 0, t, sl]).then_inc(node_split, 1)
                        if name == "wo":
                            for t in range(NT):
                                dve.wait_ge(base1_ready, t + 1)
                                wait_full(dve, f"wo.{c}.{t}")
                                emptied(dve.tensor_tensor(base1[:, t, sl], base1[:, t, sl], out_of(f"wo.{c}.{t}")[:], ALU.add),
                                        f"wo.{c}.{t}")
                        if name == "g1":
                            wait_row(dve, "gnn_b1")
                            for t in range(NT):
                                wait_full(dve, f"g1.0.{t}")
                                emptied(dve.tensor_tensor(g[:, t], out_of(f"g1.0.{t}")[:], row("gnn_b1"), ALU.add), f"g1.0.{t}")
                            for t in range(NT):
                                wait_emptied(dve, f"g1.0.{t}")
                                lo_part(g2[:, 1, t], g[:, t], g2[:, 0, t]).then_inc(g_ready, 1)
                        if name == "wp":
                            for t in range(NT):
                                if c == 0:
                                    dve.wait_ge(base3_ready, t + 1)
                                wait_full(dve, f"wp.{c}.{t}")
                                emptied(dve.tensor_tensor(x_sb[:, t, sl], x_sb[:, t, sl], out_of(f"wp.{c}.{t}")[:], ALU.add),
                                        f"wp.{c}.{t}")
                        if name == "e2":
                            for t in range(NT):
                                dve.wait_ge(base4_ready, 2 * NT)
                                wait_full(dve, f"e2.{c}.{t}")
                                dve.tensor_tensor(x_sb[:, t, sl], x_sb[:, t, sl], out_of(f"e2.{c}.{t}")[:],
                                                  ALU.add).then_inc(out_ready, 1)
                    if name == "e1" and i >= 4:
                        expert_split(i)
                if kind == "mix0_kT":
                    for t in range(NT):
                        lo_part(mkn[:, 1, t], out_of(f"kn.{t}")[:], mkn[:, 0, t], f"kn.{t}")
                if kind == "mix0_context":
                    wait_emptied(dve, "mk.3")
                    link(dve.reciprocal(mk_s[:, 2], mk_s[:, 1]))
                    wait_full(dve, "mix_context")
                    emptied(dve.tensor_tensor(mctx[:], out_of("mix_context")[:].rearrange("p (j c) -> p j c", c=P),
                                              bcast(mk_s[:, 2], [P, KH, P]), ALU.mult), "mix_context")
                    wait_emptied(dve, "mix_context")
                    dve.memset(f(mctx2[:]), 0.0).then_inc(mctx_f, 1)
                    dve.wait_ge(mctx_f, 1)
                    for r in range(2):
                        hs = slice(64 * r, 64 * r + 64)
                        lo_part(mctx2[hs, 1, :, hs], mctx[hs, :, hs], mctx2[hs, 0, :, hs]).then_inc(mctx_ready, 1)
                if kind == "mix0_qT":
                    for j in range(KH):
                        lo_part(mqT[:, 1, j], out_of(f"qT.{j}")[:, 0:N], mqT[:, 0, j], f"qT.{j}")
                if kind == "mix0_out":
                    for j in range(KH):
                        chunk_lo("mixo", j, f"mixo.{j}")
                if kind == "scores":
                    h = s[1]
                    b = h % 2
                    if h == 0:
                        dve.wait_ge(mask_ready, 1)
                        wait_full(dve, "mixo.3")
                    if h >= 2:
                        wait_full(dve, f"pT.{h - 2}.2")
                    for t in range(NT):
                        pr = f"scores.{h}.{t}"
                        wait_full(dve, pr)
                        emptied(dve.tensor_tensor_reduce(out=prob[:, b, t], in0=out_of(pr)[:, 0:N], in1=mask[:, t], scale=1.0,
                                                         scalar=-3.0e38, op0=ALU.add, op1=ALU.max,
                                                         accum_out=top1[:, 0, t:t + 1]), pr)
                    for t in range(NT):
                        wait_emptied(dve, f"scores.{h}.{t}")
                    dve.tensor_scalar(nmax[:, b], top1[:, 0], -0.125, None, ALU.mult).then_inc(s_max, 1)
                if kind == "probs":
                    h = s[1]
                    b = h % 2
                    dve.wait_ge(s_exp, NT * (h + 1))
                    link(dve.reciprocal(rsum[:, b], rsum[:, b]))
                    for t in range(NT):
                        dve.tensor_scalar(prob[:, b, t], prob[:, b, t], rsum[:, b, t:t + 1], None, ALU.mult).then_inc(p_ready, 1)
                    for m in range(NT):
                        lo_part(probT[:, 1, m], out_of(f"pT.{h}.{m}")[:, 0:N], probT[:, 0, m], f"pT.{h}.{m}")
                if kind == "attend":
                    h = s[1]
                    hs = slice(64 * (h % 2), 64 * (h % 2) + 64)
                    lo_part(TT["o"][hs, 1, h // 2], out_of(f"attend.{h}")[hs, 0:N], TT["o"][hs, 0, h // 2], f"attend.{h}")
                if kind == "ffn_mean":
                    wait_full(dve, "w_sum")
                    emptied(dve.tensor_scalar(w_s[:, 1], out_of("w_sum")[:, 0:2], 1.0 / (D * HID), EPS, ALU.mult, ALU.max), "w_sum")
                    wait_emptied(dve, "w_sum")
                    link(dve.reciprocal(w_s[:, 0], w_s[:, 1]))
                    for w, r in enumerate((w1r, w2r)):
                        link(dve.tensor_scalar(r[:], r[:], w_s[:, 0, w:w + 1], 1.0, ALU.mult, ALU.min))
                        dve.tensor_scalar(r[:], r[:], -1.0, ROUND, ALU.max, ALU.add).then_inc(w_unit, 1)
                if kind == "ffn":
                    for t in range(NT):
                        for c in range(2):
                            wait_emptied(dve, f"wo.{c}.{t}")
                    layer_norm(base1, xn2)
                    dve.wait_ge(sq_ready, NT)
                    dve.wait_ge(nat_ready, 2 * NT)
                    abs_quant(xn2, D, xq, 1)
                    for k in range(KD // 2):
                        pr = f"xqT.{k}"
                        wait_full(dve, pr)
                        emptied(dve.tensor_scalar(xqT[:, 2 * k:2 * k + 2], out_of(pr)[:].bitcast(BF16)[:, 0:2 * N].rearrange(
                            "p (a n) -> p a n", a=2), -128.0, None, ALU.max), pr)
                    wait_row(dve, "ffn_b1")
                    for t in range(NT):
                        wait_full(dve, f"ffn_h.{t}")
                        emptied(dve.scalar_tensor_tensor(hn[:, t], out_of(f"ffn_h.{t}")[:], q_s[:, 6, t:t + 1], row("ffn_b1"),
                                                         ALU.mult, ALU.add), f"ffn_h.{t}")
                    dve.wait_ge(sq_ready, 2 * NT)
                    dve.wait_ge(h_gelu, NT)
                    abs_quant(hn, HID, hq, 2)
                    for k in range(KH // 2):
                        pr = f"hqT.{k}"
                        wait_full(dve, pr)
                        emptied(dve.tensor_scalar(hqT[:, 2 * k:2 * k + 2], out_of(pr)[:].bitcast(BF16)[:, 0:2 * N].rearrange(
                            "p (a n) -> p a n", a=2), -128.0, None, ALU.max), pr)
                    for t in range(NT):
                        dve.wait_ge(base2_ready, t + 1)
                        for c in range(2):
                            pr = f"ffn_o.{t}.{c}"
                            sl = slice(c * HALF, (c + 1) * HALF)
                            wait_full(dve, pr)
                            emptied(dve.scalar_tensor_tensor(x_sb[:, t, sl], out_of(pr)[:], q_s[:, 7, t:t + 1], base2[:, t, sl],
                                                             ALU.mult, ALU.add), pr)
                    for t in range(NT):
                        for c in range(2):
                            wait_emptied(dve, f"ffn_o.{t}.{c}")
                if kind == "hop_row":
                    n = s[1]
                    for t in range(NT):
                        wait_emptied(dve, f"hop.{n - 1}.{t}" if n else f"g1.0.{t}")
                    wait_row(dve, f"wg{n}")
                    for t in range(NT):
                        for j in range(2):
                            link(dve.tensor_tensor_reduce(out=gjunk[:], in0=g[:, t], in1=row(f"wg{n}", j * HID, (j + 1) * HID),
                                                          scale=1.0, scalar=0.0, op0=ALU.mult, op1=ALU.add,
                                                          accum_out=aij[:, j, t:t + 1]))
                    dve.tensor_scalar(aij[:, 1], aij[:, 1], tiny_sb[:, 4 + n:5 + n], None, ALU.add).then_inc(aij_ready, 1)
                    wait_emptied(dve, f"ai.{n}")
                    dve.tensor_tensor(msg[:], msg[:], count[:], ALU.mult).then_inc(msg_f, 1)
                    dve.wait_ge(msg_f, n + 1)
                    lo_part(msg2[:, 1], msg[:], msg2[:, 0]).then_inc(msg_ready, 1)
                if kind == "hop_sum":
                    n = s[1]
                    for t in range(NT):
                        pr = f"hop.{n}.{t}"
                        wait_full(dve, pr)
                        emptied(dve.tensor_tensor(g[:, t], g[:, t], out_of(pr)[:], ALU.add), pr)
                    if n < HOPS - 1:
                        for t in range(NT):
                            wait_emptied(dve, f"hop.{n}.{t}")
                            lo_part(g2[:, 1, t], g[:, t], g2[:, 0, t]).then_inc(g_ready, 1)
                if kind == "context":
                    dve.memset(f(ctx1[:]), 0.0).then_inc(ctx_f, 1)
                    dve.wait_ge(ctx_f, 1)
                    for b in range(3):
                        np_ = min(3, KD - 3 * b)
                        src = out_of(f"context.{b}")[:, 0:130 * np_].rearrange("p (j c) -> p j c", c=130)
                        hi[0] += 4
                        dve.wait_ge(act_hi, hi[0])
                        for r in range(2):
                            hs = slice(64 * r, 64 * r + 64)
                            js = slice(3 * b, 3 * b + np_)
                            note(dve.tensor_tensor(ctx1[hs, 1, js, hs], src[hs, :, hs], f(ctx1[hs, 0, js, hs]), ALU.subtract))
                            ins = dve.tensor_tensor(ctx1[hs, 1, js, P + r], src[hs, :, P], f(ctx1[hs, 0, js, P + r]),
                                                    ALU.subtract)
                            if r == 1:
                                emptied(ins, f"context.{b}")
                            else:
                                note(ins)
                if kind == "queries":
                    for j in range(KD):
                        chunk_lo("q1T", j, f"q1T.{j}")
                    for t in range(NT):
                        for b in range(3):
                            pr = f"y.{t}.{b}"
                            np_ = min(3, KD - 3 * b)
                            wait_full(dve, pr)
                            src = out_of(pr)[:, 0:130 * np_].rearrange("p (j c) -> p j c", c=130)
                            rd = den[:, 0:2 * np_]
                            link(dve.reciprocal(rd.rearrange("p (j c) -> p j c", c=2), src[:, :, P:P + 2]))
                            tmp = ytmp[:, 0:P * np_]
                            for r in range(2):
                                ins = dve.tensor_tensor(tmp.rearrange("p (j c) -> p j c", c=P)[:, :, 64 * r:64 * r + 64],
                                                        src[:, :, 64 * r:64 * r + 64],
                                                        bcast(rd.rearrange("p (j c) -> p j c", c=2)[:, :, r], [P, np_, DH]), ALU.mult)
                                if r:
                                    emptied(ins, pr)
                                else:
                                    note(ins)
                            noted()
                            wait_emptied(dve, pr)
                            qs = qf[:, t, 384 * b:384 * b + P * np_]
                            dve.tensor_tensor(qs, qs, tmp, ALU.add).then_inc(y_ready, 1)
                            dve.wait_ge(y_ready, 3 * t + b + 1)
                if kind == "gate":
                    dve.wait_ge(gate_hi, 1)
                    dve.tensor_tensor(gate2[:, 1].rearrange("p a b -> p (a b)"), gate[:],
                                      f(gate2[:, 0]).rearrange("p a b -> p (a b)"), ALU.subtract).then_inc(gate_ready, 1)
                    link(dve.memset(cw[:], 0.0))
                    dve.wait_ge(consts, 8)
                    for t in range(NT):
                        pr = f"logits.{t}"
                        wait_full(dve, pr)
                        link(dve.tensor_reduce(gsum[:, 0, t:t + 1], out_of(pr)[:, 0:EXPERTS], X, ALU.max, negate=True))
                        emptied(dve.tensor_scalar(lg[:, t], out_of(pr)[:, 0:EXPERTS], gsum[:, 0, t:t + 1], None, ALU.add), pr)
                    for t in range(NT):
                        dve.wait_ge(lg_exp, t + 1)
                        link(dve.tensor_reduce(gsum[:, 1, t:t + 1], lg[:, t], X, ALU.add))
                        link(dve.reciprocal(gsum[:, 1, t:t + 1], gsum[:, 1, t:t + 1]))
                        link(dve.tensor_scalar(lg[:, t], lg[:, t], gsum[:, 1, t:t + 1], None, ALU.mult))
                        link(dve.max(top[:, t], lg[:, t]))
                        link(dve.max_index(top_at[:, t], top[:, t], lg[:, t]))
                        link(dve.tensor_copy(top_f[:, t], top_at[:, t]))
                        link(dve.scalar_tensor_tensor(gsum[:, 2, t:t + 1], top[:, t, 0:1], 1e-8, top[:, t, 1:2], ALU.add, ALU.add))
                        link(dve.reciprocal(gsum[:, 2, t:t + 1], gsum[:, 2, t:t + 1]))
                        link(dve.tensor_scalar(top[:, t, 0:2], top[:, t, 0:2], gsum[:, 2, t:t + 1], None, ALU.mult))
                        for j in range(2):
                            link(dve.tensor_scalar(pick[:, j], expert[:], top_f[:, t, j:j + 1], top[:, t, j:j + 1],
                                                   ALU.is_equal, ALU.mult))
                        dve.tensor_tensor(cw[:, t, 0:EXPERTS], pick[:, 0], pick[:, 1], ALU.add).then_inc(cw_ready, 1)
                        dve.wait_ge(cw_ready, t + 1)
                if kind == "gate_rows":
                    wait_full(dve, "cwT")
                    emptied(dve.tensor_copy(cwT[:], out_of("cwT")[:, 0:N]), "cwT")
                    for i in range(4):
                        expert_split(i)

        @block.tensor
        def _(pe):
            HI, LO = 0, 1
            PASSES = ((HI, HI), (HI, LO), (LO, HI))

            def products(dst, terms):
                last = None
                for n, (a, b) in enumerate(terms):
                    for m, (pa, pb) in enumerate(PASSES):
                        last = pe.matmul(dst, a(pa), b(pb), start=(n == 0 and m == 0),
                                         stop=(n == len(terms) - 1 and m == 2))
                return last

            def transposes(name, srcs):
                wait_bank(pe, name)
                for n, src in enumerate(srcs):
                    last = pe.transpose(out_of(name)[:, n * P:(n + 1) * P], src, ident[:])
                full(last, name)

            def spread(name, col):
                wait_bank(pe, name)
                for t in range(NT):
                    last = pe.matmul(out_of(name)[:, t * P:(t + 1) * P], col(t).to_broadcast([P, P]), ident[:],
                                     start=True, stop=True)
                full(last, name)

            pe.wait_ge(consts, 7)
            pe.wait_ge(key_ready, 1)
            nats = {"xn1": (xn1, NT), "xn3": (xn3, 3 * NT), "xn4": (xn4, 4 * NT)}
            for s in STEPS:
                kind = s[0]
                if kind == "graph":
                    def keys(q):
                        pr = f"keys.{q}"
                        wait_bank(pe, pr)
                        for j in range(4):
                            last = pe.matmul(out_of(pr)[:, j * P:(j + 1) * P],
                                             key[:, 4 * q + j:4 * q + j + 1].to_broadcast([P, P]), ident[:],
                                             start=True, stop=True)
                        full(last, pr)

                    keys(0)
                    keys(1)
                    for t in range(NT):
                        pe.matmul(bank[t][:, 0:N], ident_b[:], diag[:, (2 - t) * P:(2 - t) * P + N], start=True, stop=False)
                    for c in range(EC):
                        pe.wait_ge(onehots, c + 1)
                        for t in range(NT):
                            src = onehot[:, c % 4, 0, t * P:(t + 1) * P]
                            a = pe.matmul(bank[t][:, 0:N], src, onehot[:, c % 4, 2], start=False, stop=(c == EC - 1))
                            b = pe.matmul(bank[3 + t][:, 0:N], src, onehot[:, c % 4, 1], start=(c == 0), stop=(c == EC - 1))
                            if c == EC - 1:
                                full(a, f"last_edge.{t}")
                                full(b, f"count.{t}")
                        if c < EC - 1:
                            b.then_inc(onehots_used, 1)
                        if c % 4 == 3 and c // 4 + 2 < EC // 4:
                            keys(c // 4 + 2)
                if kind == "transpose":
                    if s[1] == "y":
                        pe.wait_ge(y_ready, 3 * NT)
                        src = qf
                    else:
                        src, n = nats[s[1]]
                        pe.wait_ge(nat_ready, n)
                    for k in range(KD):
                        transposes(f"{s[1]}.{k}", [src[:, t, k * P:(k + 1) * P] for t in range(NT)])
                if kind == "degree":
                    wait_emptied(pe, "count.2")
                    wait_bank(pe, "degree")
                    for c in range(NT):
                        for r in range(NT):
                            last = pe.matmul(out_of("degree")[:, 2 * c:2 * c + 2], count[:, r, c * P:(c + 1) * P], ones[:, 0:2],
                                             start=(r == 0), stop=(r == NT - 1))
                    full(last, "degree")
                if kind == "norm":
                    pe.wait_ge(dis_ready, 1)
                    spread("norm", lambda t: dis[:, 1, t:t + 1])
                if kind == "unit":
                    _, u, name, i = s
                    pe.wait_ge(unit_split, u + 1)
                    w = (w_hi, w_lo)
                    slot = u % RING
                    if name in FEATURE_MAJOR:
                        src = FEATURE_MAJOR[name]
                        pr = f"{name}.{i}"
                        wait_bank(pe, pr)
                        if i == 0 and name not in ("mk", "q1", "k1"):
                            wait_emptied(pe, f"{src}.{KD - 1}")
                        if i == 0 and (name in ("v1", "e1", "q2", "k2")):
                            wait_emptied(pe, f"{src}.{KD - 2}")
                        last = products(out_of(pr)[:, 0:N],
                                        [(lambda p, k=k: w[p][:, slot, k * P:(k + 1) * P],
                                          lambda p, k=k: TT[src][:, p, k]) for k in range(KD)])
                        last.then_inc(unit_done, 1)
                    else:
                        src, per = NODE_MAJOR[name]
                        c, kk = i // per, i % per
                        if name == "e2":
                            if c == 0:
                                pe.wait_ge(h_scaled, 2 * (2 * kk + 2))
                            if i == 0:
                                pe.wait_ge(eb2_landed, 16)
                                wait_emptied(pe, "cwT")
                        elif name == "wo":
                            if i == 0:
                                wait_emptied(pe, "attend.15")
                                wait_emptied(pe, "attend.14")
                            if i == 4:
                                wait_emptied(pe, "mixo.2")
                                wait_emptied(pe, "mixo.3")
                        elif i == 0 and name in ("v2", "g1", "wp"):
                            wait_emptied(pe, f"{src}.{KD - 1}")
                            wait_emptied(pe, f"{src}.{KD - 2}")
                        for t in range(NT):
                            pr = f"{name}.{c}.{t}"
                            ts = slice(t * P, (t + 1) * P)
                            if kk == 0:
                                wait_bank(pe, pr)
                                if name == "e2":
                                    pe.matmul(out_of(pr)[:], cwT[0:EXPERTS, ts], eb2[:, c * HALF:(c + 1) * HALF],
                                              start=True, stop=False)
                            for j in range(2):
                                k = 2 * kk + j
                                if name == "e2":
                                    tile = TT["h_a"] if k < KD else TT["h_b"]
                                    k = k % KD
                                elif name == "wo":
                                    tile, k = (TT["o"], k) if k < KD else (TT["mixo"], k - KD)
                                else:
                                    tile = TT[src]
                                for m, (pa, pb) in enumerate(PASSES):
                                    last = pe.matmul(out_of(pr)[:], tile[:, pa, k, ts], w[pb][:, slot, j * HALF:(j + 1) * HALF],
                                                     start=(kk == 0 and j == 0 and m == 0 and name != "e2"),
                                                     stop=(kk == per - 1 and j == 1 and m == 2))
                            if t == NT - 1:
                                last.then_inc(unit_done, 1)
                            elif kk == per - 1:
                                full(last, pr)
                if kind == "mix0_kT":
                    wait_emptied(pe, "mk.3")
                    for t in range(NT):
                        transposes(f"kn.{t}", [ekT[:, j, t * P:(t + 1) * P] for j in range(KH)])
                if kind == "mix0_context":
                    pr = "mix_context"
                    wait_emptied(pe, "kn.2")
                    wait_emptied(pe, "kn.1")
                    wait_emptied(pe, "mv.0.2")
                    wait_bank(pe, pr)
                    for j in range(KH):
                        js = slice(j * P, (j + 1) * P)
                        last = products(out_of(pr)[:, js], [(lambda p, t=t: mkn[:, p, t, js], lambda p, t=t: mvn[:, p, t, js])
                                                            for t in range(NT)])
                    full(last, pr)
                if kind == "mix0_qT":
                    pe.wait_ge(q_ready, sub_no("mq", 0, NT - 1))
                    for j in range(KH):
                        transposes(f"qT.{j}", [mqn[:, t, j * P:(j + 1) * P] for t in range(NT)])
                if kind == "mix0_out":
                    pe.wait_ge(mctx_ready, 2)
                    for j in range(KH):
                        wait_emptied(pe, f"qT.{j}")
                    for j in range(KH):
                        pr = f"mixo.{j}"
                        wait_bank(pe, pr)
                        full(products(out_of(pr)[:, 0:N], [(lambda p: mctx2[:, p, j], lambda p: mqT[:, p, j])]), pr)
                if kind == "scores":
                    h = s[1]
                    j, hs = h // 2, slice(64 * (h % 2), 64 * (h % 2) + 64)
                    wait_emptied(pe, f"q2.{j}")
                    wait_emptied(pe, f"k2.{j}")
                    for t in range(NT):
                        pr = f"scores.{h}.{t}"
                        wait_bank(pe, pr)
                        full(products(out_of(pr)[:, 0:N], [(lambda p: qk[hs, j % 2, 0, p, t * P:(t + 1) * P],
                                                            lambda p: qk[hs, j % 2, 1, p])]), pr)
                if kind == "probs":
                    h = s[1]
                    pe.wait_ge(p_ready, NT * (h + 1))
                    for m in range(NT):
                        transposes(f"pT.{h}.{m}", [prob[:, h % 2, t, m * P:(m + 1) * P] for t in range(NT)])
                if kind == "attend":
                    h = s[1]
                    pr = f"attend.{h}"
                    if h == 0:
                        pe.wait_ge(node_split, 2 * NT)
                    wait_emptied(pe, f"pT.{h}.2")
                    wait_emptied(pe, f"pT.{h}.1")
                    wait_bank(pe, pr)
                    js = slice(h // 2 * P, (h // 2 + 1) * P)
                    full(products(out_of(pr)[:, 0:N], [(lambda p, m=m: v2[:, p, m, js], lambda p, m=m: probT[:, p, m])
                                                       for m in range(NT)]), pr)
                if kind == "ffn_mean":
                    pe.wait_ge(w_abs, 2)
                    wait_bank(pe, "w_sum")
                    full(pe.matmul(out_of("w_sum")[:, 0:2], ones[:], w_s[:, 0], start=True, stop=True), "w_sum")
                if kind == "ffn":
                    def transposes_b(name, srcs):
                        wait_bank(pe, name)
                        view = out_of(name)[:].bitcast(BF16)
                        for n, src in enumerate(srcs):
                            last = pe.transpose(view[:, n * P:(n + 1) * P], src, ident_b[:])
                        full(last, name)

                    pe.wait_ge(quant_ready, NT)
                    for k in range(KD // 2):
                        transposes_b(f"xqT.{k}", [xq[:, t, (2 * k + a) * P:(2 * k + a + 1) * P] for a in range(2) for t in range(NT)])
                    pe.wait_ge(w_quant, 2)
                    wait_emptied(pe, f"xqT.{KD // 2 - 1}")
                    wait_emptied(pe, f"xqT.{KD // 2 - 2}")
                    for t in range(NT):
                        pr = f"ffn_h.{t}"
                        wait_bank(pe, pr)
                        for k in range(KD):
                            last = pe.matmul(out_of(pr)[:], xqT[:, k, t * P:(t + 1) * P], w1q[:, k], start=(k == 0), stop=(k == KD - 1))
                        full(last, pr)
                    pe.wait_ge(quant_ready, 2 * NT)
                    for k in range(KH // 2):
                        transposes_b(f"hqT.{k}", [hq[:, t, (2 * k + a) * P:(2 * k + a + 1) * P] for a in range(2) for t in range(NT)])
                    wait_emptied(pe, "hqT.0")
                    wait_emptied(pe, "hqT.1")
                    for t in range(NT):
                        for c in range(2):
                            pr = f"ffn_o.{t}.{c}"
                            wait_bank(pe, pr)
                            for k in range(KH):
                                last = pe.matmul(out_of(pr)[:], hqT[:, k, t * P:(t + 1) * P], w2q[:, k, c * HALF:(c + 1) * HALF],
                                                 start=(k == 0), stop=(k == KH - 1))
                            full(last, pr)
                if kind == "hop_row":
                    n = s[1]
                    pe.wait_ge(aij_ready, n + 1)
                    spread(f"ai.{n}", lambda t: aij[:, 0, t:t + 1])
                if kind == "hop_sum":
                    n = s[1]
                    pe.wait_ge(msg_ready, n + 1)
                    pe.wait_ge(g_ready, NT * (n + 1))
                    for c in range(NT):
                        pr = f"hop.{n}.{c}"
                        wait_bank(pe, pr)
                        cs = slice(c * P, (c + 1) * P)
                        full(products(out_of(pr)[:], [(lambda p, r=r: msg2[:, p, r, cs], lambda p, r=r: g2[:, p, r])
                                                      for r in range(NT)]), pr)
                if kind == "context":
                    pe.wait_ge(node_split, 6 * NT)
                    for b in range(3):
                        pr = f"context.{b}"
                        wait_bank(pe, pr)
                        for j in range(3 * b, min(3 * b + 3, KD)):
                            js = slice(j * P, (j + 1) * P)
                            o = out_of(pr)[:, 130 * (j % 3):130 * (j % 3) + 130]
                            products(o[:, 0:P], [(lambda p, t=t: k2n[:, p, t, js], lambda p, t=t: v2n[:, p, t, js])
                                                 for t in range(NT)])
                            for t in range(NT):
                                for p in (HI, LO):
                                    last = pe.matmul(o[:, P:P + 2], k2n[:, p, t, js], ones_r[:], start=(t == 0 and p == HI),
                                                     stop=(t == NT - 1 and p == LO))
                        full(last, pr)
                if kind == "queries":
                    pe.wait_ge(q_ready, sub_no("q", 1, NT - 1))
                    for j in range(KD):
                        transposes(f"q1T.{j}", [qf[:, t, j * P:(j + 1) * P] for t in range(NT)])
                    for b in range(3):
                        wait_emptied(pe, f"context.{b}")
                    wait_emptied(pe, "q1T.7")
                    wait_emptied(pe, "q1T.6")
                    for t in range(NT):
                        ts = slice(t * P, (t + 1) * P)
                        for b in range(3):
                            pr = f"y.{t}.{b}"
                            wait_bank(pe, pr)
                            for j in range(3 * b, min(3 * b + 3, KD)):
                                last = products(out_of(pr)[:, 130 * (j % 3):130 * (j % 3) + 130],
                                                [(lambda p: TT["q1T"][:, p, j, ts], lambda p: ctx1[:, p, j])])
                            full(last, pr)
                if kind == "gate":
                    pe.wait_ge(gate_ready, 1)
                    wait_emptied(pe, "xn4.7")
                    wait_emptied(pe, "xn4.6")
                    for t in range(NT):
                        pr = f"logits.{t}"
                        wait_bank(pe, pr)
                        full(products(out_of(pr)[:, 0:EXPERTS], [(lambda p, k=k: TT["xn4"][:, p, k, t * P:(t + 1) * P],
                                                                  lambda p, k=k: gate2[:, p, k]) for k in range(KD)]), pr)
                if kind == "gate_rows":
                    pe.wait_ge(cw_ready, NT)
                    transposes("cwT", [cw[:, t] for t in range(NT)])
                    for e in range(EXPERTS):
                        spread(f"cw.{e}", lambda t: cw[:, t, e:e + 1])


def kernel(**inputs):
    import numpy as np
    import concourse.bacc as bacc
    from concourse.bass_utils import run_bass_kernel_spmd

    a = {k: np.asarray(v) for k, v in inputs.items()}

    def feature_major(w):
        k, m = w.shape
        return w.reshape(k // P, P, m // P, P).transpose(2, 1, 0, 3).reshape(-1, P, D)

    def node_major(w):
        k, m = w.shape
        return w.reshape(k // (2 * P), 2, P, m // HALF, HALF).transpose(3, 0, 2, 1, 4).reshape(m // HALF, k // (2 * P), P, D)

    packs = {"v1": feature_major(a["L0_gnn_wv"].T), "v2": node_major(a["L0_gnn_wiv"].T).reshape(-1, P, D),
             "mk": feature_major(a["L0_mix_Wk"]), "mv": node_major(a["L0_mix_Wv"])[0], "mq": node_major(a["L0_mix_Wq"])[0],
             "q1": feature_major(a["L0_gnn_wq"].T), "k1": feature_major(a["L0_gnn_wk"].T),
             "q2": feature_major(a["L0_gnn_wiq"].T), "k2": feature_major(a["L0_gnn_wik"].T),
             "wo": np.concatenate([node_major(a["L0_gnn_wo"].T), node_major(a["L0_mix_Wo"])], axis=1).reshape(-1, P, D),
             "g1": node_major(a["L1_gnn_W1"])[0]}
    for n in "kvq":
        packs[n] = node_major(a[f"L1_mix_W{n}"]).reshape(-1, P, D)
    packs["wp"] = node_major(a["L1_mix_Wp"]).reshape(-1, P, D)
    packs["e1"] = np.concatenate([feature_major(a["L1_ffn_W1"][e]) for e in range(EXPERTS)])
    packs["e2"] = node_major(a["L1_ffn_W2"].reshape(EXPERTS * EHID, D)).reshape(-1, P, D)
    rows = {"biv": a["L0_gnn_biv"], "bo": a["L0_gnn_bo"], "mix_bo": a["L0_mix_bo"], "ffn_b1": a["L0_ffn_b1"],
            "ffn_b2": a["L0_ffn_b2"], "gnn_b1": a["L1_gnn_b1"], "bk": a["L1_mix_bk"], "bv": a["L1_mix_bv"],
            "bq": a["L1_mix_bq"], "bp": a["L1_mix_bp"]} | {f"wg{n}": a["L1_gnn_Wg"][n, :, 0] for n in range(HOPS)}
    arrays = {
        "weights": np.stack([packs[n][i] for n, i in UNITS]),
        "x_in": np.ascontiguousarray(a["x"]),
        "edges": np.ascontiguousarray(np.stack([a["src"], a["dst"], a["edge_type_5"]]).reshape(3, EC, P).transpose(2, 0, 1)),
        "rows": np.concatenate([rows[n] for n in ROW_ORDER]),
        "cols": np.ascontiguousarray(np.concatenate(
            [a[f"L0_gnn_{n}"].reshape(KD, P) for n in ("bv", "bq", "bk", "biq", "bik")]
            + [a["L1_ffn_b1"].reshape(EXPERTS * 2, P)]).T),
        "tiny": np.concatenate([a["L0_gnn_edge_type_weights"], a["L1_gnn_bg"][:, 0]]),
        "w1_in": np.ascontiguousarray(a["L0_ffn_w1"].T.reshape(KD, P, HID).transpose(1, 0, 2).reshape(P, -1)),
        "w2_in": np.ascontiguousarray(a["L0_ffn_w2"].T.reshape(KH, P, D).transpose(1, 0, 2).reshape(P, -1)),
        "gate_in": np.ascontiguousarray(a["L1_ffn_gate_W"].reshape(KD, P, EXPERTS).transpose(1, 0, 2).reshape(P, -1)),
        "eb2_in": np.ascontiguousarray(a["L1_ffn_b2"]),
    }
    nc = bacc.Bacc("TRN2", target_bir_lowering=False, num_devices=1)
    args = [nc.dram_tensor(n, v.shape, mybir.dt.from_np(v.dtype), kind="ExternalInput").ap() for n, v in arrays.items()]
    args.append(nc.dram_tensor("out", (N, D), F32, kind="ExternalOutput").ap())
    gps_kernel(nc, *args)
    return run_bass_kernel_spmd(nc, [arrays], core_ids=[0]).results[0]["out"]
```

```python
import concourse.bass as bass
from concourse import mybir
from contextlib import ExitStack

F32 = mybir.dt.float32
F32R = mybir.dt.float32r
BF16 = mybir.dt.bfloat16
F16 = mybir.dt.float16
I32 = mybir.dt.int32
U32 = mybir.dt.uint32
ALU = mybir.AluOpType
ACT = mybir.ActivationFunctionType
X = mybir.AxisListType.X

P = 128
N = 384
NT = N // P
D = 1024
KD = D // P
H0, DH = 16, 64
HID = 512
KH = HID // P
E = 6144
EC = E // P
NTYPE = 4
HOPS = 4
EXPERTS, EHID = 8, 256
HALF = 512
EPS = 1e-5
CLIP = 1e-5
ROUND = 12582912.0
NO_EDGE = -1.0e30

GROUPS = EC // 4
LATE = 5
RAW, RING, AHEAD = 3, 4, 3

ROWS = {}
_at = 0
for _n, _l in (("biv", D), ("bo", D), ("mix_bo", D), ("ffn_b1", HID), ("ffn_b2", D), ("gnn_b1", HID),
               ("wg0", D), ("bk", D), ("wg1", D), ("bv", D), ("wg2", D), ("bq", D), ("wg3", D), ("bp", D)):
    ROWS[_n] = (_at, _l)
    _at += _l
ROW_ORDER = list(ROWS)
ROW_SLOTS = 3
COLS = {"v1": 0, "q1": 8, "k1": 16, "q2": 24, "k2": 32, "e1": 40}


def schedule():
    steps, units = [], []

    def unit(name, i):
        steps.append(("unit", len(units), name, i))
        units.append((name, i))

    def run(name, a, b):
        for i in range(a, b):
            unit(name, i)

    steps.append(("transpose", "xn1"))
    for i in range(GROUPS):
        run("v1", i, i + 1) if i < KD else run("mk", i - KD, i - KD + 1)
        steps.append(("graph", i))
    run("v2", 0, 1)
    steps.append(("degree",))
    run("v2", 1, 2)
    steps.append(("norm",))
    run("v2", 2, 8)
    run("mv", 0, 4)
    run("mq", 0, 4)
    run("q1", 0, 2)
    steps.append(("mix0_kT",))
    run("q1", 2, 4)
    steps.append(("mix0_context",))
    run("q1", 4, 6)
    steps.append(("mix0_qT",))
    run("q1", 6, 8)
    steps.append(("mix0_out",))
    run("k1", 0, 8)
    unit("q2", 0)
    unit("k2", 0)
    unit("q2", 1)
    steps.append(("scores", 0))
    steps.append(("scores", 1))
    unit("k2", 1)
    steps.append(("normalise", 0))
    for h in range(H0):
        steps.append(("probs", h))
        if h + 1 < H0:
            steps.append(("normalise", h + 1))
        if h % 2 == 0 and h // 2 + 2 < KD:
            unit("q2", h // 2 + 2)
        if h + 2 < H0:
            steps.append(("scores", h + 2))
        if h % 2 == 1 and h // 2 + 2 < KD:
            unit("k2", h // 2 + 2)
        steps.append(("attend", h))
    run("wo", 0, 6)
    steps.append(("ffn_mean",))
    run("wo", 6, 12)
    steps.append(("ffn",))
    steps.append(("transpose", "xn3"))
    run("g1", 0, 4)
    hops = {a + d: (k, n) for n, a in enumerate((1, 7, 13, 19))
            for d, k in enumerate(("hop_dot", "hop_row", "hop_msg", None, "hop_sum")) if k and (n, k) != (3, "hop_sum")}
    n = 0
    for name in ("k", "v", "q"):
        for i in range(8):
            unit(name, i)
            n += 1
            if n in hops:
                steps.append(hops[n])
            if name == "q":
                steps.extend({1: [("context",)], 5: [("queries", 0)], 6: [("y", 0)], 7: [("transpose_y", 0)]}.get(i, []))
    steps.append(("hop_sum", 3))
    steps.append(("queries", 1))
    run("wp", 0, 1)
    steps.append(("y", 1))
    run("wp", 1, 2)
    run("wp", 4, 6)
    steps.append(("transpose_y", 1))
    run("wp", 2, 4)
    steps.append(("gate_weights",))
    run("wp", 6, 8)
    steps.append(("transpose", "xn4"))
    run("e1", 0, 1)
    steps.append(("gate",))
    run("e1", 1, 2)
    steps.append(("gate_pick",))
    run("e1", 2, LATE)
    steps.append(("gate_rows",))
    run("e1", LATE, 16)
    run("e2", 0, 16)
    return steps, units


def evacuation_order(steps):
    steps = list(steps)
    for n in range(len(steps) - 1):
        if steps[n][0] == "scores" and steps[n + 1][0] == "unit" and steps[n + 1][2] == "k2" and steps[n][1] > 1:
            steps[n], steps[n + 1] = steps[n + 1], steps[n]
    return steps


STEPS, UNITS = schedule()
EVAC_STEPS = evacuation_order(STEPS)
UNIT_OF = {u: n for n, u in enumerate(UNITS)}
FEATURE_MAJOR = {"v1": "xn1", "mk": "xn1", "q1": "xn1", "k1": "xn1", "q2": "q1", "k2": "k1", "e1": "xn4"}
NODE_MAJOR = {"v2": ("v1", 4), "mv": ("xn1", 4), "mq": ("xn1", 4), "wo": ("o", 6), "g1": ("xn3", 4), "k": ("xn3", 4),
              "v": ("xn3", 4), "q": ("xn3", 4), "wp": ("y", 4), "e2": ("h", 8)}


def plan_banks():
    uses, fulls, where = [0] * 8, [0] * 8, {}

    def product(name, bank, unit=None):
        uses[bank] += 1
        if unit is None:
            fulls[bank] += 1
            where[name] = (bank, uses[bank], None, fulls[bank])
        else:
            where[name] = (bank, uses[bank], "unit", unit + 1)

    single = group = 0
    for s in STEPS:
        kind = s[0]
        if kind == "unit":
            _, u, name, i = s
            if name in FEATURE_MAJOR:
                if name in ("v1", "mk"):
                    product(f"{name}.{i}", 6, u)
                elif name in ("q2", "k2"):
                    product(f"{name}.{i}", 1 if name == "k2" and i < 2 else 0, u)
                else:
                    product(f"{name}.{i}", single % 6, u)
                    single += 1
            else:
                per = NODE_MAJOR[name][1]
                if i % per == 0:
                    for t in range(NT):
                        product(f"{name}.{i // per}.{t}", 3 * (group % 2) + t, UNIT_OF[(name, i + per - 1)] if t == NT - 1 else None)
                    group += 1
        elif kind == "graph":
            if s[1] + 1 < GROUPS:
                product(f"keys.{s[1] + 1}", 7)
            if s[1] == GROUPS - 1:
                for t in range(NT):
                    product(f"last_edge.{t}", t)
                    product(f"count.{t}", 3 + t)
        elif kind == "transpose":
            for k in range(KD):
                product(f"{s[1]}.{k}", k)
            if s[1] == "xn1":
                product("keys.0", 7)
        elif kind == "transpose_y":
            for k in range(4 * s[1], 4 * s[1] + 4):
                product(f"y.{k}", 6 + k % 2)
        elif kind == "degree":
            product("degree", 7)
        elif kind == "norm":
            product("norm", 7)
        elif kind == "mix0_kT":
            for t in range(NT):
                product(f"kn.{t}", 6 + t % 2)
        elif kind == "mix0_context":
            product("mix_context", 7)
        elif kind == "mix0_qT":
            for j in range(KH):
                product(f"qT.{j}", 6 + j % 2)
        elif kind == "mix0_out":
            for j in range(KH):
                product(f"mixo.{j}", 6 + j % 2)
        elif kind == "scores":
            for t in range(NT):
                product(f"scores.{s[1]}.{t}", (2, 3, 6)[t])
        elif kind == "probs":
            for m in range(NT):
                product(f"pT.{s[1]}.{m}", (4, 5, 1)[m])
        elif kind == "attend":
            product(f"attend.{s[1]}", 7)
        elif kind == "ffn_mean":
            product("w_sum", 7)
        elif kind == "ffn":
            for k in range(KD // 2):
                product(f"xqT.{k}", 6 + k % 2)
            for t in range(NT):
                product(f"ffn_h.{t}", t)
            for k in range(KH // 2):
                product(f"hqT.{k}", 6 + k % 2)
            for t in range(NT):
                for c in range(2):
                    product(f"ffn_o.{t}.{c}", 3 * c + t)
        elif kind == "hop_row":
            product(f"ai.{s[1]}", 6)
        elif kind == "hop_sum":
            for t in range(NT):
                product(f"hop.{s[1]}.{t}", 7 if t % 2 == 0 else 6)
        elif kind == "context":
            for b in range(3):
                product(f"context.{b}", 6 + b % 2)
        elif kind == "queries":
            for j in range(4 * s[1], 4 * s[1] + 4):
                product(f"q1T.{j}", 6 + j % 2)
        elif kind == "y":
            for t in range(NT):
                for b in range(2):
                    product(f"yn.{s[1]}.{t}.{b}", 6 + b)
        elif kind == "gate":
            product("logitsT", 6)
        elif kind == "gate_pick":
            product("logits", 7)
        elif kind == "gate_rows":
            product("cwT", 7)
            for e in range(EXPERTS):
                product(f"cw.{e}", 6 + e % 2)
    return where


WHERE = plan_banks()


def sub_no(name, c, t):
    return {"mq": 0, "k": NT, "q": 3 * NT}[name] + NT * c + t + 1


def gps_kernel(nc, weights, x_in, edges, rows, cols, tiny, w1_in, w2_in, gate_in, eb2_in, out):
    with ExitStack() as ctx:
        def sem(name):
            return ctx.enter_context(nc.semaphore(name))

        base = (nc.sbuf_base + 63) // 64 * 64
        fence = ctx.enter_context(nc.sbuf_tensor("fence", [P, (nc.sbuf_usable_end - nc.sbuf_base) // 4 - 16], F32))
        del fence

        def at(name, shape, dt, kib):
            return nc.alloc_sbuf_tensor_at(name, shape, dt, offset=base + int(kib * 1024))

        XA, R0, R1, R2, R3, AT, MASK, CNT, RAWS, HIS, LOS, ROWS_AT, SMALL = (
            0, 12, 36, 60, 84.25, 108.25, 138.25, 142.75, 147.25, 159.25, 175.25, 191.25, 203.25)
        x_sb = at("x_sb", [P, NT, D], F32, XA)
        raw = at("raw", [P, RAW, D], F32, RAWS)
        w_hi = at("w_hi", [P, RING, D], F32R, HIS)
        w_lo = at("w_lo", [P, RING, D], F32R, LOS)
        row_sb = at("row_sb", [P, ROW_SLOTS, D], F32, ROWS_AT)
        mask = at("mask", [P, NT, N], F32, MASK)
        count = at("count", [P, NT, N], F32, CNT)

        def pair(name, chunks, width, kib):
            return at(name, [P, 2, chunks, width], F32R, kib)

        TT = {"xn1": pair("xn1T", KD, N, R0), "v1": pair("v1T", KD, N, R1), "q1": pair("q1T", KD, N, R1),
              "k1": pair("k1T", KD, N, R3), "o": pair("oT", KD, N, R0), "mixo": pair("mixoT", KH, N, XA),
              "xn3": pair("xn3T", KD, N, R0), "q1T": pair("qT_l1", KD, N, R3), "y": at("yT", [P, KD, 2, N], F32R, R1).rearrange("p k a n -> p a k n"),
              "xn4": pair("xn4T", KD, N, R0), "h_a": pair("hT_a", KD, N, R1), "h_b": pair("hT_b", KD, N, R3)}
        xn1 = at("xn1_nat", [P, NT, D], F32, R2 + 10)
        onehot = at("onehot", [P, 8, 3, N], BF16, R3 + 2)
        edge_i = at("edge_i", [P, 3, EC], I32, R2)
        edge_f = at("edge_f", [P, 3, EC], F32, R2 + 1)
        key = at("key", [P, EC], F32, R2 + 2)
        four0 = at("four0", [P, EC], F32, R2 + 2.25)
        cls = at("cls", [P, EC], F32, R2 + 2.5)
        power = at("power", [P, EC], I32, R2 + 2.75)
        dead = at("dead", [P, EC], F32, R2 + 3)
        value = at("value", [P, EC], F32, R2 + 3.25)
        chunk_no = at("chunk_no", [P, EC], I32, R2 + 3.5)
        same = at("same", [P, 2, P], F32, R2 + 4)
        later = at("later", [P, P], F32, R2 + 5)
        node_i = at("node_i", [P, N], I32, R2 + 5.5)
        node = at("node", [P, N], F16, R2 + 7)
        diag = at("diag", [P, 5 * P], BF16, R2 + 8)
        key_part = at("key_part", [P, 2, EC], F16, R2 + 9.25)
        edge_cls = at("edge_cls", [P, NT, N], I32, R3 + 2)
        no_edge = at("no_edge", [P, NT, N], F32, R3 + 6.5)
        picked = at("picked", [P, 2, NT, N], F32, R3 + 11)
        v2f = at("v2f", [P, NT, D], F32, AT + 18)
        v2 = at("v2", [P, 2, NT, D], F32R, R2)
        qcat = at("qcat", [P, 2, 2, N], F32R, AT)
        kcat = at("kcat", [P, 2, 2, N], F32R, AT + 6)
        prob = at("prob", [P, 2, NT, N], F32, AT + 12)
        probT = at("probT", [P, 2, NT, N], F32R, AT + 21)
        ekT = at("ekT", [P, KH, N], F32, AT)
        mqn = at("mqn", [P, NT, HID], F32, AT + 6)
        mqT = at("mqT", [P, 2, KH, N], F32R, AT + 12)
        mctx = at("mctx", [P, KH, P], F32, AT + 24)
        mctx2 = at("mctx2", [P, 2, KH, P], F32R, AT + 26)
        mkn = at("mkn", [P, 2, NT, HID], F32R, R3)
        mvn = at("mvn", [P, 2, NT, HID], F32R, R3 + 12)
        base1 = at("base1", [P, NT, D], F32, R1)
        base2 = at("base2", [P, NT, D], F32, R1 + 12)
        w1r = at("w1r", [P, KD * HID], F32, R2)
        w2r = at("w2r", [P, KH * D], F32, R3)
        w1q = at("w1q", [P, KD, HID], BF16, R2 + 16)
        w2q = at("w2q", [P, KH, D], BF16, R3 + 16)
        xn2 = at("xn2_nat", [P, NT, D], F32, R0)
        xq = at("xq", [P, NT, D], BF16, R0 + 12)
        xqT = at("xqT", [P, KD, N], BF16, R0 + 18)
        hn = at("hn", [P, NT, HID], F32, AT)
        hq = at("hq", [P, NT, HID], BF16, AT + 6)
        hqT = at("hqT", [P, KH, N], BF16, AT + 9)
        junk = at("junk", [P, D], F32, AT + 12)
        xn3 = at("xn3_nat", [P, NT, D], F32, R2)
        g = at("g", [P, NT, HID], F32, AT)
        g2 = at("g2", [P, 2, NT, HID], F32R, AT + 6)
        msg = at("msg", [P, NT, N], F32, MASK)
        msg2 = at("msg2", [P, 2, NT, N], F32R, AT + 18)
        gjunk = at("gjunk", [P, HID], F32, AT + 27)
        kf = at("kf", [P, NT, D], F32, R1)
        k2n = at("k2n", [P, 2, NT, D], F32R, R3)
        v_hi = at("v_hi", [P, NT, KD, P + 2], F32R, R2)
        v_lo = at("v_lo", [P, NT, KD, P], F32R, R2 + 12.1875)
        qf = at("qf", [P, NT, D], F32, R2)
        ctx1 = at("ctx1", [P, 2, KD, P + 2], F32R, R1 + 12)
        ytmp = at("ytmp", [P, 3 * P], F32, R1 + 21)
        xn4 = at("xn4_nat", [P, NT, D], F32, R2)
        cw_row = at("cw_row", [P, EXPERTS, N], F32, AT)
        hf = at("hf", [P, 2, N], F32, AT + 12)
        gate = at("gate", [P, KD * EXPERTS], F32, AT + 15)
        gate2 = at("gate2", [P, 2, KD, P], F32R, AT + 16)
        eb2 = at("eb2", [EXPERTS, D], F32, AT + 24)
        lgT = at("lgT", [P, N], F32, AT + 28)
        cw = at("cw", [P, NT, P], F32, MASK)
        cwT = at("cwT", [P, N], F32, MASK + 1.5)
        lg = at("lg", [P, NT, EXPERTS], F32, MASK + 3)
        top = at("top", [P, NT, 8], F32, MASK + 3.125)
        top_at = at("top_at", [P, NT, 8], U32, MASK + 3.25)
        top_f = at("top_f", [P, NT, 8], F32, MASK + 3.375)
        gsum = at("gsum", [P, 4, NT], F32, MASK + 3.5)
        pick = at("pick", [P, 2, EXPERTS], F32, MASK + 3.5625)
        expert = at("expert", [P, EXPERTS], F32, MASK + 3.625)
        expert_i = at("expert_i", [P, EXPERTS], I32, MASK + 3.6875)
        ident = at("ident", [P, P], F32, SMALL)
        ident_b = at("ident_b", [P, P], BF16, SMALL + 0.5)
        ones = at("ones", [P, P], F32, SMALL + 0.75)
        ident_h = at("ident_h", [P, P], F16, SMALL + 3.125)
        bias = at("bias", [P, 56], F32, SMALL + 1.3125)
        tiny_sb = at("tiny_sb", [P, 8], F32, SMALL + 1.5625)
        w8 = at("w8", [P, 3, 4], F32, SMALL + 1.625)
        stats = at("stats", [P, NT, 2, 6], F32, SMALL + 1.6875)
        mv = at("mv", [P, NT, 2], F32, SMALL + 1.875)
        rstd = at("rstd", [P, NT], F32, SMALL + 1.9375)
        minus_half = at("minus_half", [P, 2 * NT], F32, SMALL + 2)
        dis = at("dis", [P, 2, NT], F32, SMALL + 2.0625)
        top1 = at("top1", [P, 2, NT], F32, SMALL + 2.125)
        rsum = at("rsum", [P, 2, NT], F32, SMALL + 2.1875)
        nmax = at("nmax", [P, 2, NT], F32, SMALL + 2.25)
        mk_s = at("mk_s", [P, 3, KH], F32, SMALL + 2.3125)
        h8 = at("h8", [P, 2, 16], F32, SMALL + 2.375)
        q_s = at("q_s", [P, 8, NT], F32, SMALL + 2.5)
        w_s = at("w_s", [P, 2, 2], F32, SMALL + 2.625)
        aij = at("aij", [P, 2, NT], F32, SMALL + 2.6875)
        den = at("den", [P, 6], F32, SMALL + 2.75)
        k8 = at("k8", [P, 2, 16], F32, SMALL + 2.8125)
        span = at("span", [P, 2, 2, NT], F32, SMALL + 2.9375)
        power_in = at("power_in", [P, 2, NT], F32, SMALL + 3)
        power_out = at("power_out", [P, 2, NT], F32, SMALL + 3.0625)

        bank = [ctx.enter_context(nc.psum_tensor(f"bank{b}", [P, 512], F32)) for b in range(8)]

        bank_full = [sem(f"bank_full{b}") for b in range(8)]
        bank_emptied = [sem(f"bank_emptied{b}") for b in range(8)]
        raw_landed = [sem(f"raw_landed{r}") for r in range(RAW)]
        hi_split = sem("hi_split")
        unit_split = sem("unit_split")
        unit_done = sem("unit_done")
        act_hi = sem("act_hi")
        row_landed = [sem(f"row_landed{r}") for r in range(ROW_SLOTS)]
        x_landed = sem("x_landed")
        x_tile = [sem(f"x_tile{t}") for t in range(NT)]
        small_landed = sem("small_landed")
        edges_landed = sem("edges_landed")
        consts = sem("consts")
        onehots = sem("onehots")
        onehots_used = sem("onehots_used")
        key_ready = sem("key_ready")
        w8_exp, w8_ln, w8_neg, w8_one, w8_ready = (sem(n) for n in ("w8_exp", "w8_ln", "w8_neg", "w8_one", "w8_ready"))
        mask_ready = sem("mask_ready")
        ln_stats, ln_rstd, nat_ready = sem("ln_stats"), sem("ln_rstd"), sem("nat_ready")
        dis_ready = sem("dis_ready")
        v_ones = sem("v_ones")
        node_split = sem("node_split")
        mk_max, mk_exp = sem("mk_max"), sem("mk_exp")
        lgT_ready = sem("lgT_ready")
        gate_zero = sem("gate_zero")
        power_ready, power_done = sem("power_ready"), sem("power_done")
        q_sub, q_exp, q_ready = sem("q_sub"), sem("q_exp"), sem("q_ready")
        mctx_f, mctx_ready = sem("mctx_f"), sem("mctx_ready")
        s_max, s_exp, p_ready = sem("s_max"), sem("s_exp"), sem("p_ready")
        k_twice = sem("k_twice")
        base1_ready, base2_ready = sem("base1_ready"), sem("base2_ready")
        ffn_landed, w_abs, w_unit, w_quant = sem("ffn_landed"), sem("w_abs"), sem("w_unit"), sem("w_quant")
        sq_ready, rms_ready, quant_ready = sem("sq_ready"), sem("rms_ready"), sem("quant_ready")
        h_gelu = sem("h_gelu")
        aij_ready, tanh_done, msg_f, msg_ready = sem("aij_ready"), sem("tanh_done"), sem("msg_f"), sem("msg_ready")
        g_ready = sem("g_ready")
        base3_ready, base4_ready = sem("base3_ready"), sem("base4_ready")
        ctx_f, ctx_ready, y_ready = sem("ctx_f"), sem("ctx_ready"), sem("y_ready")
        gate_landed, eb2_landed, gate_hi, gate_ready = sem("gate_landed"), sem("eb2_landed"), sem("gate_hi"), sem("gate_ready")
        lg_exp, cw_ready = sem("lg_exp"), sem("cw_ready")
        h_relu, h_scaled = sem("h_relu"), sem("h_scaled")
        out_ready, out_stored = sem("out_ready"), sem("out_stored")
        v_chain, a_chain, p_chain = sem("v_chain"), sem("a_chain"), sem("p_chain")
        block = ctx.enter_context(nc.Block())

        def f(ap):
            return ap.bitcast(F32)

        def out_of(name):
            return bank[WHERE[name][0]]

        def wait_bank(pe, name):
            b, n, _, _ = WHERE[name]
            if n > 1:
                pe.wait_ge(bank_emptied[b], n - 1)

        def wait_full(eng, name):
            b, _, by, n = WHERE[name]
            eng.wait_ge(unit_done if by else bank_full[b], n)

        def full(ins, name):
            ins.then_inc(bank_full[WHERE[name][0]], 1)

        def wait_emptied(eng, name):
            b, n, _, _ = WHERE[name]
            eng.wait_ge(bank_emptied[b], n)

        def emptied(ins, name):
            ins.then_inc(bank_emptied[WHERE[name][0]], 1)

        def wait_unit(eng, name, i):
            eng.wait_ge(unit_done, UNIT_OF[(name, i)] + 1)

        def row_slot(name):
            i = ROW_ORDER.index(name)
            return i % ROW_SLOTS, 16 * (i // ROW_SLOTS + 1)

        def wait_row(eng, name):
            slot, n = row_slot(name)
            eng.wait_ge(row_landed[slot], n)

        def row(name, a=0, b=None):
            return row_sb[:, row_slot(name)[0], a:ROWS[name][1] if b is None else b]

        def bcast(ap, shape):
            return ap.unsqueeze(len(shape) - 1).to_broadcast(shape)

        def heads(ap):
            return ap.rearrange("p (h d) -> p h d", d=DH)

        @block.sync
        def _(sp):
            sp.dma_start(edge_i[:], edges).then_inc(edges_landed, 16)
            for t in range(NT):
                sp.dma_start(x_sb[:, t], x_in[t * P:(t + 1) * P, :]).then_inc(x_tile[t], 16)
            sp.dma_start(bias[:], cols).then_inc(small_landed, 16)
            sp.dma_start(tiny_sb[:], tiny.partition_broadcast(P)).then_inc(small_landed, 16)

            def load_row(name, free=None):
                if free:
                    free()
                o, n = ROWS[name]
                sp.dma_start(row(name), rows[o:o + n].partition_broadcast(P)).then_inc(row_landed[row_slot(name)[0]], 16)

            for s in STEPS:
                if s[0] == "unit":
                    _, u, name, i = s
                    if u >= RAW:
                        sp.wait_ge(unit_split, u - RAW + 1)
                    sp.dma_start(raw[:, u % RAW, :], weights[u]).then_inc(raw_landed[u % RAW], 16)
                    if (name, i) == ("v1", 4):
                        for n in ROW_ORDER[:ROW_SLOTS]:
                            load_row(n)
                    if (name, i) == ("wo", 1):
                        wait_unit(sp, "q2", 7)
                        sp.dma_start(base1[:], x_in.rearrange("(t p) d -> p t d", p=P)).then_inc(x_landed, 16)
                        load_row("ffn_b1", lambda: wait_emptied(sp, "v2.1.2"))
                    if (name, i) == ("wo", 3):
                        wait_full(sp, "attend.15")
                        sp.dma_start(w1r[:], w1_in).then_inc(ffn_landed, 16)
                    if (name, i) == ("wo", 5):
                        sp.dma_start(w2r[:], w2_in).then_inc(ffn_landed, 16)
                    if (name, i) == ("wo", 11):
                        load_row("ffn_b2", lambda: sp.wait_ge(base1_ready, NT))
                        load_row("gnn_b1")
                    if (name, i) == ("g1", 3):
                        load_row("wg0", lambda: wait_emptied(sp, "ffn_h.2"))
                        load_row("bk", lambda: sp.wait_ge(base2_ready, NT))
                    if (name, i) == ("k", 2):
                        load_row("wg1", lambda: wait_emptied(sp, "g1.0.2"))
                    if (name, i) == ("k", 6):
                        load_row("bv", lambda: sp.wait_ge(aij_ready, 1))
                    if (name, i) == ("v", 2):
                        load_row("wg2", lambda: wait_emptied(sp, "k.1.2"))
                    if (name, i) == ("v", 5):
                        load_row("bq", lambda: sp.wait_ge(aij_ready, 2))
                    if (name, i) == ("q", 2):
                        load_row("wg3", lambda: wait_emptied(sp, "v.1.2"))
                    if (name, i) == ("q", 4):
                        load_row("bp", lambda: sp.wait_ge(aij_ready, 3))
                    if (name, i) == ("wp", 3):
                        sp.wait_ge(base3_ready, NT)
                        sp.dma_start(gate[:], gate_in).then_inc(gate_landed, 16)
                        sp.dma_start(eb2[:], eb2_in).then_inc(eb2_landed, 16)
            n = 0
            for c in range(2):
                for t in range(NT):
                    n += 1
                    sp.wait_ge(out_ready, n)
                    sp.dma_start(out[t * P:(t + 1) * P, c * HALF:(c + 1) * HALF],
                                 x_sb[:, t, c * HALF:(c + 1) * HALF]).then_inc(out_stored, 16)
            sp.wait_ge(out_stored, 16 * n)

        @block.gpsimd
        def _(pool):
            pn = [0]

            def link(ins):
                pn[0] += 1
                ins.then_inc(p_chain, 1)
                pool.wait_ge(p_chain, pn[0])

            pool.memset(minus_half[:], -0.5).then_inc(consts, 1)
            link(pool.memset(ident[:], 0.0))
            link(pool.affine_select(out=ident[:], in_=ident[:], compare_op=ALU.not_equal, fill=1.0, base=0,
                                    pattern=[[-1, P]], channel_multiplier=1))
            pool.tensor_copy(ident_b[:], ident[:]).then_inc(consts, 1)
            link(pool.memset(ones[:], 1.0))
            pool.tensor_copy(ident_h[:], ident[:]).then_inc(consts, 1)
            pool.affine_select(out=later[:], in_=ones[:], compare_op=ALU.is_gt, fill=0.0, base=0,
                               pattern=[[1, P]], channel_multiplier=-1).then_inc(consts, 1)
            link(pool.iota(node_i[:], pattern=[[1, N]], base=0, channel_multiplier=0))
            pool.tensor_copy(node[:], node_i[:]).then_inc(consts, 1)
            pool.iota(chunk_no[:], pattern=[[4, EC]], base=32, channel_multiplier=0).then_inc(consts, 1)
            link(pool.memset(diag[:], 0.0))
            pool.tensor_scalar(diag[:, 2 * P:3 * P], ident[:], 2.0 ** -96, None, ALU.mult).then_inc(consts, 1)

            def power(dst, src, scale, n):
                link(pool.tensor_scalar(dst, src, scale, EPS, ALU.mult, ALU.add))
                return pool.tensor_tensor(dst, dst, minus_half[:, 0:n], ALU.pow)

            def norm_power():
                lns[0] += 1
                pool.wait_ge(ln_stats, NT * lns[0])
                power(rstd[:], mv[:, :, 1], 1.0, NT).then_inc(ln_rstd, 1)

            lns = [0]
            norm_power()
            for s in STEPS:
                if s[:2] in (("transpose", "xn3"), ("transpose", "xn4")):
                    norm_power()
                if s[0] == "unit" and s[2] == "k2":
                    wait_emptied(pool, f"k2.{s[3]}")
                    for r in range(2):
                        own, other = slice(64 * r, 64 * r + 64), slice(64 - 64 * r, 128 - 64 * r)
                        pool.dma_start(f(kcat[other, r]), f(kcat[own, r])).then_inc(k_twice, 16)
                if s[0] == "degree":
                    wait_emptied(pool, "degree")
                    pool.tensor_tensor(dis[:, 1], dis[:, 0], minus_half[:, 0:NT], ALU.pow).then_inc(dis_ready, 1)
                    for t in range(NT):
                        wait_emptied(pool, f"last_edge.{t}")
                    wait_full(pool, "count.2")
                    pool.wait_ge(w8_ready, 1)
                    link(pool.tensor_scalar(picked[:, 0], edge_cls[:], 0.0, w8[:, 2, 0:1], ALU.is_equal, ALU.mult))
                    link(pool.tensor_tensor(mask[:], no_edge[:], picked[:, 0], ALU.add))
                    for k in range(1, NTYPE):
                        link(pool.tensor_scalar(picked[:, k % 2], edge_cls[:], float(k), w8[:, 2, k:k + 1],
                                                ALU.is_equal, ALU.mult))
                        ins = pool.tensor_tensor(mask[:], mask[:], picked[:, k % 2], ALU.add)
                        if k < NTYPE - 1:
                            link(ins)
                    ins.then_inc(mask_ready, 1)
                if s[0] == "attend" and s[1] == H0 - 1:
                    pool.wait_ge(x_landed, 16)
                    wait_row(pool, "bo")
                    wait_row(pool, "mix_bo")
                    link(pool.tensor_tensor(row("bo"), row("bo"), row("mix_bo"), ALU.add))
                    for t in range(NT):
                        pool.tensor_tensor(base1[:, t], base1[:, t], row("bo"), ALU.add).then_inc(base1_ready, 1)
                if s[0] == "ffn_mean":
                    for w in range(2):
                        pool.wait_ge(w_unit, w + 1)
                        src, dst = ((w1r, w1q), (w2r, w2q))[w]
                        pool.tensor_scalar(dst[:].rearrange("p a b -> p (a b)"), src[:], ROUND, None,
                                           ALU.subtract).then_inc(w_quant, 1)
                if s[0] == "ffn":
                    pool.wait_ge(power_ready, 1)
                    pool.tensor_tensor(power_out[:].rearrange("p a t -> p (a t)"), power_in[:].rearrange("p a t -> p (a t)"),
                                       minus_half[:], ALU.pow).then_inc(power_done, 1)
                    wait_row(pool, "ffn_b2")
                    for t in range(NT):
                        wait_emptied(pool, f"wo.0.{t}")
                        wait_emptied(pool, f"wo.1.{t}")
                        pool.tensor_tensor(base2[:, t], base1[:, t], row("ffn_b2"), ALU.add).then_inc(base2_ready, 1)
                    pool.wait_ge(sq_ready, NT)
                    power(q_s[:, 1], q_s[:, 0], 1.0 / HID, NT).then_inc(rms_ready, 1)
                if s[0] == "hop_sum" and s[1] == 0:
                    pool.wait_ge(g_ready, NT)
                    for t in range(NT):
                        pool.tensor_tensor(x_sb[:, t, 0:HID], x_sb[:, t, 0:HID], f(g2[:, 0, t]), ALU.add).then_inc(p_chain, 1)
                        pn[0] += 1
                    pool.wait_ge(p_chain, pn[0])
                    for t in range(NT):
                        pool.tensor_tensor(x_sb[:, t, 0:HID], x_sb[:, t, 0:HID], f(g2[:, 1, t]), ALU.add).then_inc(base4_ready, 1)
                if s[0] == "hop_sum" and s[1] == HOPS - 1:
                    wait_row(pool, "bp")
                    for t in range(NT):
                        wait_emptied(pool, f"hop.{HOPS - 1}.{t}")
                    pool.wait_ge(base4_ready, NT)
                    for t in range(NT):
                        pool.tensor_tensor(x_sb[:, t, HID:D], x_sb[:, t, HID:D], g[:, t], ALU.add).then_inc(p_chain, 1)
                        pn[0] += 1
                    pool.wait_ge(p_chain, pn[0])
                    for t in range(NT):
                        pool.tensor_tensor(x_sb[:, t], x_sb[:, t], row("bp"), ALU.add).then_inc(base3_ready, 1)
                if s[0] == "gate_weights":
                    pool.wait_ge(base3_ready, NT)
                    pool.memset(f(gate2[:]), 0.0).then_inc(gate_zero, 1)
                if s[0] == "gate":
                    pool.wait_ge(nat_ready, 3 * NT)
                    link(pool.iota(expert_i[:], pattern=[[1, EXPERTS]], base=0, channel_multiplier=0))
                    pool.tensor_copy(expert[:], expert_i[:]).then_inc(consts, 1)
                    for t in range(NT):
                        pool.tensor_tensor(x_sb[:, t], x_sb[:, t], xn4[:, t], ALU.add).then_inc(base4_ready, 1)

        @block.scalar
        def _(act):
            hi = [0]

            def hi_part(dst, src, name=None, bias=0.0):
                if name:
                    wait_full(act, name)
                act.activation(dst, src, ACT.Identity, bias=bias).then_inc(act_hi, 1)
                hi[0] += 1

            def split_unit(u):
                act.wait_ge(raw_landed[u % RAW], 16 * (u // RAW + 1))
                if u >= RING:
                    act.wait_ge(unit_done, u - RING + 1)
                act.activation(w_hi[:, u % RING], raw[:, u % RAW], ACT.Copy).then_inc(hi_split, 1)

            def chunk_hi(tname, k, name, col=None):
                b = 0.0 if col is None else bias[:, col:col + 1]
                hi_part(TT[tname][:, 0, k], out_of(name)[:, 0:N], name, b)

            def expert(i):
                wait_full(act, f"e1.{i}")
                if i >= 2:
                    act.wait_ge(h_scaled, 2 * (i - 2) + 2)
                emptied(act.activation(hf[:, i % 2], out_of(f"e1.{i}")[:, 0:N], ACT.Relu,
                                       bias=bias[:, COLS["e1"] + i:COLS["e1"] + i + 1]), f"e1.{i}")
                act.wait_ge(h_scaled, 2 * i + 1)
                hi_part(TT["h_a" if i < KD else "h_b"][:, 0, i % KD], hf[:, i % 2])

            act.wait_ge(small_landed, 32)
            act.wait_ge(w8_neg, 1)
            act.activation(w8[:, 1], w8[:, 0], ACT.Exp).then_inc(w8_exp, 1)
            for u in range(AHEAD):
                split_unit(u)
            for s in EVAC_STEPS:
                kind = s[0]
                if s == ("graph", 0):
                    act.wait_ge(w8_one, 1)
                    act.activation(w8[:, 2], w8[:, 1], ACT.Ln).then_inc(w8_ln, 1)
                if s == ("graph", GROUPS - 1):
                    for t in range(NT):
                        wait_full(act, f"count.{t}")
                        emptied(act.activation(count[:, t], out_of(f"count.{t}")[:, 0:N], ACT.Copy), f"count.{t}")
                if kind == "transpose":
                    if s[1] == "xn4":
                        wait_unit(act, "q", 7)
                    for k in range(KD):
                        chunk_hi(s[1], k, f"{s[1]}.{k}")
                if kind == "transpose_y":
                    if s[1] == 1:
                        wait_full(act, "yn.1.2.1")
                    for k in range(4 * s[1], 4 * s[1] + 4):
                        chunk_hi("y", k, f"y.{k}")
                if kind == "unit":
                    _, u, name, i = s
                    if u + AHEAD < len(UNITS):
                        split_unit(u + AHEAD)
                    if name in ("v1", "q1", "k1"):
                        if (name, i) == ("q1", 0):
                            wait_unit(act, "v2", 7)
                        if (name, i) == ("k1", 0):
                            wait_full(act, "mixo.3")
                        chunk_hi(name, i, f"{name}.{i}", COLS[name] + i)
                    if name in ("q2", "k2"):
                        behind = 2 * i - 3 if name == "q2" else 2 * i - 1
                        if behind > 0:
                            wait_full(act, f"scores.{behind}.2")
                        for r in range(2):
                            hs = slice(64 * r, 64 * r + 64)
                            dst = qcat[hs, i % 2, r] if name == "q2" else kcat[hs, r, 0]
                            hi_part(dst, out_of(f"{name}.{i}")[hs, 0:N], f"{name}.{i}",
                                    bias[hs, COLS[name] + i:COLS[name] + i + 1])
                    if name == "mk":
                        act.wait_ge(mk_max, i + 1)
                        emptied(act.activation(ekT[:, i], out_of(f"mk.{i}")[:, 0:N], ACT.Exp, bias=mk_s[:, 0, i:i + 1],
                                               accum_out=mk_s[:, 1, i:i + 1]), f"mk.{i}")
                    if name in NODE_MAJOR and i % NODE_MAJOR[name][1] == NODE_MAJOR[name][1] - 1:
                        c = i // NODE_MAJOR[name][1]
                        for t in range(NT):
                            pr = f"{name}.{c}.{t}"
                            sl = slice(c * HALF, (c + 1) * HALF)
                            if name == "v2":
                                wait_emptied(act, pr)
                                hi_part(v2[:, 0, t, sl], v2f[:, t, sl])
                            if name == "v":
                                wait_emptied(act, pr)
                                hi_part(v_hi[:, t, 4 * c:4 * c + 4, 0:P], kf[:, t, sl].rearrange("p (j c) -> p j c", c=P))
                            if name == "mv":
                                act.wait_ge(mask_ready, 1)
                                hi_part(mvn[:, 0, t], out_of(pr)[:], pr)
                            if name in ("mq", "k", "q"):
                                src = {"mq": mqn[:, t], "k": kf[:, t, sl], "q": qf[:, t, sl]}[name]
                                if name == "mq":
                                    wait_emptied(act, pr)
                                else:
                                    act.wait_ge(q_sub, sub_no(name, c, t) - NT)
                                act.activation(src, src, ACT.Exp).then_inc(q_exp, 1)
                        if name == "k":
                            for t in range(NT):
                                act.wait_ge(q_ready, sub_no(name, c, t))
                                hi_part(k2n[:, 0, t, c * HALF:(c + 1) * HALF], kf[:, t, c * HALF:(c + 1) * HALF])
                        if name == "g1":
                            for t in range(NT):
                                wait_emptied(act, f"g1.0.{t}")
                                hi_part(g2[:, 0, t], g[:, t])
                    if name == "e1" and i >= LATE:
                        expert(i)
                if kind == "gate_rows":
                    for e in range(EXPERTS):
                        wait_full(act, f"cw.{e}")
                        emptied(act.activation(cw_row[:, e], out_of(f"cw.{e}")[:, 0:N], ACT.Copy), f"cw.{e}")
                    for i in range(LATE):
                        expert(i)
                if kind == "mix0_kT":
                    for t in range(NT):
                        hi_part(mkn[:, 0, t], out_of(f"kn.{t}")[:], f"kn.{t}")
                if kind == "mix0_context":
                    act.wait_ge(mctx_f, 1)
                    for r in range(2):
                        hs = slice(64 * r, 64 * r + 64)
                        hi_part(mctx2[hs, 0, :, hs], mctx[hs, :, hs])
                if kind == "mix0_qT":
                    for j in range(KH):
                        hi_part(mqT[:, 0, j], out_of(f"qT.{j}")[:, 0:N], f"qT.{j}")
                if kind == "mix0_out":
                    for j in range(KH):
                        hi_part(TT["mixo"][:, 0, j], out_of(f"mixo.{j}")[:, 0:N], f"mixo.{j}")
                if kind == "scores":
                    h = s[1]
                    act.wait_ge(s_max, h + 1)
                    for t in range(NT):
                        act.activation(prob[:, h % 2, t], prob[:, h % 2, t], ACT.Exp, scale=0.125,
                                       bias=nmax[:, h % 2, t:t + 1], accum_out=rsum[:, h % 2, t:t + 1]).then_inc(s_exp, 1)
                if kind == "probs":
                    h = s[1]
                    if h:
                        wait_full(act, f"attend.{h - 1}")
                    for m in range(NT):
                        hi_part(probT[:, 0, m], out_of(f"pT.{h}.{m}")[:, 0:N], f"pT.{h}.{m}")
                if kind == "attend":
                    h = s[1]
                    hs = slice(64 * (h % 2), 64 * (h % 2) + 64)
                    if h == 0:
                        wait_unit(act, "k1", 7)
                    hi_part(TT["o"][hs, 0, h // 2], out_of(f"attend.{h}")[hs, 0:N], f"attend.{h}")
                if kind == "ffn_mean":
                    act.wait_ge(ffn_landed, 32)
                    for w in range(2):
                        src, dst = ((w1r, w1q), (w2r, w2q))[w]
                        act.activation(dst[:].rearrange("p a b -> p (a b)"), src[:], ACT.Abs,
                                       accum_out=w_s[:, 0, w:w + 1]).then_inc(w_abs, 1)
                if kind == "ffn":
                    for t in range(NT):
                        wait_emptied(act, f"ffn_h.{t}")
                        act.activation(hn[:, t], hn[:, t], ACT.Gelu).then_inc(h_gelu, 1)
                    for t in range(NT):
                        act.wait_ge(h_gelu, t + 1)
                        if t:
                            act.wait_ge(sq_ready, t)
                        act.activation(junk[:, 0:HID], hn[:, t], ACT.Square, accum_out=q_s[:, 0, t:t + 1]).then_inc(sq_ready, 1)
                if kind == "hop_row":
                    n = s[1]
                    wait_full(act, f"ai.{n}")
                    act.wait_ge(aij_ready, n + 1)
                    for t in range(NT):
                        ins = act.activation(msg[:, t], out_of(f"ai.{n}")[:, 0:N], ACT.Tanh, bias=aij[:, 1, t:t + 1])
                        if t < NT - 1:
                            ins.then_inc(tanh_done, 1)
                        else:
                            emptied(ins, f"ai.{n}")
                if kind == "hop_msg":
                    n = s[1]
                    act.wait_ge(msg_f, n + 1)
                    if n:
                        wait_full(act, f"hop.{n - 1}.2")
                    hi_part(msg2[:, 0], msg[:])
                if kind == "hop_sum" and s[1] < HOPS - 1:
                    wait_full(act, f"hop.{s[1]}.{NT - 1}")
                    for t in range(NT):
                        wait_emptied(act, f"hop.{s[1]}.{t}")
                        if s[1] == 0:
                            act.wait_ge(base4_ready, t + 1)
                        hi_part(g2[:, 0, t], g[:, t])
                if kind == "context":
                    for b in range(3):
                        wait_full(act, f"context.{b}")
                        act.wait_ge(ctx_f, 1)
                        np_ = min(3, KD - 3 * b)
                        src = out_of(f"context.{b}")[:, 0:130 * np_].rearrange("p (j c) -> p j c", c=130)
                        for r in range(2):
                            hs = slice(64 * r, 64 * r + 64)
                            hi_part(ctx1[hs, 0, 3 * b:3 * b + np_, hs], src[hs, :, hs])
                            hi_part(ctx1[hs, 0, 3 * b:3 * b + np_, P + r], src[hs, :, P])
                if kind == "queries":
                    if s[1] == 0:
                        wait_full(act, "context.2")
                    for j in range(4 * s[1], 4 * s[1] + 4):
                        hi_part(TT["q1T"][:, 0, j], out_of(f"q1T.{j}")[:, 0:N], f"q1T.{j}")
                if kind == "gate_weights":
                    act.wait_ge(gate_landed, 16)
                    act.wait_ge(gate_zero, 1)
                    act.activation(gate2[:, 0, :, 0:EXPERTS], gate[:].rearrange("p (k e) -> p k e", e=EXPERTS),
                                   ACT.Copy).then_inc(gate_hi, 1)
                if kind == "gate_pick":
                    wait_emptied(act, "logits")
                    for t in range(NT):
                        act.activation(lg[:, t], lg[:, t], ACT.Exp).then_inc(lg_exp, 1)

        @block.vector
        def _(dve):
            vn, hi = [0], [0]

            def link(ins):
                vn[0] += 1
                ins.then_inc(v_chain, 1)
                dve.wait_ge(v_chain, vn[0])

            def note(ins):
                vn[0] += 1
                ins.then_inc(v_chain, 1)

            def noted():
                dve.wait_ge(v_chain, vn[0])

            def lo_part(dst, src, hi_ap, name=None, col=None):
                hi[0] += 1
                dve.wait_ge(act_hi, hi[0])
                if col is None:
                    ins = dve.tensor_tensor(dst, src, f(hi_ap), ALU.subtract)
                else:
                    ins = dve.scalar_tensor_tensor(dst, src, bias[:, col:col + 1], f(hi_ap), ALU.add, ALU.subtract)
                if name:
                    emptied(ins, name)
                return ins

            def split_unit(u):
                dve.wait_ge(hi_split, u + 1)
                dve.tensor_tensor(w_lo[:, u % RING], raw[:, u % RAW], f(w_hi[:, u % RING]),
                                  ALU.subtract).then_inc(unit_split, 1)

            def chunk_lo(tname, k, name, col=None):
                t = TT[tname]
                lo_part(t[:, 1, k], out_of(name)[:, 0:N], t[:, 0, k], name, col)

            lns = [0]

            def half_stats(src, t, c):
                note(dve.bn_stats(stats[:, t, c], src[:, t, c * HALF:(c + 1) * HALF]))

            def layer_norm(src, dst):
                noted()
                for t in range(NT):
                    dve.bn_aggr(mv[:, t], stats[:, t]).then_inc(ln_stats, 1)
                lns[0] += 1
                dve.wait_ge(ln_rstd, lns[0])
                dve.wait_ge(ln_stats, NT * lns[0])
                for t in range(NT):
                    dve.tensor_scalar(dst[:, t], src[:, t], mv[:, t, 0:1], rstd[:, t:t + 1], ALU.subtract,
                                      ALU.mult).then_inc(nat_ready, 1)

            def softmax_heads(name, c, t, scale=None):
                pr = f"{name}.{c}.{t}"
                sl = slice(c * HALF, (c + 1) * HALF)
                nh = HALF // DH
                tile = {"mq": mqn, "k": kf, "q": qf}[name]
                tile = tile[:, t] if name == "mq" else tile[:, t, sl]
                wait_full(dve, pr)
                n = sub_no(name, c, t)
                m = h8[:, n % 2, 0:nh]
                if name == "mq":
                    link(dve.tensor_reduce(m, heads(out_of(pr)[:]), X, ALU.max, negate=True))
                    emptied(dve.tensor_tensor(heads(tile), heads(out_of(pr)[:]), bcast(m, [P, nh, DH]), ALU.add), pr)
                else:
                    wait_row(dve, "b" + name)
                    emptied(dve.tensor_tensor(tile, out_of(pr)[:], row("b" + name, c * HALF, (c + 1) * HALF), ALU.add), pr)
                    wait_emptied(dve, pr)
                    link(dve.tensor_reduce(m, heads(tile), X, ALU.max, negate=True))
                    dve.tensor_tensor(heads(tile), heads(tile), bcast(m, [P, nh, DH]), ALU.add).then_inc(q_sub, 1)

            def softmax_heads_end(name, c, t, scale=None):
                sl = slice(c * HALF, (c + 1) * HALF)
                nh = HALF // DH
                tile = {"mq": mqn, "k": kf, "q": qf}[name]
                tile = tile[:, t] if name == "mq" else tile[:, t, sl]
                n = sub_no(name, c, t)
                dve.wait_ge(q_exp, n)
                sm, rc = k8[:, 0, 0:nh], k8[:, 1, 0:nh]
                link(dve.tensor_reduce(sm, heads(tile), X, ALU.add))
                link(dve.reciprocal(rc, sm))
                if scale is not None:
                    link(dve.tensor_scalar(rc, rc, scale, None, ALU.mult))
                dve.tensor_tensor(heads(tile), heads(tile), bcast(rc, [P, nh, DH]), ALU.mult).then_inc(q_ready, 1)

            def hidden_quant():
                for t in range(NT):
                    dve.wait_ge(h_gelu, t + 1)
                    note(dve.tensor_reduce(q_s[:, 2, t:t + 1], hn[:, t], X, ALU.max, apply_absolute_value=True))
                noted()
                dve.wait_ge(rms_ready, 1)
                link(dve.tensor_tensor(q_s[:, 3], q_s[:, 2], q_s[:, 1], ALU.mult))
                quant_rows(q_s[:, 1], 2)
                dve.wait_ge(sq_ready, NT)
                for t in range(NT):
                    note(dve.tensor_scalar(hn[:, t], hn[:, t], q_s[:, 5, t:t + 1], ROUND, ALU.mult, ALU.add))
                noted()
                for t in range(NT):
                    dve.tensor_scalar(hq[:, t], hn[:, t], ROUND, None, ALU.subtract).then_inc(quant_ready, 1)

            def quant_rows(factor, n):
                link(dve.tensor_scalar(q_s[:, 3], q_s[:, 3], CLIP, None, ALU.max))
                link(dve.reciprocal(q_s[:, 4], q_s[:, 3]))
                link(dve.scalar_tensor_tensor(q_s[:, 5], q_s[:, 4], 127.0, factor, ALU.mult, ALU.mult))
                link(dve.tensor_scalar(q_s[:, 5 + n], q_s[:, 3], 1.0 / 127.0, w_s[:, 1, n - 1:n], ALU.mult, ALU.mult))

            def norm_quant():
                noted()
                for t in range(NT):
                    note(dve.bn_aggr(mv[:, t], stats[:, t]))
                note(dve.tensor_tensor(span[:, 0, 0], span[:, 0, 0], span[:, 0, 1], ALU.max))
                note(dve.tensor_tensor(span[:, 1, 0], span[:, 1, 0], span[:, 1, 1], ALU.min))
                noted()
                link(dve.tensor_scalar(power_in[:, 0], mv[:, :, 1], EPS, None, ALU.add))
                link(dve.reciprocal(q_s[:, 4], power_in[:, 0]))
                link(dve.tensor_tensor(power_in[:, 1], q_s[:, 4], mv[:, :, 1], ALU.mult))
                dve.tensor_scalar(power_in[:, 1], power_in[:, 1], EPS, None, ALU.add).then_inc(power_ready, 1)
                note(dve.tensor_tensor(span[:, 0, 0], span[:, 0, 0], mv[:, :, 0], ALU.subtract))
                link(dve.tensor_tensor(span[:, 1, 0], mv[:, :, 0], span[:, 1, 0], ALU.subtract))
                link(dve.tensor_tensor(q_s[:, 2], span[:, 0, 0], span[:, 1, 0], ALU.max))
                dve.wait_ge(power_done, 1)
                link(dve.tensor_tensor(q_s[:, 1], power_out[:, 0], power_out[:, 1], ALU.mult))
                link(dve.tensor_tensor(q_s[:, 3], q_s[:, 2], q_s[:, 1], ALU.mult))
                quant_rows(q_s[:, 1], 1)
                for t in range(NT):
                    link(dve.tensor_scalar(xn2[:, t], base1[:, t], mv[:, t, 0:1], q_s[:, 5, t:t + 1], ALU.subtract, ALU.mult))
                    dve.tensor_scalar(xq[:, t], xn2[:, t], ROUND, ROUND, ALU.add, ALU.subtract).then_inc(quant_ready, 1)

            def expert_split(i):
                e = i // 2
                tile = TT["h_a"] if i < KD else TT["h_b"]
                wait_emptied(dve, f"e1.{i}")
                wait_emptied(dve, f"cw.{e}")
                dve.tensor_tensor(hf[:, i % 2], hf[:, i % 2], cw_row[:, e], ALU.mult).then_inc(h_scaled, 1)
                dve.wait_ge(h_scaled, 2 * i + 1)
                hi[0] += 1
                dve.wait_ge(act_hi, hi[0])
                dve.tensor_tensor(tile[:, 1, i % KD], hf[:, i % 2], f(tile[:, 0, i % KD]), ALU.subtract).then_inc(h_scaled, 1)

            dve.wait_ge(edges_landed, 16)
            link(dve.tensor_copy(edge_f[:], edge_i[:]))
            link(dve.scalar_tensor_tensor(key[:], edge_f[:, 1], 1.0 / 512, edge_f[:, 0], ALU.mult, ALU.add))
            dve.tensor_copy(key_part[:, 0], edge_f[:, 0])
            dve.tensor_scalar(key_part[:, 1], edge_f[:, 1], 1.0 / 512, None, ALU.mult).then_inc(key_ready, 1)
            for t in range(NT):
                dve.wait_ge(x_tile[t], 16)
                for c in range(2):
                    half_stats(x_sb, t, c)
            layer_norm(x_sb, xn1)
            link(dve.tensor_scalar(four0[:], edge_f[:, 2], 0.0, 4.0, ALU.is_equal, ALU.mult))
            link(dve.scalar_tensor_tensor(cls[:], edge_f[:, 2], -1.0, four0[:], ALU.add, ALU.add))
            dve.wait_ge(consts, 7)
            link(dve.tensor_tensor(cls[:], cls[:], chunk_no[:], ALU.add))
            link(dve.tensor_scalar(power[:], cls[:], 8388608.0, None, ALU.mult))
            dve.wait_ge(small_landed, 32)
            link(dve.tensor_scalar(w8[:, 2], tiny_sb[:, 0:4], -1.0, None, ALU.mult))
            dve.tensor_tensor(w8[:, 0], tiny_sb[:, 0:4], w8[:, 2], ALU.min).then_inc(w8_neg, 1)
            for u in range(AHEAD):
                split_unit(u)
            dve.wait_ge(w8_exp, 1)
            dve.tensor_scalar(w8[:, 1], w8[:, 1], 1.0, None, ALU.add).then_inc(w8_one, 1)

            def edge_group(q):
                pr = f"keys.{q}"
                wait_full(dve, pr)
                for j in range(4):
                    c = 4 * q + j
                    ins = dve.scalar_tensor_tensor(same[:, c % 2], out_of(pr)[:, j * P:(j + 1) * P], key[:, c:c + 1],
                                                   later[:], ALU.is_equal, ALU.mult, accum_out=dead[:, c:c + 1])
                    if j == 3:
                        emptied(ins, pr)
                        wait_emptied(dve, pr)
                    else:
                        link(ins)
                sl = slice(4 * q, 4 * q + 4)
                link(dve.scalar_tensor_tensor(value[:, sl], dead[:, sl], 0.0, power[:, sl].bitcast(F32),
                                              ALU.is_equal, ALU.mult))
                for j in range(4):
                    c = 4 * q + j
                    if c >= 8:
                        dve.wait_ge(onehots_used, c - 7)
                    dve.tensor_scalar(onehot[:, c % 8, 0], node[:], edge_f[:, 0, c:c + 1], None, ALU.is_equal)
                    dve.tensor_scalar(onehot[:, c % 8, 1], node[:], edge_f[:, 1, c:c + 1], None, ALU.is_equal)
                    dve.tensor_scalar(onehot[:, c % 8, 2], node[:], edge_f[:, 1, c:c + 1], value[:, c:c + 1],
                                      ALU.is_equal, ALU.mult).then_inc(onehots, 1)

            for s in EVAC_STEPS:
                kind = s[0]
                if kind == "graph":
                    if s[1] == 0:
                        dve.wait_ge(key_ready, 1)
                        edge_group(0)
                        dve.wait_ge(w8_ln, 1)
                        link(dve.tensor_scalar(w8[:, 0], tiny_sb[:, 0:4], 0.0, None, ALU.max))
                        link(dve.tensor_tensor(w8[:, 2], w8[:, 2], w8[:, 0], ALU.add))
                        dve.tensor_scalar(w8[:, 2], w8[:, 2], 8.0, None, ALU.mult).then_inc(w8_ready, 1)
                    if s[1] + 1 < GROUPS:
                        edge_group(s[1] + 1)
                if s == ("graph", GROUPS - 1):
                    for t in range(NT):
                        pr = f"last_edge.{t}"
                        wait_full(dve, pr)
                        dve.tensor_scalar(no_edge[:, t], out_of(pr)[:, 0:N], 0.0, 8 * NO_EDGE, ALU.is_equal, ALU.mult)
                        emptied(dve.tensor_scalar(edge_cls[:, t], out_of(pr)[:, 0:N].bitcast(I32), 23, 3,
                                                  ALU.logical_shift_right, ALU.bitwise_and), pr)
                if kind == "transpose":
                    if s[1] == "xn3":
                        layer_norm(x_sb, xn3)
                    if s[1] == "xn4":
                        layer_norm(x_sb, xn4)
                    for k in range(KD):
                        chunk_lo(s[1], k, f"{s[1]}.{k}")
                if kind == "transpose_y":
                    for k in range(4 * s[1], 4 * s[1] + 4):
                        chunk_lo("y", k, f"y.{k}")
                if kind == "degree":
                    wait_full(dve, "degree")
                    emptied(dve.tensor_scalar(dis[:, 0], out_of("degree")[:, 0:2 * NT:2], 1.0, None, ALU.max), "degree")
                if kind == "norm":
                    wait_full(dve, "norm")
                    for t in range(NT):
                        ins = dve.scalar_tensor_tensor(count[:, t], count[:, t], dis[:, 1, t:t + 1], out_of("norm")[:, 0:N],
                                                       ALU.mult, ALU.mult)
                        if t == NT - 1:
                            emptied(ins, "norm")
                if kind == "unit":
                    _, u, name, i = s
                    if u + AHEAD < len(UNITS):
                        split_unit(u + AHEAD)
                    if name in ("v1", "q1", "k1"):
                        chunk_lo(name, i, f"{name}.{i}", COLS[name] + i)
                    if name in ("q2", "k2"):
                        hi[0] += 2
                        dve.wait_ge(act_hi, hi[0])
                        for r in range(2):
                            own, other = slice(64 * r, 64 * r + 64), slice(64 - 64 * r, 128 - 64 * r)
                            src, high, low = ((qcat[own, i % 2, r], qcat[other, i % 2, r]) if name == "q2" else
                                              (kcat[own, r, 0], kcat[own, r, 1])), None, None
                            high, low = src
                            ins = dve.scalar_tensor_tensor(low, out_of(f"{name}.{i}")[own, 0:N],
                                                           bias[own, COLS[name] + i:COLS[name] + i + 1], f(high),
                                                           ALU.add, ALU.subtract)
                            if r:
                                emptied(ins, f"{name}.{i}")
                    if name == "mk":
                        wait_full(dve, f"mk.{i}")
                        dve.tensor_reduce(mk_s[:, 0, i:i + 1], out_of(f"mk.{i}")[:, 0:N], X, ALU.max,
                                          negate=True).then_inc(mk_max, 1)
                    if name in NODE_MAJOR and i % NODE_MAJOR[name][1] == NODE_MAJOR[name][1] - 1:
                        c = i // NODE_MAJOR[name][1]
                        sl = slice(c * HALF, (c + 1) * HALF)
                        if name in ("v2", "v"):
                            full_t, rw = (v2f, "biv") if name == "v2" else (kf, "bv")
                            wait_row(dve, rw)
                            if (name, c) == ("v", 0):
                                dve.wait_ge(node_split, 4 * NT)
                                dve.tensor_copy(v_hi[:, :, :, P:P + 2].rearrange("p t j c -> p (t j) c"),
                                                ones[:, 0:2 * NT * KD].rearrange("p (j c) -> p j c", c=2)).then_inc(v_ones, 1)
                            for t in range(NT):
                                pr = f"{name}.{c}.{t}"
                                wait_full(dve, pr)
                                emptied(dve.tensor_tensor(full_t[:, t, sl], out_of(pr)[:], row(rw, c * HALF, (c + 1) * HALF),
                                                          ALU.add), pr)
                            for t in range(NT):
                                wait_emptied(dve, f"{name}.{c}.{t}")
                                if name == "v2":
                                    low, high, src = v2[:, 1, t, sl], v2[:, 0, t, sl], v2f[:, t, sl]
                                else:
                                    low, high = v_lo[:, t, 4 * c:4 * c + 4], v_hi[:, t, 4 * c:4 * c + 4, 0:P]
                                    src = kf[:, t, sl].rearrange("p (j c) -> p j c", c=P)
                                lo_part(low, src, high).then_inc(node_split, 1)
                        if name == "mv":
                            for t in range(NT):
                                lo_part(mvn[:, 1, t], out_of(f"mv.0.{t}")[:], mvn[:, 0, t], f"mv.0.{t}")
                        if name in ("mq", "k", "q"):
                            for t in range(NT):
                                softmax_heads(name, c, t)
                            for t in range(NT):
                                softmax_heads_end(name, c, t, 0.125 if name == "mq" else None)
                            if name == "k":
                                for t in range(NT):
                                    dve.wait_ge(q_ready, sub_no(name, c, t))
                                    lo_part(k2n[:, 1, t, sl], kf[:, t, sl], k2n[:, 0, t, sl]).then_inc(node_split, 1)
                        if name == "wo":
                            for t in range(NT):
                                dve.wait_ge(base1_ready, t + 1)
                                wait_full(dve, f"wo.{c}.{t}")
                                pr = f"wo.{c}.{t}"
                                emptied(dve.tensor_tensor_reduce(out=base1[:, t, sl], in0=out_of(pr)[:], in1=base1[:, t, sl],
                                                                 scale=1.0, scalar=-3.0e38, op0=ALU.add, op1=ALU.max,
                                                                 accum_out=span[:, 0, c, t:t + 1]), pr)
                                wait_emptied(dve, pr)
                                half_stats(base1, t, c)
                                note(dve.tensor_reduce(span[:, 1, c, t:t + 1], base1[:, t, sl], X, ALU.min))
                        if name == "g1":
                            wait_row(dve, "gnn_b1")
                            for t in range(NT):
                                wait_full(dve, f"g1.0.{t}")
                                emptied(dve.tensor_tensor(g[:, t], out_of(f"g1.0.{t}")[:], row("gnn_b1"), ALU.add), f"g1.0.{t}")
                            for t in range(NT):
                                wait_emptied(dve, f"g1.0.{t}")
                                lo_part(g2[:, 1, t], g[:, t], g2[:, 0, t]).then_inc(g_ready, 1)
                        if name == "wp":
                            for t in range(NT):
                                dve.wait_ge(base3_ready, t + 1)
                                wait_full(dve, f"wp.{c}.{t}")
                                emptied(dve.tensor_tensor(x_sb[:, t, sl], x_sb[:, t, sl], out_of(f"wp.{c}.{t}")[:], ALU.add),
                                        f"wp.{c}.{t}")
                                wait_emptied(dve, f"wp.{c}.{t}")
                                half_stats(x_sb, t, c)
                        if name == "e2":
                            for t in range(NT):
                                dve.wait_ge(base4_ready, 2 * NT)
                                wait_full(dve, f"e2.{c}.{t}")
                                dve.tensor_tensor(x_sb[:, t, sl], x_sb[:, t, sl], out_of(f"e2.{c}.{t}")[:],
                                                  ALU.add).then_inc(out_ready, 1)
                    if name == "e1" and i >= LATE:
                        expert_split(i)
                if kind == "mix0_kT":
                    for t in range(NT):
                        lo_part(mkn[:, 1, t], out_of(f"kn.{t}")[:], mkn[:, 0, t], f"kn.{t}")
                if kind == "mix0_context":
                    wait_emptied(dve, "mk.3")
                    link(dve.reciprocal(mk_s[:, 2], mk_s[:, 1]))
                    wait_full(dve, "mix_context")
                    emptied(dve.tensor_tensor(mctx[:], out_of("mix_context")[:].rearrange("p (j c) -> p j c", c=P),
                                              bcast(mk_s[:, 2], [P, KH, P]), ALU.mult), "mix_context")
                    wait_emptied(dve, "mix_context")
                    dve.memset(f(mctx2[:]), 0.0).then_inc(mctx_f, 1)
                    dve.wait_ge(mctx_f, 1)
                    for r in range(2):
                        hs = slice(64 * r, 64 * r + 64)
                        lo_part(mctx2[hs, 1, :, hs], mctx[hs, :, hs], mctx2[hs, 0, :, hs]).then_inc(mctx_ready, 1)
                if kind == "mix0_qT":
                    for j in range(KH):
                        lo_part(mqT[:, 1, j], out_of(f"qT.{j}")[:, 0:N], mqT[:, 0, j], f"qT.{j}")
                if kind == "mix0_out":
                    for j in range(KH):
                        chunk_lo("mixo", j, f"mixo.{j}")
                if kind == "scores":
                    h = s[1]
                    b = h % 2
                    if h == 0:
                        dve.wait_ge(mask_ready, 1)
                        wait_full(dve, "mixo.3")
                    if h >= 1:
                        dve.wait_ge(s_max, h)
                    if h >= 2:
                        wait_full(dve, f"pT.{h - 2}.2")
                    for t in range(NT):
                        pr = f"scores.{h}.{t}"
                        wait_full(dve, pr)
                        emptied(dve.tensor_tensor_reduce(out=prob[:, b, t], in0=out_of(pr)[:, 0:N], in1=mask[:, t], scale=1.0,
                                                         scalar=-3.0e38, op0=ALU.add, op1=ALU.max,
                                                         accum_out=top1[:, 0, t:t + 1]), pr)
                    for t in range(NT):
                        wait_emptied(dve, f"scores.{h}.{t}")
                    dve.tensor_scalar(nmax[:, b], top1[:, 0], -0.125, None, ALU.mult).then_inc(s_max, 1)
                if kind == "probs":
                    h = s[1]
                    b = h % 2
                    for m in range(NT):
                        lo_part(probT[:, 1, m], out_of(f"pT.{h}.{m}")[:, 0:N], probT[:, 0, m], f"pT.{h}.{m}")
                if kind == "normalise":
                    h = s[1]
                    dve.wait_ge(s_exp, NT * (h + 1))
                    link(dve.reciprocal(rsum[:, h % 2], rsum[:, h % 2]))
                    for t in range(NT):
                        dve.tensor_scalar(prob[:, h % 2, t], prob[:, h % 2, t], rsum[:, h % 2, t:t + 1], None,
                                          ALU.mult).then_inc(p_ready, 1)
                if kind == "attend":
                    h = s[1]
                    hs = slice(64 * (h % 2), 64 * (h % 2) + 64)
                    lo_part(TT["o"][hs, 1, h // 2], out_of(f"attend.{h}")[hs, 0:N], TT["o"][hs, 0, h // 2], f"attend.{h}")
                if kind == "ffn_mean":
                    wait_full(dve, "w_sum")
                    emptied(dve.tensor_scalar(w_s[:, 1], out_of("w_sum")[:, 0:2], 1.0 / (D * HID), CLIP, ALU.mult, ALU.max), "w_sum")
                    wait_emptied(dve, "w_sum")
                    link(dve.reciprocal(w_s[:, 0], w_s[:, 1]))
                    for w, r in enumerate((w1r, w2r)):
                        link(dve.tensor_scalar(r[:], r[:], w_s[:, 0, w:w + 1], 1.0, ALU.mult, ALU.min))
                        dve.tensor_scalar(r[:], r[:], -1.0, ROUND, ALU.max, ALU.add).then_inc(w_unit, 1)
                if kind == "ffn":
                    norm_quant()
                    for k in range(KD // 2):
                        pr = f"xqT.{k}"
                        wait_full(dve, pr)
                        emptied(dve.tensor_scalar(xqT[:, 2 * k:2 * k + 2], out_of(pr)[:].bitcast(BF16)[:, 0:2 * N].rearrange(
                            "p (a n) -> p a n", a=2), 127.0, -128.0, ALU.min, ALU.max), pr)
                    wait_row(dve, "ffn_b1")
                    for t in range(NT):
                        wait_full(dve, f"ffn_h.{t}")
                        emptied(dve.scalar_tensor_tensor(hn[:, t], out_of(f"ffn_h.{t}")[:], q_s[:, 6, t:t + 1], row("ffn_b1"),
                                                         ALU.mult, ALU.add), f"ffn_h.{t}")
                    hidden_quant()
                    for k in range(KH // 2):
                        pr = f"hqT.{k}"
                        wait_full(dve, pr)
                        emptied(dve.tensor_scalar(hqT[:, 2 * k:2 * k + 2], out_of(pr)[:].bitcast(BF16)[:, 0:2 * N].rearrange(
                            "p (a n) -> p a n", a=2), 127.0, -128.0, ALU.min, ALU.max), pr)
                    for t in range(NT):
                        dve.wait_ge(base2_ready, t + 1)
                        for c in range(2):
                            pr = f"ffn_o.{t}.{c}"
                            sl = slice(c * HALF, (c + 1) * HALF)
                            wait_full(dve, pr)
                            emptied(dve.scalar_tensor_tensor(x_sb[:, t, sl], out_of(pr)[:], q_s[:, 7, t:t + 1], base2[:, t, sl],
                                                             ALU.mult, ALU.add), pr)
                            wait_emptied(dve, pr)
                            half_stats(x_sb, t, c)
                if kind == "hop_dot":
                    n = s[1]
                    for t in range(NT):
                        wait_emptied(dve, f"hop.{n - 1}.{t}" if n else f"g1.0.{t}")
                    wait_row(dve, f"wg{n}")
                    for t in range(NT):
                        for j in range(2):
                            link(dve.tensor_tensor_reduce(out=gjunk[:], in0=g[:, t], in1=row(f"wg{n}", j * HID, (j + 1) * HID),
                                                          scale=1.0, scalar=0.0, op0=ALU.mult, op1=ALU.add,
                                                          accum_out=aij[:, j, t:t + 1]))
                    dve.tensor_scalar(aij[:, 1], aij[:, 1], tiny_sb[:, 4 + n:5 + n], None, ALU.add).then_inc(aij_ready, 1)
                if kind == "hop_msg":
                    n = s[1]
                    wait_emptied(dve, f"ai.{n}")
                    dve.tensor_tensor(msg[:], msg[:], count[:], ALU.mult).then_inc(msg_f, 1)
                    dve.wait_ge(msg_f, n + 1)
                    lo_part(msg2[:, 1], msg[:], msg2[:, 0]).then_inc(msg_ready, 1)
                if kind == "hop_sum":
                    n = s[1]
                    for t in range(NT):
                        pr = f"hop.{n}.{t}"
                        wait_full(dve, pr)
                        emptied(dve.tensor_tensor(g[:, t], g[:, t], out_of(pr)[:], ALU.add), pr)
                    if n < HOPS - 1:
                        for t in range(NT):
                            wait_emptied(dve, f"hop.{n}.{t}")
                            lo_part(g2[:, 1, t], g[:, t], g2[:, 0, t]).then_inc(g_ready, 1)
                if kind == "context":
                    dve.memset(f(ctx1[:]), 0.0).then_inc(ctx_f, 1)
                    dve.wait_ge(ctx_f, 1)
                    for b in range(3):
                        np_ = min(3, KD - 3 * b)
                        src = out_of(f"context.{b}")[:, 0:130 * np_].rearrange("p (j c) -> p j c", c=130)
                        hi[0] += 4
                        dve.wait_ge(act_hi, hi[0])
                        for r in range(2):
                            hs = slice(64 * r, 64 * r + 64)
                            js = slice(3 * b, 3 * b + np_)
                            note(dve.tensor_tensor(ctx1[hs, 1, js, hs], src[hs, :, hs], f(ctx1[hs, 0, js, hs]), ALU.subtract))
                            ins = dve.tensor_tensor(ctx1[hs, 1, js, P + r], src[hs, :, P], f(ctx1[hs, 0, js, P + r]),
                                                    ALU.subtract)
                            if r == 1:
                                emptied(ins, f"context.{b}")
                            else:
                                note(ins)
                if kind == "queries":
                    for j in range(4 * s[1], 4 * s[1] + 4):
                        chunk_lo("q1T", j, f"q1T.{j}")
                if kind == "y":
                    for t in range(NT):
                        for b, np_ in enumerate((3, 1)):
                            pr = f"yn.{s[1]}.{t}.{b}"
                            wait_full(dve, pr)
                            src = out_of(pr)[:, 0:130 * np_].rearrange("p (j c) -> p j c", c=130)
                            rd = den[:, 0:2 * np_]
                            link(dve.reciprocal(rd.rearrange("p (j c) -> p j c", c=2), src[:, :, P:P + 2]))
                            tmp = ytmp[:, 0:P * np_]
                            for r in range(2):
                                ins = dve.tensor_tensor(tmp.rearrange("p (j c) -> p j c", c=P)[:, :, 64 * r:64 * r + 64],
                                                        src[:, :, 64 * r:64 * r + 64],
                                                        bcast(rd.rearrange("p (j c) -> p j c", c=2)[:, :, r], [P, np_, DH]), ALU.mult)
                                if r:
                                    emptied(ins, pr)
                                else:
                                    note(ins)
                            noted()
                            wait_emptied(dve, pr)
                            at_ = HALF * s[1] + 384 * b
                            qs = qf[:, t, at_:at_ + P * np_]
                            dve.tensor_tensor(qs, qs, tmp, ALU.add).then_inc(y_ready, 1)
                            dve.wait_ge(y_ready, 6 * s[1] + 2 * t + b + 1)
                if kind == "gate_weights":
                    dve.wait_ge(gate_hi, 1)
                    dve.tensor_tensor(gate2[:, 1, :, 0:EXPERTS], gate[:].rearrange("p (k e) -> p k e", e=EXPERTS),
                                      f(gate2[:, 0, :, 0:EXPERTS]), ALU.subtract).then_inc(gate_ready, 1)
                if kind == "gate":
                    wait_full(dve, "logitsT")
                    emptied(dve.tensor_copy(lgT[:], out_of("logitsT")[:, 0:N]), "logitsT")
                if kind == "gate_pick":
                    link(dve.memset(cw[:], 0.0))
                    dve.wait_ge(consts, 8)
                    wait_full(dve, "logits")
                    logits = out_of("logits")[:, 0:N].rearrange("p (t c) -> p t c", c=P)[:, :, 0:EXPERTS]
                    link(dve.tensor_reduce(gsum[:, 0], logits, X, ALU.max, negate=True))
                    emptied(dve.tensor_tensor(lg[:], logits, bcast(gsum[:, 0], [P, NT, EXPERTS]), ALU.add), "logits")
                    for t in range(NT):
                        dve.wait_ge(lg_exp, t + 1)
                        link(dve.tensor_reduce(gsum[:, 1, t:t + 1], lg[:, t], X, ALU.add))
                        link(dve.reciprocal(gsum[:, 1, t:t + 1], gsum[:, 1, t:t + 1]))
                        link(dve.tensor_scalar(lg[:, t], lg[:, t], gsum[:, 1, t:t + 1], None, ALU.mult))
                        link(dve.max(top[:, t], lg[:, t]))
                        link(dve.max_index(top_at[:, t], top[:, t], lg[:, t]))
                        link(dve.tensor_copy(top_f[:, t], top_at[:, t]))
                        link(dve.scalar_tensor_tensor(gsum[:, 2, t:t + 1], top[:, t, 0:1], 1e-8, top[:, t, 1:2], ALU.add, ALU.add))
                        link(dve.reciprocal(gsum[:, 2, t:t + 1], gsum[:, 2, t:t + 1]))
                        link(dve.tensor_scalar(top[:, t, 0:2], top[:, t, 0:2], gsum[:, 2, t:t + 1], None, ALU.mult))
                        for j in range(2):
                            link(dve.tensor_scalar(pick[:, j], expert[:], top_f[:, t, j:j + 1], top[:, t, j:j + 1],
                                                   ALU.is_equal, ALU.mult))
                        dve.tensor_tensor(cw[:, t, 0:EXPERTS], pick[:, 0], pick[:, 1], ALU.add).then_inc(cw_ready, 1)
                        dve.wait_ge(cw_ready, t + 1)
                if kind == "gate_rows":
                    wait_full(dve, "cwT")
                    emptied(dve.tensor_copy(cwT[:], out_of("cwT")[:, 0:N]), "cwT")
                    for i in range(LATE):
                        expert_split(i)

        @block.tensor
        def _(pe):
            HI, LO = 0, 1
            PASSES = ((HI, HI), (HI, LO), (LO, HI))

            def products(dst, terms):
                last = None
                for n, (a, b) in enumerate(terms):
                    for m, (pa, pb) in enumerate(PASSES):
                        last = pe.matmul(dst, a(pa), b(pb), start=(n == 0 and m == 0),
                                         stop=(n == len(terms) - 1 and m == 2))
                return last

            def transposes(name, srcs):
                wait_bank(pe, name)
                for n, src in enumerate(srcs):
                    last = pe.transpose(out_of(name)[:, n * P:(n + 1) * P], src, ident[:])
                full(last, name)

            def spread(name, col):
                wait_bank(pe, name)
                for t in range(NT):
                    last = pe.matmul(out_of(name)[:, t * P:(t + 1) * P], col(t).to_broadcast([P, P]), ident[:],
                                     start=True, stop=True)
                full(last, name)

            pe.wait_ge(consts, 7)
            pe.wait_ge(key_ready, 1)
            nats = {"xn1": (xn1, 0), "xn3": (xn3, NT), "xn4": (xn4, 2 * NT)}

            def keys(q):
                pr = f"keys.{q}"
                wait_bank(pe, pr)
                for j in range(4):
                    c = 4 * q + j
                    for h in range(2):
                        last = pe.matmul(out_of(pr)[:, j * P:(j + 1) * P], key_part[:, h, c:c + 1].to_broadcast([P, P]),
                                         ident_h[:], start=(h == 0), stop=(h == 1))
                full(last, pr)

            for s in STEPS:
                kind = s[0]
                if kind == "graph":
                    if s[1] == 0:
                        for t in range(NT):
                            for b in (t, 3 + t):
                                wait_emptied(pe, f"xn1.{b}")
                        for t in range(NT):
                            pe.matmul(bank[t][:, 0:N], ident_b[:], diag[:, (2 - t) * P:(2 - t) * P + N], start=True, stop=False)
                    if s[1] + 1 < GROUPS:
                        keys(s[1] + 1)
                    for c in range(4 * s[1], 4 * s[1] + 4):
                        pe.wait_ge(onehots, c + 1)
                        for t in range(NT):
                            src = onehot[:, c % 8, 0, t * P:(t + 1) * P]
                            a = pe.matmul(bank[t][:, 0:N], src, onehot[:, c % 8, 2], start=False, stop=(c == EC - 1))
                            b = pe.matmul(bank[3 + t][:, 0:N], src, onehot[:, c % 8, 1], start=(c == 0), stop=(c == EC - 1))
                            if c == EC - 1:
                                full(a, f"last_edge.{t}")
                                full(b, f"count.{t}")
                        if c < EC - 1:
                            b.then_inc(onehots_used, 1)
                if kind == "transpose":
                    src, n = nats[s[1]]
                    for t in range(NT):
                        pe.wait_ge(nat_ready, n + t + 1)
                        for k in range(KD):
                            pr = f"{s[1]}.{k}"
                            if t == 0:
                                wait_bank(pe, pr)
                            last = pe.transpose(out_of(pr)[:, t * P:(t + 1) * P], src[:, t, k * P:(k + 1) * P], ident[:])
                            if t == NT - 1:
                                full(last, pr)
                    if s[1] == "xn1":
                        keys(0)
                if kind == "transpose_y":
                    pe.wait_ge(y_ready, 6 * (s[1] + 1))
                    for k in range(4 * s[1], 4 * s[1] + 4):
                        transposes(f"y.{k}", [qf[:, t, k * P:(k + 1) * P] for t in range(NT)])
                if kind == "degree":
                    wait_emptied(pe, "count.2")
                    wait_bank(pe, "degree")
                    for c in range(NT):
                        for r in range(NT):
                            last = pe.matmul(out_of("degree")[:, 2 * c:2 * c + 2], count[:, r, c * P:(c + 1) * P], ones[:, 0:2],
                                             start=(r == 0), stop=(r == NT - 1))
                    full(last, "degree")
                if kind == "norm":
                    pe.wait_ge(dis_ready, 1)
                    spread("norm", lambda t: dis[:, 1, t:t + 1])
                if kind == "unit":
                    _, u, name, i = s
                    pe.wait_ge(unit_split, u + 1)
                    w = (w_hi, w_lo)
                    slot = u % RING
                    if name in FEATURE_MAJOR:
                        src = FEATURE_MAJOR[name]
                        pr = f"{name}.{i}"
                        wait_bank(pe, pr)
                        for k in range(KD):
                            if i == 0 and name in ("v1", "q2", "k2", "e1"):
                                wait_emptied(pe, f"{src}.{k}")
                            for m, (pa, pb) in enumerate(PASSES):
                                last = pe.matmul(out_of(pr)[:, 0:N], w[pa][:, slot, k * P:(k + 1) * P], TT[src][:, pb, k],
                                                 start=(k == 0 and m == 0), stop=(k == KD - 1 and m == 2))
                        last.then_inc(unit_done, 1)
                    else:
                        src, per = NODE_MAJOR[name]
                        c, kk = i // per, i % per
                        if name == "e2":
                            if c == 0:
                                pe.wait_ge(h_scaled, 2 * (2 * kk + 2))
                            if i == 0:
                                pe.wait_ge(eb2_landed, 16)
                                wait_emptied(pe, "cwT")
                        elif name == "wo":
                            if i == 0:
                                wait_emptied(pe, "attend.15")
                                wait_emptied(pe, "attend.14")
                            if i == 4:
                                wait_emptied(pe, "mixo.2")
                                wait_emptied(pe, "mixo.3")
                        elif c == 0 and name in ("v2", "g1") or name == "wp":
                            wait_emptied(pe, f"{src}.{2 * kk}")
                            wait_emptied(pe, f"{src}.{2 * kk + 1}")
                        for t in range(NT):
                            pr = f"{name}.{c}.{t}"
                            ts = slice(t * P, (t + 1) * P)
                            if kk == 0:
                                wait_bank(pe, pr)
                                if name == "e2":
                                    pe.matmul(out_of(pr)[:], cwT[0:EXPERTS, ts], eb2[:, c * HALF:(c + 1) * HALF],
                                              start=True, stop=False)
                            for j in range(2):
                                k = 2 * kk + j
                                if name == "e2":
                                    tile = TT["h_a"] if k < KD else TT["h_b"]
                                    k = k % KD
                                elif name == "wo":
                                    tile, k = (TT["o"], k) if k < KD else (TT["mixo"], k - KD)
                                else:
                                    tile = TT[src]
                                for m, (pa, pb) in enumerate(PASSES):
                                    last = pe.matmul(out_of(pr)[:], tile[:, pa, k, ts], w[pb][:, slot, j * HALF:(j + 1) * HALF],
                                                     start=(kk == 0 and j == 0 and m == 0 and name != "e2"),
                                                     stop=(kk == per - 1 and j == 1 and m == 2))
                            if t == NT - 1:
                                last.then_inc(unit_done, 1)
                            elif kk == per - 1:
                                full(last, pr)
                if kind == "mix0_kT":
                    wait_emptied(pe, "mk.3")
                    for t in range(NT):
                        transposes(f"kn.{t}", [ekT[:, j, t * P:(t + 1) * P] for j in range(KH)])
                if kind == "mix0_context":
                    pr = "mix_context"
                    wait_emptied(pe, "kn.2")
                    wait_emptied(pe, "kn.1")
                    wait_emptied(pe, "mv.0.2")
                    wait_bank(pe, pr)
                    for j in range(KH):
                        js = slice(j * P, (j + 1) * P)
                        last = products(out_of(pr)[:, js], [(lambda p, t=t: mkn[:, p, t, js], lambda p, t=t: mvn[:, p, t, js])
                                                            for t in range(NT)])
                    full(last, pr)
                if kind == "mix0_qT":
                    pe.wait_ge(q_ready, sub_no("mq", 0, NT - 1))
                    for j in range(KH):
                        transposes(f"qT.{j}", [mqn[:, t, j * P:(j + 1) * P] for t in range(NT)])
                if kind == "mix0_out":
                    pe.wait_ge(mctx_ready, 2)
                    for j in range(KH):
                        wait_emptied(pe, f"qT.{j}")
                    for j in range(KH):
                        pr = f"mixo.{j}"
                        wait_bank(pe, pr)
                        full(products(out_of(pr)[:, 0:N], [(lambda p: mctx2[:, p, j], lambda p: mqT[:, p, j])]), pr)
                if kind == "scores":
                    h = s[1]
                    j, r = h // 2, h % 2
                    wait_emptied(pe, f"q2.{j}")
                    pe.wait_ge(k_twice, 32 * (j + 1))
                    for t in range(NT):
                        pr = f"scores.{h}.{t}"
                        wait_bank(pe, pr)
                        for p in (HI, LO):
                            last = pe.matmul(out_of(pr)[:, 0:N], qcat[:, j % 2, r, t * P:(t + 1) * P], kcat[:, r, p],
                                             start=(p == HI), stop=(p == LO))
                        full(last, pr)
                if kind == "probs":
                    h = s[1]
                    pe.wait_ge(p_ready, NT * (h + 1))
                    for m in range(NT):
                        transposes(f"pT.{h}.{m}", [prob[:, h % 2, t, m * P:(m + 1) * P] for t in range(NT)])
                if kind == "attend":
                    h = s[1]
                    pr = f"attend.{h}"
                    if h == 0:
                        pe.wait_ge(node_split, 2 * NT)
                    wait_emptied(pe, f"pT.{h}.2")
                    wait_emptied(pe, f"pT.{h}.1")
                    wait_emptied(pe, f"pT.{h}.0")
                    wait_bank(pe, pr)
                    js = slice(h // 2 * P, (h // 2 + 1) * P)
                    full(products(out_of(pr)[:, 0:N], [(lambda p, m=m: v2[:, p, m, js], lambda p, m=m: probT[:, p, m])
                                                       for m in range(NT)]), pr)
                if kind == "ffn_mean":
                    pe.wait_ge(w_abs, 2)
                    wait_bank(pe, "w_sum")
                    full(pe.matmul(out_of("w_sum")[:, 0:2], ones[:], w_s[:, 0], start=True, stop=True), "w_sum")
                if kind == "ffn":
                    def transposes_b(name, srcs):
                        wait_bank(pe, name)
                        view = out_of(name)[:].bitcast(BF16)
                        for n, src in enumerate(srcs):
                            last = pe.transpose(view[:, n * P:(n + 1) * P], src, ident_b[:])
                        full(last, name)

                    pe.wait_ge(quant_ready, NT)
                    for k in range(KD // 2):
                        transposes_b(f"xqT.{k}", [xq[:, t, (2 * k + a) * P:(2 * k + a + 1) * P] for a in range(2) for t in range(NT)])
                    pe.wait_ge(w_quant, 2)
                    wait_emptied(pe, f"xqT.{KD // 2 - 1}")
                    wait_emptied(pe, f"xqT.{KD // 2 - 2}")
                    for t in range(NT):
                        pr = f"ffn_h.{t}"
                        wait_bank(pe, pr)
                        for k in range(KD):
                            last = pe.matmul(out_of(pr)[:], xqT[:, k, t * P:(t + 1) * P], w1q[:, k], start=(k == 0), stop=(k == KD - 1))
                        full(last, pr)
                    pe.wait_ge(quant_ready, 2 * NT)
                    for k in range(KH // 2):
                        transposes_b(f"hqT.{k}", [hq[:, t, (2 * k + a) * P:(2 * k + a + 1) * P] for a in range(2) for t in range(NT)])
                    wait_emptied(pe, "hqT.0")
                    wait_emptied(pe, "hqT.1")
                    for t in range(NT):
                        for c in range(2):
                            pr = f"ffn_o.{t}.{c}"
                            wait_bank(pe, pr)
                            for k in range(KH):
                                last = pe.matmul(out_of(pr)[:], hqT[:, k, t * P:(t + 1) * P], w2q[:, k, c * HALF:(c + 1) * HALF],
                                                 start=(k == 0), stop=(k == KH - 1))
                            full(last, pr)
                if kind == "hop_row":
                    n = s[1]
                    pe.wait_ge(aij_ready, n + 1)
                    spread(f"ai.{n}", lambda t: aij[:, 0, t:t + 1])
                if kind == "hop_sum":
                    n = s[1]
                    pe.wait_ge(msg_ready, n + 1)
                    pe.wait_ge(g_ready, NT * (n + 1))
                    for c in range(NT):
                        pr = f"hop.{n}.{c}"
                        wait_bank(pe, pr)
                        cs = slice(c * P, (c + 1) * P)
                        full(products(out_of(pr)[:], [(lambda p, r=r: msg2[:, p, r, cs], lambda p, r=r: g2[:, p, r])
                                                      for r in range(NT)]), pr)
                if kind == "context":
                    pe.wait_ge(node_split, 6 * NT)
                    for b in range(3):
                        pr = f"context.{b}"
                        wait_bank(pe, pr)
                        for j in range(3 * b, min(3 * b + 3, KD)):
                            js = slice(j * P, (j + 1) * P)
                            o = out_of(pr)[:, 130 * (j % 3):130 * (j % 3) + 130]
                            for t in range(NT):
                                pe.matmul(o, k2n[:, HI, t, js], v_hi[:, t, j], start=(t == 0), stop=False)
                                pe.matmul(o[:, 0:P], k2n[:, HI, t, js], v_lo[:, t, j], start=False, stop=False)
                                last = pe.matmul(o, k2n[:, LO, t, js], v_hi[:, t, j], start=False, stop=(t == NT - 1))
                        full(last, pr)
                if kind == "queries":
                    pe.wait_ge(q_ready, sub_no("q", s[1], NT - 1))
                    for j in range(4 * s[1], 4 * s[1] + 4):
                        transposes(f"q1T.{j}", [qf[:, t, j * P:(j + 1) * P] for t in range(NT)])
                if kind == "y":
                    c = s[1]
                    for b in range(3):
                        wait_emptied(pe, f"context.{b}")
                    wait_emptied(pe, f"q1T.{4 * c + 3}")
                    for t in range(NT):
                        ts = slice(t * P, (t + 1) * P)
                        for b in range(2):
                            pr = f"yn.{c}.{t}.{b}"
                            wait_bank(pe, pr)
                            for n, j in enumerate(range(4 * c + 3 * b, 4 * c + 3 + b)):
                                last = products(out_of(pr)[:, 130 * n:130 * n + 130],
                                                [(lambda p: TT["q1T"][:, p, j, ts], lambda p: ctx1[:, p, j])])
                            full(last, pr)
                if kind == "gate":
                    pe.wait_ge(gate_ready, 1)
                    wait_bank(pe, "logitsT")
                    full(products(out_of("logitsT")[:, 0:N], [(lambda p, k=k: gate2[:, p, k],
                                                               lambda p, k=k: TT["xn4"][:, p, k]) for k in range(KD)]), "logitsT")
                if kind == "gate_pick":
                    wait_emptied(pe, "logitsT")
                    transposes("logits", [lgT[:, t * P:(t + 1) * P] for t in range(NT)])
                if kind == "gate_rows":
                    pe.wait_ge(cw_ready, NT)
                    transposes("cwT", [cw[:, t] for t in range(NT)])
                    for e in range(EXPERTS):
                        spread(f"cw.{e}", lambda t: cw[:, t, e:e + 1])


def kernel(**inputs):
    import numpy as np
    import concourse.bacc as bacc
    from concourse.bass_utils import run_bass_kernel_spmd

    a = {k: np.asarray(v) for k, v in inputs.items()}

    def feature_major(w):
        k, m = w.shape
        return w.reshape(k // P, P, m // P, P).transpose(2, 1, 0, 3).reshape(-1, P, D)

    def node_major(w):
        k, m = w.shape
        return w.reshape(k // (2 * P), 2, P, m // HALF, HALF).transpose(3, 0, 2, 1, 4).reshape(m // HALF, k // (2 * P), P, D)

    packs = {"v1": feature_major(a["L0_gnn_wv"].T), "v2": node_major(a["L0_gnn_wiv"].T).reshape(-1, P, D),
             "mk": feature_major(a["L0_mix_Wk"]), "mv": node_major(a["L0_mix_Wv"])[0], "mq": node_major(a["L0_mix_Wq"])[0],
             "q1": feature_major(a["L0_gnn_wq"].T), "k1": feature_major(a["L0_gnn_wk"].T),
             "q2": feature_major(a["L0_gnn_wiq"].T), "k2": feature_major(a["L0_gnn_wik"].T),
             "wo": np.concatenate([node_major(a["L0_gnn_wo"].T), node_major(a["L0_mix_Wo"])], axis=1).reshape(-1, P, D),
             "g1": node_major(a["L1_gnn_W1"])[0]}
    for n in "kvq":
        packs[n] = node_major(a[f"L1_mix_W{n}"]).reshape(-1, P, D)
    packs["wp"] = node_major(a["L1_mix_Wp"]).reshape(-1, P, D)
    packs["e1"] = np.concatenate([feature_major(a["L1_ffn_W1"][e]) for e in range(EXPERTS)])
    packs["e2"] = node_major(a["L1_ffn_W2"].reshape(EXPERTS * EHID, D)).reshape(-1, P, D)
    rows = {"biv": a["L0_gnn_biv"], "bo": a["L0_gnn_bo"], "mix_bo": a["L0_mix_bo"], "ffn_b1": a["L0_ffn_b1"],
            "ffn_b2": a["L0_ffn_b2"], "gnn_b1": a["L1_gnn_b1"], "bk": a["L1_mix_bk"], "bv": a["L1_mix_bv"],
            "bq": a["L1_mix_bq"], "bp": a["L1_mix_bp"]} | {f"wg{n}": a["L1_gnn_Wg"][n, :, 0] for n in range(HOPS)}
    arrays = {
        "weights": np.stack([packs[n][i] for n, i in UNITS]),
        "x_in": np.ascontiguousarray(a["x"]),
        "edges": np.ascontiguousarray(np.stack([a["src"], a["dst"], a["edge_type_5"]]).reshape(3, EC, P).transpose(2, 0, 1)),
        "rows": np.concatenate([rows[n] for n in ROW_ORDER]),
        "cols": np.ascontiguousarray(np.concatenate(
            [a[f"L0_gnn_{n}"].reshape(KD, P) for n in ("bv", "bq", "bk", "biq", "bik")]
            + [a["L1_ffn_b1"].reshape(EXPERTS * 2, P)]).T),
        "tiny": np.concatenate([a["L0_gnn_edge_type_weights"], a["L1_gnn_bg"][:, 0]]),
        "w1_in": np.ascontiguousarray(a["L0_ffn_w1"].T.reshape(KD, P, HID).transpose(1, 0, 2).reshape(P, -1)),
        "w2_in": np.ascontiguousarray(a["L0_ffn_w2"].T.reshape(KH, P, D).transpose(1, 0, 2).reshape(P, -1)),
        "gate_in": np.ascontiguousarray(a["L1_ffn_gate_W"].reshape(KD, P, EXPERTS).transpose(1, 0, 2).reshape(P, -1)),
        "eb2_in": np.ascontiguousarray(a["L1_ffn_b2"]),
    }
    nc = bacc.Bacc("TRN2", target_bir_lowering=False, num_devices=1)
    args = [nc.dram_tensor(n, v.shape, mybir.dt.from_np(v.dtype), kind="ExternalInput").ap() for n, v in arrays.items()]
    args.append(nc.dram_tensor("out", (N, D), F32, kind="ExternalOutput").ap())
    gps_kernel(nc, *args)
    return run_bass_kernel_spmd(nc, [arrays], core_ids=[0]).results[0]["out"]
```

```python
import concourse.bass as bass
from concourse import mybir
from contextlib import ExitStack

F32 = mybir.dt.float32
F32R = mybir.dt.float32r
BF16 = mybir.dt.bfloat16
F16 = mybir.dt.float16
I32 = mybir.dt.int32
U32 = mybir.dt.uint32
ALU = mybir.AluOpType
ACT = mybir.ActivationFunctionType
X = mybir.AxisListType.X

P = 128
N = 384
NT = N // P
D = 1024
KD = D // P
H0, DH = 16, 64
HID = 512
KH = HID // P
E = 6144
EC = E // P
NTYPE = 4
HOPS = 4
EXPERTS, EHID = 8, 256
HALF = 512
EPS = 1e-5
CLIP = 1e-5
ROUND = 12582912.0
NO_EDGE = -1.0e30

GROUPS = EC // 4
LATE = 5
RAW, RING, AHEAD = 3, 4, 3


ROWS = {}
_at = 0
for _n, _l in (("biv", D), ("bo", D), ("mix_bo", D), ("ffn_b1", HID), ("ffn_b2", D), ("gnn_b1", HID),
               ("wg0", D), ("bk", D), ("wg1", D), ("bv", D), ("wg2", D), ("bq", D), ("wg3", D), ("bp", D)):
    ROWS[_n] = (_at, _l)
    _at += _l
ROW_ORDER = list(ROWS)
ROW_SLOTS = 3
COLS = {"v1": 0, "q1": 8, "k1": 16, "q2": 24, "k2": 32, "e1": 40}


def schedule():
    steps, units = [], []

    def unit(name, i):
        steps.append(("unit", len(units), name, i))
        units.append((name, i))

    def run(name, a, b):
        for i in range(a, b):
            unit(name, i)

    steps.append(("transpose", "xn1"))
    for i in range(GROUPS):
        run("v1", i, i + 1) if i < KD else run("mk", i - KD, i - KD + 1)
        steps.append(("graph", i))
    run("v2", 0, 1)
    steps.append(("degree",))
    run("v2", 1, 2)
    steps.append(("norm",))
    run("v2", 2, 8)
    run("mv", 0, 4)
    run("mq", 0, 4)
    run("q1", 0, 2)
    steps.append(("mix0_kT", (0, 1)))
    run("q1", 2, 3)
    steps.append(("mix0_kT", (2,)))
    run("q1", 3, 4)
    steps.append(("mix0_context",))
    run("q1", 4, 6)
    steps.append(("mix0_qT", (0, 1)))
    run("q1", 6, 7)
    steps.append(("mix0_qT", (2, 3)))
    run("q1", 7, 8)
    steps.append(("mix0_out", (0, 1)))
    run("k1", 0, 1)
    steps.append(("mix0_out", (2, 3)))
    run("k1", 1, 8)
    unit("k2", 0)
    unit("q2", 0)
    unit("q2", 1)
    steps.append(("scores", 0))
    steps.append(("scores", 1))
    steps.append(("exps", 0))
    steps.append(("normalise", 0))
    unit("k2", 1)
    for h in range(H0):
        steps.append(("probs", h))
        if h + 1 < H0:
            steps.append(("exps", h + 1))
            steps.append(("normalise", h + 1))
        odd = h % 2 == 1 and h // 2 + 2 < KD
        if odd:
            steps.append(("scores", h + 2))
            unit("k2", h // 2 + 2)
        elif h // 2 + 2 < KD:
            unit("q2", h // 2 + 2)
        if h >= 12:
            run("wo", h - 12 + (h > 12), h - 10)
        if h + 2 < H0 and not odd:
            steps.append(("scores", h + 2))
        if h == H0 - 1:
            steps.append(("ffn_abs", 1))
        steps.append(("attend", h))
    steps.append(("ffn_mean", 1))
    run("wo", 5, 8)
    steps.append(("ffn_abs", 0))
    run("wo", 8, 9)
    steps.append(("ffn_mean", 0))
    run("wo", 9, 12)
    steps.append(("ffn",))
    steps.append(("transpose", "xn3"))
    run("g1", 0, 4)
    hops = {a: (k, n) for n, at in enumerate(((1, 2, 3, 6), (7, 9, 10, 13), (14, 15, 16, 18)))
            for k, a in zip(("hop_dot", "hop_row", "hop_msg", "hop_sum"), at)}
    n = 0
    for name in ("k", "v", "q"):
        for i in range(8):
            unit(name, i)
            n += 1
            if n in hops:
                steps.append(hops[n])
            if name == "q":
                steps.extend({1: [("context",)], 2: [("hop_dot", 3)], 5: [("hop_row", 3)],
                              6: [("queries", 0), ("queries", 1), ("hop_msg", 3)], 7: [("y", 0)]}.get(i, []))
    steps.extend([("transpose_y", 0), ("transpose_y", 1), ("softmax", "q", 1)])
    run("wp", 0, 2)
    steps.extend([("queries", 2), ("queries", 3)])
    run("wp", 4, 5)
    steps.extend([("y", 1), ("hop_sum", 3), ("transpose_y", 2)])
    run("wp", 5, 6)
    steps.append(("transpose_y", 3))
    run("wp", 2, 4)
    steps.append(("gate_weights",))
    run("wp", 6, 8)
    steps.append(("transpose", "xn4"))
    run("e1", 0, 1)
    steps.append(("gate",))
    run("e1", 1, 2)
    steps.append(("gate_pick",))
    run("e1", 2, LATE)
    steps.append(("gate_rows",))
    run("e1", LATE, 16)
    run("e2", 0, 16)
    return steps, units


def evacuation_order(steps):
    steps = list(steps)
    for n in range(len(steps) - 1):
        if steps[n][0] == "scores" and steps[n][1] > 1 and steps[n + 1][0] == "unit":
            steps[n], steps[n + 1] = steps[n + 1], steps[n]
    return steps


STEPS, UNITS = schedule()
EVAC_STEPS = evacuation_order(STEPS)
UNIT_OF = {u: n for n, u in enumerate(UNITS)}
POOL_UNITS = {UNIT_OF[(name, i)] for name in ("k", "v", "q") for i in range(1, 8, 2)}
FEATURE_MAJOR = {"v1": "xn1", "mk": "xn1", "q1": "xn1", "k1": "xn1", "q2": "q1", "k2": "k1", "e1": "xn4"}
NODE_MAJOR = {"v2": ("v1", 4), "mv": ("xn1", 4), "mq": ("xn1", 4), "wo": ("o", 6), "g1": ("xn3", 4), "k": ("xn3", 4),
              "v": ("xn3", 4), "q": ("xn3", 4), "wp": ("y", 4), "e2": ("h", 8)}


STAGGERED = (("wo", 1), ("wp", 1), ("e2", 1))


def plan_banks():
    uses, fulls, where = [0] * 8, [0] * 8, {}

    def product(name, bank, unit=None):
        uses[bank] += 1
        if unit is None:
            fulls[bank] += 1
            where[name] = (bank, uses[bank], None, fulls[bank])
        else:
            where[name] = (bank, uses[bank], "unit", unit + 1)

    single = group = 0
    for s in STEPS:
        kind = s[0]
        if kind == "unit":
            _, u, name, i = s
            if name in FEATURE_MAJOR:
                if name in ("v1", "mk"):
                    product(f"{name}.{i}", 6, u)
                elif name in ("q2", "k2"):
                    product(f"{name}.{i}", {("k2", 0): 1, ("k2", 1): 1, ("q2", 0): 4}.get((name, i), 0), u)
                else:
                    product(f"{name}.{i}", single % 6, u)
                    single += 1
            else:
                per = NODE_MAJOR[name][1]
                if i % per == 0:
                    for t in range(NT):
                        b = (0, 6, 1)[t] if (name, i) == ("wo", 0) else 3 * (group % 2) + t
                        product(f"{name}.{i // per}.{t}", b, UNIT_OF[(name, i + per - 1)] if t == NT - 1 else None)
                    group += 1
        elif kind == "graph":
            if s[1] + 1 < GROUPS:
                product(f"keys.{s[1] + 1}", 7)
            if s[1] == GROUPS - 1:
                for t in range(NT):
                    product(f"last_edge.{t}", t)
                    product(f"count.{t}", 3 + t)
        elif kind == "transpose":
            if s[1] == "xn1":
                product("keys.0", 7)
            for k in range(KD):
                product(f"{s[1]}.{k}", (6, 0, 1, 2, 3, 4, 5, 7)[k] if s[1] == "xn1" else k)
        elif kind == "transpose_y":
            for k in range(2 * s[1], 2 * s[1] + 2):
                product(f"y.{k}", 6 + k % 2)
        elif kind == "degree":
            product("degree", 7)
        elif kind == "norm":
            product("norm", 7)
        elif kind == "mix0_kT":
            for t in s[1]:
                product(f"kn.{t}", 6 + t % 2)
        elif kind == "mix0_context":
            product("mix_context", 7)
        elif kind == "mix0_qT":
            for j in s[1]:
                product(f"qT.{j}", 6 + j % 2)
        elif kind == "mix0_out":
            for j in s[1]:
                product(f"mixo.{j}", 6 + j % 2)
        elif kind == "scores":
            for t in range(NT):
                product(f"scores.{s[1]}.{t}", (5, 7, 4)[t] if s[1] == 1 else (2, 3, 6 if s[1] < H0 - 2 else 2)[t])
        elif kind == "probs":
            for m in range(NT):
                product(f"pT.{s[1]}.{m}", (4, 5, 1 if s[1] < H0 - 3 else 4 if s[1] < H0 - 2 else 2)[m])
        elif kind == "attend":
            product(f"attend.{s[1]}", 7)
        elif kind == "ffn_mean":
            product(f"w_sum.{s[1]}", 7)
        elif kind == "ffn":
            for k in range(KD // 2):
                product(f"xqT.{k}", 4 + k)
            for t in range(NT):
                product(f"ffn_h.{t}", t)
            for k in range(KH // 2):
                product(f"hqT.{k}", 6 + k % 2)
            for t in range(NT):
                for c in range(2):
                    product(f"ffn_o.{t}.{c}", 3 * c + t)
        elif kind == "hop_row":
            product(f"ai.{s[1]}", 6)
        elif kind == "hop_sum":
            for t in range(NT):
                product(f"hop.{s[1]}.{t}", 3 * (group % 2) + t if s[1] < HOPS - 1 else 6 + t % 2)
        elif kind == "context":
            for b in range(3):
                product(f"context.{b}", 6 + b % 2)
        elif kind == "queries":
            for j in range(2 * s[1], 2 * s[1] + 2):
                product(f"q1T.{j}", 6 + j % 2)
        elif kind == "y":
            for b in range(NT + 1):
                product(f"yn.{s[1]}.{b}", 6 + b % 2)
        elif kind == "gate":
            product("logitsT", 6)
        elif kind == "gate_pick":
            product("logits", 7)
        elif kind == "gate_rows":
            product("cwT", 7)
            for e in range(EXPERTS):
                product(f"cw.{e}", 6 + e % 2)
    return where


WHERE = plan_banks()


def sub_no(name, c, t):
    return {"mq": 0, "k": NT, "q": 3 * NT}[name] + NT * c + t + 1


def gps_kernel(nc, weights, x_in, edges, rows, cols, tiny, w1_in, w2_in, gate_in, eb2_in, out):
    with ExitStack() as ctx:
        def sem(name):
            return ctx.enter_context(nc.semaphore(name))

        base = (nc.sbuf_base + 63) // 64 * 64
        fence = ctx.enter_context(nc.sbuf_tensor("fence", [P, (nc.sbuf_usable_end - nc.sbuf_base) // 4 - 16], F32))
        del fence

        def at(name, shape, dt, kib):
            return nc.alloc_sbuf_tensor_at(name, shape, dt, offset=base + int(kib * 1024))

        XA, R0, R1, R2, R3, AT, MASK, CNT, RAWS, HIS, LOS, ROWS_AT, SMALL = (
            0, 12, 36, 60, 84.25, 108.25, 138.25, 142.75, 147.25, 159.25, 175.25, 191.25, 203.25)
        x_sb = at("x_sb", [P, NT, D], F32, XA)
        raw = at("raw", [P, RAW, D], F32, RAWS)
        w_hi = at("w_hi", [P, RING, D], F32R, HIS)
        w_lo = at("w_lo", [P, RING, D], F32R, LOS)
        row_sb = at("row_sb", [P, ROW_SLOTS, D], F32, ROWS_AT)
        mask = at("mask", [P, NT, N], F32, MASK)
        count = at("count", [P, NT, N], F32, CNT)

        def pair(name, chunks, width, kib):
            return at(name, [P, 2, chunks, width], F32R, kib)

        TT = {"xn1": pair("xn1T", KD, N, R0), "v1": pair("v1T", KD, N, R1), "q1": pair("q1T", KD, N, R1),
              "k1": pair("k1T", KD, N, R3), "o": pair("oT", KD, N, R0), "mixo": pair("mixoT", KH, N, XA),
              "xn3": pair("xn3T", KD, N, R0), "q1T": pair("qT_l1", KD, N, R3), "y": at("yT", [P, KD, 2, N], F32R, R1).rearrange("p k a n -> p a k n"),
              "xn4": pair("xn4T", KD, N, R0), "h_a": pair("hT_a", KD, N, R1), "h_b": pair("hT_b", KD, N, R3)}
        xn1 = at("xn1_nat", [P, NT, D], F32, R2 + 10)
        onehot = at("onehot", [P, 8, 3, N], BF16, R3 + 2)
        edge_i = at("edge_i", [P, 3, EC], I32, R2)
        edge_f = at("edge_f", [P, 3, EC], F32, R2 + 1)
        key = at("key", [P, EC], F32, R2 + 2)
        four0 = at("four0", [P, EC], F32, R2 + 2.25)
        cls = at("cls", [P, EC], F32, R2 + 2.5)
        power = at("power", [P, EC], I32, R2 + 2.75)
        dead = at("dead", [P, EC], F32, R2 + 3)
        value = at("value", [P, EC], F32, R2 + 3.25)
        chunk_no = at("chunk_no", [P, EC], I32, R2 + 3.5)
        same = at("same", [P, 2, P], F32, R2 + 4)
        later = at("later", [P, P], F32, R2 + 5)
        node_i = at("node_i", [P, N], I32, R2 + 5.5)
        node = at("node", [P, N], F16, R2 + 7)
        diag = at("diag", [P, 5 * P], BF16, R2 + 8)
        key_part = at("key_part", [P, 2, EC], F16, R2 + 9.25)
        edge_cls = at("edge_cls", [P, NT, N], I32, R3 + 2)
        no_edge = at("no_edge", [P, NT, N], F32, R3 + 6.5)
        picked = at("picked", [P, 2, NT, N], F32, R3 + 11)
        v2f = at("v2f", [P, NT, D], F32, AT + 18)
        v2 = at("v2", [P, 2, NT, D], F32R, R2)
        qcat = at("qcat", [P, 2, 2, N], F32R, AT)
        kcat = at("kcat", [P, 2, 2, N], F32R, AT + 6)
        prob = at("prob", [P, 2, NT, N], F32, AT + 12)
        probT = at("probT", [P, 2, NT, N], F32R, AT + 21)
        ekT = at("ekT", [P, KH, N], F32, AT)
        mqn = at("mqn", [P, NT, HID], F32, AT + 6)
        mqT = at("mqT", [P, 2, KH, N], F32R, AT + 12)
        mctx = at("mctx", [P, KH, P], F32, AT + 24)
        mctx2 = at("mctx2", [P, 2, KH, P], F32R, AT + 26)
        mkn = at("mkn", [P, 2, NT, HID], F32R, R3)
        mvn = at("mvn", [P, 2, NT, HID], F32R, R3 + 12)
        base1 = at("base1", [P, NT, D], F32, R1)
        base2 = at("base2", [P, NT, D], F32, R1 + 12)
        w1r = at("w1r", [P, KD * HID], F32, R2)
        w2r = at("w2r", [P, KH * D], F32, R3)
        w1q = at("w1q", [P, KD, HID], BF16, R2 + 16)
        w2q = at("w2q", [P, KH, D], BF16, R3 + 16)
        xn2 = at("xn2_nat", [P, NT, D], F32, R0)
        xq = at("xq", [P, NT, D], BF16, R0 + 12)
        xqT = at("xqT", [P, KD, N], BF16, R0 + 18)
        hn = at("hn", [P, NT, HID], F32, AT)
        hq = at("hq", [P, NT, HID], BF16, AT + 6)
        hqT = at("hqT", [P, KH, N], BF16, AT + 9)
        junk = at("junk", [P, D], F32, AT + 12)
        xn3 = at("xn3_nat", [P, NT, D], F32, R2)
        g = at("g", [P, NT, HID], F32, AT)
        g2 = at("g2", [P, 2, NT, HID], F32R, AT + 6)
        msg = at("msg", [P, NT, N], F32, MASK)
        msg2 = at("msg2", [P, 2, NT, N], F32R, AT + 18)
        gjunk = at("gjunk", [P, 2, HID], F32, MASK)
        kf = at("kf", [P, NT, D], F32, R1)
        k2n = at("k2n", [P, 2, NT, D], F32R, R3)
        v_hi = at("v_hi", [P, NT, KD, P + 2], F32R, R2)
        v_lo = at("v_lo", [P, NT, KD, P], F32R, R2 + 12.1875)
        qf = at("qf", [P, NT, D], F32, R2)
        ctx1 = at("ctx1", [P, 2, KD, P + 2], F32R, R1 + 12)
        ytmp = at("ytmp", [P, 3 * P], F32, R1 + 21)
        xn4 = at("xn4_nat", [P, NT, D], F32, R2)
        cw_row = at("cw_row", [P, EXPERTS, N], F32, AT)
        hf = at("hf", [P, 2, N], F32, AT + 12)
        gate = at("gate", [P, KD * EXPERTS], F32, AT + 15)
        gate2 = at("gate2", [P, 2, KD, P], F32R, AT + 16)
        eb2 = at("eb2", [P, D], F32, AT + 24)
        eb2_parts = at("eb2_parts", [P, D], F32R, CNT)
        lgT = at("lgT", [P, N], F32, AT + 28)
        cw = at("cw", [P, NT, P], F32, MASK)
        cwT = at("cwT", [P, N], F32R, MASK + 1.5)
        lg = at("lg", [P, NT, EXPERTS], F32, MASK + 3)
        top = at("top", [P, NT, 8], F32, MASK + 3.125)
        top_at = at("top_at", [P, NT, 8], U32, MASK + 3.25)
        top_f = at("top_f", [P, NT, 8], F32, MASK + 3.375)
        gsum = at("gsum", [P, 4, NT], F32, MASK + 3.5)
        pick = at("pick", [P, 2, EXPERTS], F32, MASK + 3.5625)
        expert = at("expert", [P, EXPERTS], F32, MASK + 3.625)
        expert_i = at("expert_i", [P, EXPERTS], I32, MASK + 3.6875)
        ident = at("ident", [P, P], F32, SMALL)
        ident_b = at("ident_b", [P, P], BF16, SMALL + 0.5)
        ones = at("ones", [P, P], F32, SMALL + 0.75)
        ident_h = at("ident_h", [P, P], F16, SMALL + 3.125)
        bias = at("bias", [P, 56], F32, SMALL + 1.3125)
        tiny_sb = at("tiny_sb", [P, 8], F32, SMALL + 1.5625)
        w8 = at("w8", [P, 3, 4], F32, SMALL + 1.625)
        stats = at("stats", [P, NT, 2, 6], F32, SMALL + 1.6875)
        mv = at("mv", [P, NT, 2], F32, SMALL + 1.875)
        rstd = at("rstd", [P, NT], F32, SMALL + 1.9375)
        minus_half = at("minus_half", [P, 2 * NT], F32, SMALL + 2)
        minus_round = at("minus_round", [P, 1], F32, SMALL + 3.375)
        dis = at("dis", [P, 2, NT], F32, SMALL + 2.0625)
        top1 = at("top1", [P, 2, NT], F32, SMALL + 2.125)
        rsum = at("rsum", [P, 2, NT], F32, SMALL + 2.1875)
        nmax = at("nmax", [P, 2, NT], F32, SMALL + 2.25)
        mk_s = at("mk_s", [P, 3, KH], F32, SMALL + 2.3125)
        h8 = at("h8", [P, 2, 8], F32, SMALL + 2.375)
        q_s = at("q_s", [P, 8, NT], F32, SMALL + 2.5)
        w_s = at("w_s", [P, 2, 2], F32, SMALL + 2.625)
        aij = at("aij", [P, 2, NT], F32, SMALL + 2.6875)
        den = at("den", [P, 6], F32, SMALL + 2.75)
        k8 = at("k8", [P, 2, 8], F32, SMALL + 2.8125)
        span = at("span", [P, 2, 2, NT], F32, SMALL + 2.9375)
        power_in = at("power_in", [P, 2, NT], F32, SMALL + 3)
        power_out = at("power_out", [P, 2, NT], F32, SMALL + 3.0625)

        bank = [ctx.enter_context(nc.psum_tensor(f"bank{b}", [P, 512], F32)) for b in range(8)]

        bank_full = [sem(f"bank_full{b}") for b in range(8)]
        bank_emptied = [sem(f"bank_emptied{b}") for b in range(8)]
        raw_landed = [sem(f"raw_landed{r}") for r in range(RAW)]
        hi_split = sem("hi_split")
        unit_split = sem("unit_split")
        pool_split = sem("pool_split")
        unit_done = sem("unit_done")
        act_hi = sem("act_hi")
        row_landed = [sem(f"row_landed{r}") for r in range(ROW_SLOTS)]
        x_landed = sem("x_landed")
        x_tile = [sem(f"x_tile{t}") for t in range(NT)]
        small_landed = sem("small_landed")
        edges_landed = sem("edges_landed")
        consts = sem("consts")
        onehots = sem("onehots")
        onehots_used = sem("onehots_used")
        key_ready = sem("key_ready")
        w8_exp, w8_ln, w8_neg, w8_one, w8_ready = (sem(n) for n in ("w8_exp", "w8_ln", "w8_neg", "w8_one", "w8_ready"))
        mask_ready = sem("mask_ready")
        ln_stats, ln_rstd, nat_ready = sem("ln_stats"), sem("ln_rstd"), sem("nat_ready")
        dis_ready = sem("dis_ready")
        v_ones = sem("v_ones")
        node_split = sem("node_split")
        mk_max = sem("mk_max")
        gate_zero = sem("gate_zero")
        power_ready, power_done = sem("power_ready"), sem("power_done")
        q_max, q_exp, q_ready = sem("q_max"), sem("q_exp"), sem("q_ready")
        mctx_f, mctx_ready = sem("mctx_f"), sem("mctx_ready")
        s_max, s_exp, p_ready = sem("s_max"), sem("s_exp"), sem("p_ready")
        k_twice = sem("k_twice")
        base1_ready, base2_ready = sem("base1_ready"), sem("base2_ready")
        ffn_landed = [sem(f"ffn_landed{w}") for w in range(2)]
        w_abs, w1_unit, w1_quant, w2_quant = (sem(n) for n in ("w_abs", "w1_unit", "w1_quant", "w2_quant"))
        sq_ready, rms_ready, quant_ready = sem("sq_ready"), sem("rms_ready"), sem("quant_ready")
        h_gelu = sem("h_gelu")
        aij_ready, msg_f, msg_ready = sem("aij_ready"), sem("msg_f"), sem("msg_ready")
        g_ready = sem("g_ready")
        base3_ready, base4_ready = sem("base3_ready"), sem("base4_ready")
        ctx_f, y_ready = sem("ctx_f"), sem("y_ready")
        eb2_zero, eb2_hi, eb2_ready = sem("eb2_zero"), sem("eb2_hi"), sem("eb2_ready")
        gate_landed, eb2_landed, gate_hi, gate_ready = sem("gate_landed"), sem("eb2_landed"), sem("gate_hi"), sem("gate_ready")
        lg_exp, cw_ready = sem("lg_exp"), sem("cw_ready")
        h_scaled = sem("h_scaled")
        out_ready, out_stored = sem("out_ready"), sem("out_stored")
        v_chain, p_chain = sem("v_chain"), sem("p_chain")
        block = ctx.enter_context(nc.Block())

        def f(ap):
            return ap.bitcast(F32)

        def out_of(name):
            return bank[WHERE[name][0]]

        def wait_bank(pe, name):
            b, n, _, _ = WHERE[name]
            if n > 1:
                pe.wait_ge(bank_emptied[b], n - 1)

        def wait_full(eng, name):
            b, _, by, n = WHERE[name]
            eng.wait_ge(unit_done if by else bank_full[b], n)

        def full(ins, name):
            ins.then_inc(bank_full[WHERE[name][0]], 1)

        def wait_emptied(eng, name):
            b, n, _, _ = WHERE[name]
            eng.wait_ge(bank_emptied[b], n)

        def emptied(ins, name):
            ins.then_inc(bank_emptied[WHERE[name][0]], 1)

        def wait_unit(eng, name, i):
            eng.wait_ge(unit_done, UNIT_OF[(name, i)] + 1)

        def wait_split(eng, u):
            by_pool = u in POOL_UNITS
            eng.wait_ge(pool_split if by_pool else unit_split, sum((n in POOL_UNITS) == by_pool for n in range(u + 1)))

        def row_slot(name):
            i = ROW_ORDER.index(name)
            return i % ROW_SLOTS, 16 * (i // ROW_SLOTS + 1)

        def wait_row(eng, name):
            slot, n = row_slot(name)
            eng.wait_ge(row_landed[slot], n)

        def row(name, a=0, b=None):
            return row_sb[:, row_slot(name)[0], a:ROWS[name][1] if b is None else b]

        def bcast(ap, shape):
            return ap.unsqueeze(len(shape) - 1).to_broadcast(shape)

        def heads(ap):
            return ap.rearrange("p (h d) -> p h d", d=DH)

        @block.sync
        def _(sp):
            sp.dma_start(edge_i[:], edges).then_inc(edges_landed, 16)
            for t in range(NT):
                sp.dma_start(x_sb[:, t], x_in[t * P:(t + 1) * P, :]).then_inc(x_tile[t], 16)
            sp.dma_start(bias[:], cols).then_inc(small_landed, 16)
            sp.dma_start(tiny_sb[:], tiny.partition_broadcast(P)).then_inc(small_landed, 16)

            def load_row(name, free=None):
                if free:
                    free()
                o, n = ROWS[name]
                sp.dma_start(row(name), rows[o:o + n].partition_broadcast(P)).then_inc(row_landed[row_slot(name)[0]], 16)

            for s in STEPS:
                if s[0] == "unit":
                    _, u, name, i = s
                    if u >= RAW:
                        wait_split(sp, u - RAW)
                    sp.dma_start(raw[:, u % RAW, :], weights[u]).then_inc(raw_landed[u % RAW], 16)
                    if (name, i) == ("v1", 4):
                        for n in ROW_ORDER[:ROW_SLOTS]:
                            load_row(n)
                    if (name, i) == ("wo", 1):
                        wait_unit(sp, "q2", 7)
                        sp.dma_start(base1[:], x_in.rearrange("(t p) d -> p t d", p=P)).then_inc(x_landed, 16)
                        load_row("ffn_b1", lambda: wait_emptied(sp, "v2.1.2"))
                    if (name, i) == ("wo", 3):
                        wait_unit(sp, "k2", 7)
                        sp.dma_start(w2r[:], w2_in).then_inc(ffn_landed[1], 16)
                    if (name, i) == ("wo", 7):
                        wait_full(sp, "attend.15")
                        sp.dma_start(w1r[:], w1_in).then_inc(ffn_landed[0], 16)
                    if (name, i) == ("wo", 11):
                        load_row("ffn_b2", lambda: sp.wait_ge(base1_ready, NT))
                        load_row("gnn_b1")
                    if (name, i) == ("g1", 3):
                        load_row("wg0", lambda: wait_emptied(sp, "ffn_h.2"))
                        load_row("bk", lambda: sp.wait_ge(base2_ready, NT))
                    if (name, i) == ("k", 2):
                        load_row("wg1", lambda: wait_emptied(sp, "g1.0.2"))
                    if (name, i) == ("k", 6):
                        load_row("bv", lambda: sp.wait_ge(aij_ready, 1))
                    if (name, i) == ("v", 3):
                        load_row("wg2", lambda: wait_emptied(sp, "k.1.2"))
                    if (name, i) == ("v", 5):
                        load_row("bq", lambda: sp.wait_ge(aij_ready, 2))
                    if (name, i) == ("q", 2):
                        load_row("wg3", lambda: wait_emptied(sp, "v.1.2"))
                    if (name, i) == ("q", 4):
                        load_row("bp", lambda: sp.wait_ge(aij_ready, 3))
                    if (name, i) == ("wp", 3):
                        sp.wait_ge(base3_ready, NT)
                        sp.dma_start(gate[:], gate_in).then_inc(gate_landed, 16)
                        sp.wait_ge(eb2_zero, 1)
                        for j in range(3):
                            sp.dma_start(eb2[32 * j:32 * j + EXPERTS], eb2_in).then_inc(eb2_landed, 16)
            n = 0
            for c in range(2):
                for t in range(NT):
                    n += 1
                    sp.wait_ge(out_ready, n)
                    sp.dma_start(out[t * P:(t + 1) * P, c * HALF:(c + 1) * HALF],
                                 x_sb[:, t, c * HALF:(c + 1) * HALF]).then_inc(out_stored, 16)
            sp.wait_ge(out_stored, 16 * n)

        @block.gpsimd
        def _(pool):
            pn, pool_done = [0], set()

            def link(ins):
                pn[0] += 1
                ins.then_inc(p_chain, 1)
                pool.wait_ge(p_chain, pn[0])

            link(pool.memset(minus_round[:], -ROUND))
            pool.memset(minus_half[:], -0.5).then_inc(consts, 1)
            link(pool.memset(ident[:], 0.0))
            link(pool.affine_select(out=ident[:], in_=ident[:], compare_op=ALU.not_equal, fill=1.0, base=0,
                                    pattern=[[-1, P]], channel_multiplier=1))
            pool.tensor_copy(ident_b[:], ident[:]).then_inc(consts, 1)
            link(pool.memset(ones[:], 1.0))
            pool.tensor_copy(ident_h[:], ident[:]).then_inc(consts, 1)
            pool.affine_select(out=later[:], in_=ones[:], compare_op=ALU.is_gt, fill=0.0, base=0,
                               pattern=[[1, P]], channel_multiplier=-1).then_inc(consts, 1)
            link(pool.iota(node_i[:], pattern=[[1, N]], base=0, channel_multiplier=0))
            pool.tensor_copy(node[:], node_i[:]).then_inc(consts, 1)
            pool.iota(chunk_no[:], pattern=[[4, EC]], base=32, channel_multiplier=0).then_inc(consts, 1)
            link(pool.memset(diag[:], 0.0))
            pool.tensor_scalar(diag[:, 2 * P:3 * P], ident[:], 2.0 ** -96, None, ALU.mult).then_inc(consts, 1)

            def power(dst, src, scale, n):
                link(pool.tensor_scalar(dst, src, scale, EPS, ALU.mult, ALU.add))
                return pool.tensor_tensor(dst, dst, minus_half[:, 0:n], ALU.pow)

            def norm_power():
                for t in range(NT):
                    pool.wait_ge(ln_stats, NT * lns[0] + t + 1)
                    power(rstd[:, t:t + 1], mv[:, t, 1:2], 1.0, 1).then_inc(ln_rstd, 1)
                lns[0] += 1

            lns = [0]
            norm_power()
            for s in STEPS:
                if s[:2] in (("transpose", "xn3"), ("transpose", "xn4")):
                    norm_power()
                soft = s[0] == "unit" and (s[2], s[3]) in (("mq", 3), ("k", 3), ("k", 7), ("q", 3))
                for u in sorted(POOL_UNITS & {s[1] + AHEAD, s[1] + AHEAD + soft}) if s[0] == "unit" else ():
                    if u in pool_done:
                        continue
                    pool_done.add(u)
                    pool.wait_ge(hi_split, u + 1)
                    pool.tensor_tensor(w_lo[:, u % RING], raw[:, u % RAW], f(w_hi[:, u % RING]),
                                       ALU.subtract).then_inc(pool_split, 1)
                if s[0] == "hop_msg":
                    wait_emptied(pool, f"ai.{s[1]}")
                    pool.tensor_tensor(msg[:], msg[:], count[:], ALU.mult).then_inc(msg_f, 1)
                if s[0] == "unit" and s[2] == "k2":
                    wait_emptied(pool, f"k2.{s[3]}")
                    for r in range(2):
                        own, other = slice(64 * r, 64 * r + 64), slice(64 - 64 * r, 128 - 64 * r)
                        pool.dma_start(f(kcat[other, r]), f(kcat[own, r])).then_inc(k_twice, 16)
                if s[0] == "degree":
                    wait_emptied(pool, "degree")
                    pool.tensor_tensor(dis[:, 1], dis[:, 0], minus_half[:, 0:NT], ALU.pow).then_inc(dis_ready, 1)
                    for t in range(NT):
                        wait_emptied(pool, f"last_edge.{t}")
                    wait_full(pool, "count.2")
                    pool.wait_ge(w8_ready, 1)
                    link(pool.tensor_scalar(picked[:, 0], edge_cls[:], 0.0, w8[:, 2, 0:1], ALU.is_equal, ALU.mult))
                    link(pool.tensor_tensor(mask[:], no_edge[:], picked[:, 0], ALU.add))
                    for k in range(1, NTYPE):
                        link(pool.tensor_scalar(picked[:, k % 2], edge_cls[:], float(k), w8[:, 2, k:k + 1],
                                                ALU.is_equal, ALU.mult))
                        ins = pool.tensor_tensor(mask[:], mask[:], picked[:, k % 2], ALU.add)
                        if k < NTYPE - 1:
                            link(ins)
                    ins.then_inc(mask_ready, 1)
                if s[0] == "attend" and s[1] == H0 - 1:
                    pool.wait_ge(x_landed, 16)
                    wait_row(pool, "bo")
                    wait_row(pool, "mix_bo")
                    link(pool.tensor_tensor(row("bo"), row("bo"), row("mix_bo"), ALU.add))
                    for t in range(NT):
                        pool.tensor_tensor(base1[:, t], base1[:, t], row("bo"), ALU.add).then_inc(base1_ready, 1)
                if s[0] == "ffn":
                    pool.wait_ge(power_ready, 1)
                    pool.tensor_tensor(power_out[:].rearrange("p a t -> p (a t)"), power_in[:].rearrange("p a t -> p (a t)"),
                                       minus_half[:], ALU.pow).then_inc(power_done, 1)
                    wait_row(pool, "ffn_b2")
                    for t in range(NT):
                        wait_emptied(pool, f"wo.0.{t}")
                        wait_emptied(pool, f"wo.1.{t}")
                        pool.tensor_tensor(base2[:, t], base1[:, t], row("ffn_b2"), ALU.add).then_inc(base2_ready, 1)
                    pool.wait_ge(sq_ready, NT)
                    power(q_s[:, 1], q_s[:, 0], 1.0 / HID, NT).then_inc(rms_ready, 1)
                if s[0] == "unit" and s[2:] == ("g1", 3):
                    for t in range(NT):
                        wait_emptied(pool, f"g1.0.{t}")
                        pool.tensor_tensor(x_sb[:, t, 0:HID], x_sb[:, t, 0:HID], g[:, t], ALU.add).then_inc(base4_ready, 1)
                if s == ("transpose_y", 0):
                    wait_row(pool, "bp")
                    pool.wait_ge(base4_ready, NT)
                    for t in range(NT):
                        pool.tensor_tensor(x_sb[:, t], x_sb[:, t], row("bp"), ALU.add).then_inc(p_chain, 1)
                        pn[0] += 1
                if s[0] == "hop_sum" and s[1] == HOPS - 1:
                    pool.wait_ge(p_chain, pn[0])
                    for t in range(NT):
                        wait_emptied(pool, f"hop.{HOPS - 1}.{t}")
                        pool.tensor_tensor(x_sb[:, t, HID:D], x_sb[:, t, HID:D], g[:, t], ALU.add).then_inc(base3_ready, 1)
                    wait_full(pool, f"hop.{HOPS - 1}.2")
                    pool.memset(eb2[:], 0.0).then_inc(eb2_zero, 1)
                if s[0] == "gate_weights":
                    pool.wait_ge(base3_ready, NT)
                    pool.memset(f(gate2[:]), 0.0).then_inc(gate_zero, 1)
                if s[0] == "gate":
                    pool.wait_ge(nat_ready, 3 * NT)
                    link(pool.iota(expert_i[:], pattern=[[1, EXPERTS]], base=0, channel_multiplier=0))
                    pool.tensor_copy(expert[:], expert_i[:]).then_inc(consts, 1)
                    for t in range(NT):
                        pool.tensor_tensor(x_sb[:, t], x_sb[:, t], xn4[:, t], ALU.add).then_inc(base4_ready, 1)

        @block.scalar
        def _(act):
            hi, split = [0], [0]

            def hi_part(dst, src, name=None, bias=0.0):
                if name:
                    wait_full(act, name)
                act.activation(dst, src, ACT.Identity, bias=bias).then_inc(act_hi, 1)
                hi[0] += 1

            def split_unit(u):
                act.wait_ge(raw_landed[u % RAW], 16 * (u // RAW + 1))
                if u >= RING:
                    act.wait_ge(unit_done, u - RING + 1)
                act.activation(w_hi[:, u % RING], raw[:, u % RAW], ACT.Copy).then_inc(hi_split, 1)

            def split_up_to(u):
                for n in range(split[0], min(u + 1, len(UNITS))):
                    split_unit(n)
                    split[0] = n + 1

            def chunk_hi(tname, k, name, col=None):
                b = 0.0 if col is None else bias[:, col:col + 1]
                hi_part(TT[tname][:, 0, k], out_of(name)[:, 0:N], name, b)

            def expert(i):
                wait_full(act, f"e1.{i}")
                if i >= 2:
                    act.wait_ge(h_scaled, 2 * (i - 2) + 2)
                emptied(act.activation(hf[:, i % 2], out_of(f"e1.{i}")[:, 0:N], ACT.Relu,
                                       bias=bias[:, COLS["e1"] + i:COLS["e1"] + i + 1]), f"e1.{i}")
                act.wait_ge(h_scaled, 2 * i + 1)
                hi_part(TT["h_a" if i < KD else "h_b"][:, 0, i % KD], hf[:, i % 2])

            def softmax(name, c):
                for t in range(NT):
                    dst = {"mq": mqn, "k": kf, "q": qf}[name]
                    dst = dst[:, t] if name == "mq" else dst[:, t, c * HALF:(c + 1) * HALF]
                    src = out_of(f"{name}.{c}.{t}")[:] if name == "mq" else dst
                    n = sub_no(name, c, t)
                    act.wait_ge(q_max, n)
                    if n > 2:
                        act.wait_ge(q_ready, n - 2)
                    for j in range(HALF // DH):
                        hs = slice(j * DH, (j + 1) * DH)
                        act.activation(dst[:, hs], src[:, hs], ACT.Exp, bias=h8[:, n % 2, j:j + 1],
                                       accum_out=k8[:, n % 2, j:j + 1]).then_inc(q_exp, 1)
                    if t == 0:
                        split_up_to(split[0])

            split_up_to(AHEAD - 1)
            for s in EVAC_STEPS:
                kind = s[0]
                if s == ("graph", 0):
                    act.wait_ge(w8_neg, 1)
                    act.activation(w8[:, 1], w8[:, 0], ACT.Exp).then_inc(w8_exp, 1)
                    act.wait_ge(w8_one, 1)
                    act.activation(w8[:, 2], w8[:, 1], ACT.Ln).then_inc(w8_ln, 1)
                if s == ("graph", GROUPS - 1):
                    for t in range(NT):
                        wait_full(act, f"count.{t}")
                        emptied(act.activation(count[:, t], out_of(f"count.{t}")[:, 0:N], ACT.Copy), f"count.{t}")
                if kind == "transpose":
                    if s[1] == "xn4":
                        wait_unit(act, "q", 7)
                    for k in range(KD):
                        chunk_hi(s[1], k, f"{s[1]}.{k}")
                if kind == "transpose_y":
                    if s[1] == 2:
                        wait_full(act, "yn.1.3")
                    for k in range(2 * s[1], 2 * s[1] + 2):
                        chunk_hi("y", k, f"y.{k}")
                if kind == "unit":
                    _, u, name, i = s
                    split_up_to(u + AHEAD)
                    if name in ("v1", "q1", "k1"):
                        if (name, i) == ("q1", 0):
                            wait_unit(act, "v2", 7)
                        if (name, i) == ("k1", 0):
                            wait_full(act, "mixo.3")
                        chunk_hi(name, i, f"{name}.{i}", COLS[name] + i)
                    if name in ("q2", "k2"):
                        behind = 2 * i - 3 if name == "q2" else 2 * i - 1
                        if behind > 0:
                            wait_full(act, f"scores.{behind}.2")
                        for r in range(2):
                            hs = slice(64 * r, 64 * r + 64)
                            dst = qcat[hs, i % 2, r] if name == "q2" else kcat[hs, r, 0]
                            hi_part(dst, out_of(f"{name}.{i}")[hs, 0:N], f"{name}.{i}",
                                    bias[hs, COLS[name] + i:COLS[name] + i + 1])
                    if name == "mk":
                        act.wait_ge(mk_max, i + 1)
                        emptied(act.activation(ekT[:, i], out_of(f"mk.{i}")[:, 0:N], ACT.Exp, bias=mk_s[:, 0, i:i + 1],
                                               accum_out=mk_s[:, 1, i:i + 1]), f"mk.{i}")
                    if name in NODE_MAJOR and i % NODE_MAJOR[name][1] == NODE_MAJOR[name][1] - 1:
                        c = i // NODE_MAJOR[name][1]
                        for t in range(NT):
                            pr = f"{name}.{c}.{t}"
                            sl = slice(c * HALF, (c + 1) * HALF)
                            if name == "v2":
                                wait_emptied(act, pr)
                                hi_part(v2[:, 0, t, sl], v2f[:, t, sl])
                            if name == "v":
                                wait_emptied(act, pr)
                                hi_part(v_hi[:, t, 4 * c:4 * c + 4, 0:P], kf[:, t, sl].rearrange("p (j c) -> p j c", c=P))
                            if name == "mv":
                                act.wait_ge(mask_ready, 1)
                                hi_part(mvn[:, 0, t], out_of(pr)[:], pr)
                        if name in ("mq", "k") or (name, c) == ("q", 0):
                            softmax(name, c)
                        if name == "k":
                            for t in range(NT):
                                act.wait_ge(q_ready, sub_no(name, c, t))
                                hi_part(k2n[:, 0, t, c * HALF:(c + 1) * HALF], kf[:, t, c * HALF:(c + 1) * HALF])
                        if name == "g1":
                            for t in range(NT):
                                wait_emptied(act, f"g1.0.{t}")
                                hi_part(g2[:, 0, t], g[:, t])
                    if name == "e1" and i >= LATE:
                        expert(i)
                if kind == "softmax":
                    softmax(s[1], s[2])
                if kind == "gate_rows":
                    hi_part(cwT[:], out_of("cwT")[:, 0:N], "cwT")
                    act.wait_ge(eb2_landed, 48)
                    act.activation(eb2_parts[:], eb2[:], ACT.Copy).then_inc(eb2_hi, 1)
                    for e in range(EXPERTS):
                        wait_full(act, f"cw.{e}")
                        emptied(act.activation(cw_row[:, e], out_of(f"cw.{e}")[:, 0:N], ACT.Copy), f"cw.{e}")
                    for i in range(LATE):
                        expert(i)
                if kind == "mix0_kT":
                    for t in s[1]:
                        hi_part(mkn[:, 0, t], out_of(f"kn.{t}")[:], f"kn.{t}")
                if kind == "mix0_context":
                    act.wait_ge(mctx_f, 1)
                    for r in range(2):
                        hs = slice(64 * r, 64 * r + 64)
                        hi_part(mctx2[hs, 0, :, hs], mctx[hs, :, hs])
                if kind == "mix0_qT":
                    for j in s[1]:
                        hi_part(mqT[:, 0, j], out_of(f"qT.{j}")[:, 0:N], f"qT.{j}")
                if kind == "mix0_out":
                    for j in s[1]:
                        hi_part(TT["mixo"][:, 0, j], out_of(f"mixo.{j}")[:, 0:N], f"mixo.{j}")
                if kind == "exps":
                    h = s[1]
                    act.wait_ge(s_max, h + 1)
                    for t in range(NT):
                        act.activation(prob[:, h % 2, t], prob[:, h % 2, t], ACT.Exp, scale=0.125,
                                       bias=nmax[:, h % 2, t:t + 1], accum_out=rsum[:, h % 2, t:t + 1]).then_inc(s_exp, 1)
                if kind == "probs":
                    h = s[1]
                    if h:
                        wait_full(act, f"attend.{h - 1}")
                    for m in range(NT):
                        hi_part(probT[:, 0, m], out_of(f"pT.{h}.{m}")[:, 0:N], f"pT.{h}.{m}")
                if kind == "attend":
                    h = s[1]
                    hs = slice(64 * (h % 2), 64 * (h % 2) + 64)
                    if h == 0:
                        wait_unit(act, "k1", 7)
                    hi_part(TT["o"][hs, 0, h // 2], out_of(f"attend.{h}")[hs, 0:N], f"attend.{h}")
                if kind == "ffn_abs":
                    w = s[1]
                    act.wait_ge(ffn_landed[w], 16)
                    src, dst = ((w1r, w1q), (w2r, w2q))[w]
                    act.activation(dst[:].rearrange("p a b -> p (a b)"), src[:], ACT.Abs,
                                   accum_out=w_s[:, 0, w:w + 1]).then_inc(w_abs, 1)
                if kind == "ffn":
                    act.wait_ge(w1_unit, 1)
                    act.wait_ge(consts, 7)
                    act.activation(w1q[:].rearrange("p a b -> p (a b)"), w1r[:], ACT.Identity,
                                   bias=minus_round[:]).then_inc(w1_quant, 1)
                    for t in range(NT):
                        wait_emptied(act, f"ffn_h.{t}")
                        act.activation(hn[:, t], hn[:, t], ACT.Gelu).then_inc(h_gelu, 1)
                        act.wait_ge(h_gelu, t + 1)
                        if t:
                            act.wait_ge(sq_ready, t)
                        act.activation(junk[:, 0:HID], hn[:, t], ACT.Square, accum_out=q_s[:, 0, t:t + 1]).then_inc(sq_ready, 1)
                if kind == "hop_row":
                    n = s[1]
                    wait_full(act, f"ai.{n}")
                    act.wait_ge(aij_ready, n + 1)
                    for t in range(NT):
                        ins = act.activation(msg[:, t], out_of(f"ai.{n}")[:, 0:N], ACT.Tanh, bias=aij[:, 1, t:t + 1])
                    emptied(ins, f"ai.{n}")
                if kind == "hop_msg":
                    n = s[1]
                    act.wait_ge(msg_f, n + 1)
                    if n:
                        wait_full(act, f"hop.{n - 1}.2")
                    hi_part(msg2[:, 0], msg[:])
                if kind == "hop_sum" and s[1] < HOPS - 1:
                    wait_full(act, f"hop.{s[1]}.{NT - 1}")
                    for t in range(NT):
                        wait_emptied(act, f"hop.{s[1]}.{t}")
                        hi_part(g2[:, 0, t], g[:, t])
                if kind == "context":
                    for b in range(3):
                        wait_full(act, f"context.{b}")
                        act.wait_ge(ctx_f, 1)
                        np_ = min(3, KD - 3 * b)
                        src = out_of(f"context.{b}")[:, 0:130 * np_].rearrange("p (j c) -> p j c", c=130)
                        for r in range(2):
                            hs = slice(64 * r, 64 * r + 64)
                            hi_part(ctx1[hs, 0, 3 * b:3 * b + np_, hs], src[hs, :, hs])
                            hi_part(ctx1[hs, 0, 3 * b:3 * b + np_, P + r], src[hs, :, P])
                if kind == "queries":
                    if s[1] == 0:
                        wait_full(act, "context.2")
                    for j in range(2 * s[1], 2 * s[1] + 2):
                        hi_part(TT["q1T"][:, 0, j], out_of(f"q1T.{j}")[:, 0:N], f"q1T.{j}")
                if kind == "gate_weights":
                    act.wait_ge(gate_landed, 16)
                    act.wait_ge(gate_zero, 1)
                    act.activation(gate2[:, 0, :, 0:EXPERTS], gate[:].rearrange("p (k e) -> p k e", e=EXPERTS),
                                   ACT.Copy).then_inc(gate_hi, 1)
                if kind == "gate_pick":
                    wait_emptied(act, "logits")
                    for t in range(NT):
                        act.activation(lg[:, t], lg[:, t], ACT.Exp).then_inc(lg_exp, 1)

        @block.vector
        def _(dve):
            vn, hi, split, late = [0], [0], [0], []

            def link(ins):
                vn[0] += 1
                ins.then_inc(v_chain, 1)
                dve.wait_ge(v_chain, vn[0])

            def note(ins):
                vn[0] += 1
                ins.then_inc(v_chain, 1)

            def noted():
                dve.wait_ge(v_chain, vn[0])

            def lo_part(dst, src, hi_ap, name=None, col=None):
                hi[0] += 1
                dve.wait_ge(act_hi, hi[0])
                if col is None:
                    ins = dve.tensor_tensor(dst, src, f(hi_ap), ALU.subtract)
                else:
                    ins = dve.scalar_tensor_tensor(dst, src, bias[:, col:col + 1], f(hi_ap), ALU.add, ALU.subtract)
                if name:
                    emptied(ins, name)
                return ins

            def split_unit(u):
                if u in POOL_UNITS:
                    return
                dve.wait_ge(hi_split, u + 1)
                dve.tensor_tensor(w_lo[:, u % RING], raw[:, u % RAW], f(w_hi[:, u % RING]),
                                  ALU.subtract).then_inc(unit_split, 1)

            def split_up_to(u):
                for n in range(split[0], min(u + 1, len(UNITS))):
                    split_unit(n)
                    split[0] = n + 1

            def chunk_lo(tname, k, name, col=None):
                t = TT[tname]
                lo_part(t[:, 1, k], out_of(name)[:, 0:N], t[:, 0, k], name, col)

            lns = [0]

            def half_stats(src, t, c):
                note(dve.bn_stats(stats[:, t, c], src[:, t, c * HALF:(c + 1) * HALF]))

            def tile_stats(t):
                noted()
                dve.bn_aggr(mv[:, t], stats[:, t]).then_inc(ln_stats, 1)
                lns[0] += 1

            def layer_norm(src, dst, t):
                n = (lns[0] - 1) // NT * NT + t + 1
                dve.wait_ge(ln_rstd, n)
                dve.wait_ge(ln_stats, n)
                dve.tensor_scalar(dst[:, t], src[:, t], mv[:, t, 0:1], rstd[:, t:t + 1], ALU.subtract,
                                  ALU.mult).then_inc(nat_ready, 1)

            def softmax_heads(name, c, t):
                pr = f"{name}.{c}.{t}"
                n = sub_no(name, c, t)
                wait_full(dve, pr)
                if n > 2:
                    dve.wait_ge(q_exp, (HALF // DH) * (n - 2))
                if name == "mq":
                    src = out_of(pr)[:]
                else:
                    src = {"k": kf, "q": qf}[name][:, t, c * HALF:(c + 1) * HALF]
                    wait_row(dve, "b" + name)
                    emptied(dve.tensor_tensor(src, out_of(pr)[:], row("b" + name, c * HALF, (c + 1) * HALF), ALU.add), pr)
                    wait_emptied(dve, pr)
                dve.tensor_reduce(h8[:, n % 2], heads(src), X, ALU.max, negate=True).then_inc(q_max, 1)

            def softmax_heads_end(name, c, t, scale=None):
                tile = {"mq": mqn, "k": kf, "q": qf}[name]
                tile = tile[:, t] if name == "mq" else tile[:, t, c * HALF:(c + 1) * HALF]
                n = sub_no(name, c, t)
                nh = HALF // DH
                dve.wait_ge(q_exp, nh * n)
                ins = dve.reciprocal(k8[:, n % 2], k8[:, n % 2])
                if scale is None:
                    link(ins)
                else:
                    emptied(ins, f"{name}.{c}.{t}")
                    wait_emptied(dve, f"{name}.{c}.{t}")
                    link(dve.tensor_scalar(k8[:, n % 2], k8[:, n % 2], scale, None, ALU.mult))
                dve.tensor_tensor(heads(tile), heads(tile), bcast(k8[:, n % 2], [P, nh, DH]), ALU.mult).then_inc(q_ready, 1)

            def softmax(name, c):
                for t in range(NT + 1):
                    if t < NT:
                        softmax_heads(name, c, t)
                    if t:
                        softmax_heads_end(name, c, t - 1, 0.125 if name == "mq" else None)
                    if t == 1:
                        split_up_to(split[0])

            def hidden_quant():
                for t in range(NT):
                    dve.wait_ge(h_gelu, t + 1)
                    note(dve.tensor_reduce(q_s[:, 2, t:t + 1], hn[:, t], X, ALU.max, apply_absolute_value=True))
                noted()
                dve.wait_ge(rms_ready, 1)
                link(dve.tensor_tensor(q_s[:, 3], q_s[:, 2], q_s[:, 1], ALU.mult))
                quant_rows(q_s[:, 1])
                dve.wait_ge(sq_ready, NT)
                for t in range(NT + 1):
                    if t < NT:
                        note(dve.tensor_scalar(hn[:, t], hn[:, t], q_s[:, 5, t:t + 1], ROUND, ALU.mult, ALU.add))
                    if t:
                        dve.wait_ge(v_chain, vn[0] - (t < NT))
                        dve.tensor_scalar(hq[:, t - 1], hn[:, t - 1], ROUND, None, ALU.subtract).then_inc(quant_ready, 1)
                quant_back(2)
                noted()

            def quant_rows(factor):
                link(dve.tensor_scalar(q_s[:, 3], q_s[:, 3], CLIP, None, ALU.max))
                link(dve.reciprocal(q_s[:, 4], q_s[:, 3]))
                link(dve.scalar_tensor_tensor(q_s[:, 5], q_s[:, 4], 127.0, factor, ALU.mult, ALU.mult))

            def quant_back(n):
                note(dve.tensor_scalar(q_s[:, 5 + n], q_s[:, 3], 1.0 / 127.0, w_s[:, 1, n - 1:n], ALU.mult, ALU.mult))

            def norm_quant():
                noted()
                for t in range(NT):
                    note(dve.bn_aggr(mv[:, t], stats[:, t]))
                note(dve.tensor_tensor(span[:, 0, 0], span[:, 0, 0], span[:, 0, 1], ALU.max))
                note(dve.tensor_tensor(span[:, 1, 0], span[:, 1, 0], span[:, 1, 1], ALU.min))
                noted()
                link(dve.tensor_scalar(power_in[:, 0], mv[:, :, 1], EPS, None, ALU.add))
                link(dve.reciprocal(q_s[:, 4], power_in[:, 0]))
                link(dve.tensor_tensor(power_in[:, 1], q_s[:, 4], mv[:, :, 1], ALU.mult))
                dve.tensor_scalar(power_in[:, 1], power_in[:, 1], EPS, None, ALU.add).then_inc(power_ready, 1)
                note(dve.tensor_tensor(span[:, 0, 0], span[:, 0, 0], mv[:, :, 0], ALU.subtract))
                link(dve.tensor_tensor(span[:, 1, 0], mv[:, :, 0], span[:, 1, 0], ALU.subtract))
                link(dve.tensor_tensor(q_s[:, 2], span[:, 0, 0], span[:, 1, 0], ALU.max))
                dve.wait_ge(power_done, 1)
                link(dve.tensor_tensor(q_s[:, 1], power_out[:, 0], power_out[:, 1], ALU.mult))
                link(dve.tensor_tensor(q_s[:, 3], q_s[:, 2], q_s[:, 1], ALU.mult))
                quant_rows(q_s[:, 1])
                for t in range(NT + 1):
                    if t < NT:
                        note(dve.tensor_scalar(xn2[:, t], base1[:, t], mv[:, t, 0:1], q_s[:, 5, t:t + 1], ALU.subtract, ALU.mult))
                    if t:
                        dve.wait_ge(v_chain, vn[0] - (t < NT))
                        dve.tensor_scalar(xq[:, t - 1], xn2[:, t - 1], ROUND, ROUND, ALU.add, ALU.subtract).then_inc(quant_ready, 1)
                quant_back(1)
                noted()

            def expert_split(i):
                e = i // 2
                tile = TT["h_a"] if i < KD else TT["h_b"]
                wait_emptied(dve, f"e1.{i}")
                wait_emptied(dve, f"cw.{e}")
                dve.tensor_tensor(hf[:, i % 2], hf[:, i % 2], cw_row[:, e], ALU.mult).then_inc(h_scaled, 1)
                dve.wait_ge(h_scaled, 2 * i + 1)
                hi[0] += 1
                dve.wait_ge(act_hi, hi[0])
                dve.tensor_tensor(tile[:, 1, i % KD], hf[:, i % 2], f(tile[:, 0, i % KD]), ALU.subtract).then_inc(h_scaled, 1)

            def dead_edges(q):
                pr = f"keys.{q}"
                wait_full(dve, pr)
                for j in range(4):
                    c = 4 * q + j
                    ins = dve.scalar_tensor_tensor(same[:, c % 2], out_of(pr)[:, j * P:(j + 1) * P], key[:, c:c + 1],
                                                   later[:], ALU.is_equal, ALU.mult, accum_out=dead[:, c:c + 1])
                    if j == 3:
                        emptied(ins, pr)
                        wait_emptied(dve, pr)
                    else:
                        link(ins)

            def edge_group(q):
                if q:
                    dead_edges(q)
                noted()
                sl = slice(4 * q, 4 * q + 4)
                link(dve.scalar_tensor_tensor(value[:, sl], dead[:, sl], 0.0, power[:, sl].bitcast(F32),
                                              ALU.is_equal, ALU.mult))
                for j in range(4):
                    c = 4 * q + j
                    if c >= 8:
                        dve.wait_ge(onehots_used, c - 7)
                    dve.tensor_scalar(onehot[:, c % 8, 0], node[:], edge_f[:, 0, c:c + 1], None, ALU.is_equal)
                    dve.tensor_scalar(onehot[:, c % 8, 1], node[:], edge_f[:, 1, c:c + 1], None, ALU.is_equal)
                    dve.tensor_scalar(onehot[:, c % 8, 2], node[:], edge_f[:, 1, c:c + 1], value[:, c:c + 1],
                                      ALU.is_equal, ALU.mult).then_inc(onehots, 1)

            dve.wait_ge(edges_landed, 16)
            link(dve.tensor_copy(edge_f[:], edge_i[:]))
            link(dve.scalar_tensor_tensor(key[:], edge_f[:, 1], 1.0 / 512, edge_f[:, 0], ALU.mult, ALU.add))
            dve.tensor_copy(key_part[:, 0], edge_f[:, 0])
            dve.tensor_scalar(key_part[:, 1], edge_f[:, 1], 1.0 / 512, None, ALU.mult).then_inc(key_ready, 1)
            link(dve.tensor_scalar(four0[:], edge_f[:, 2], 0.0, 4.0, ALU.is_equal, ALU.mult))
            note(dve.scalar_tensor_tensor(cls[:], edge_f[:, 2], -1.0, four0[:], ALU.add, ALU.add))
            dve.wait_ge(key_ready, 1)
            dead_edges(0)
            for t in range(NT):
                dve.wait_ge(x_tile[t], 16)
                for c in range(2):
                    half_stats(x_sb, t, c)
                tile_stats(t)
                if t:
                    layer_norm(x_sb, xn1, t - 1)
            dve.wait_ge(consts, 7)
            link(dve.tensor_tensor(cls[:], cls[:], chunk_no[:], ALU.add))
            note(dve.tensor_scalar(power[:], cls[:], 8388608.0, None, ALU.mult))
            layer_norm(x_sb, xn1, NT - 1)
            split_up_to(0)

            for s in EVAC_STEPS:
                kind = s[0]
                if kind == "graph":
                    if s[1] == 0:
                        edge_group(0)
                        dve.wait_ge(w8_exp, 1)
                        dve.tensor_scalar(w8[:, 1], w8[:, 1], 1.0, None, ALU.add).then_inc(w8_one, 1)
                    if s[1] == 1:
                        dve.wait_ge(w8_ln, 1)
                        link(dve.tensor_scalar(w8[:, 0], tiny_sb[:, 0:4], 0.0, None, ALU.max))
                        link(dve.tensor_tensor(w8[:, 2], w8[:, 2], w8[:, 0], ALU.add))
                        dve.tensor_scalar(w8[:, 2], w8[:, 2], 8.0, None, ALU.mult).then_inc(w8_ready, 1)
                    if s[1] + 1 < GROUPS:
                        edge_group(s[1] + 1)
                if s == ("graph", GROUPS - 1):
                    for t in range(NT):
                        pr = f"last_edge.{t}"
                        wait_full(dve, pr)
                        dve.tensor_scalar(no_edge[:, t], out_of(pr)[:, 0:N], 0.0, 8 * NO_EDGE, ALU.is_equal, ALU.mult)
                        emptied(dve.tensor_scalar(edge_cls[:, t], out_of(pr)[:, 0:N].bitcast(I32), 23, 3,
                                                  ALU.logical_shift_right, ALU.bitwise_and), pr)
                if kind == "transpose":
                    for k in range(KD):
                        chunk_lo(s[1], k, f"{s[1]}.{k}")
                    if s[1] == "xn1":
                        split_up_to(AHEAD - 1)
                        dve.wait_ge(small_landed, 32)
                        link(dve.tensor_scalar(w8[:, 2], tiny_sb[:, 0:4], -1.0, None, ALU.mult))
                        dve.tensor_tensor(w8[:, 0], tiny_sb[:, 0:4], w8[:, 2], ALU.min).then_inc(w8_neg, 1)
                if kind == "softmax":
                    softmax(s[1], s[2])
                if kind == "transpose_y":
                    for k in range(2 * s[1], 2 * s[1] + 2):
                        chunk_lo("y", k, f"y.{k}")
                if kind == "degree":
                    wait_full(dve, "degree")
                    emptied(dve.tensor_scalar(dis[:, 0], out_of("degree")[:, 0:2 * NT:2], 1.0, None, ALU.max), "degree")
                if kind == "norm":
                    wait_full(dve, "norm")
                    for t in range(NT):
                        ins = dve.scalar_tensor_tensor(count[:, t], count[:, t], dis[:, 1, t:t + 1], out_of("norm")[:, 0:N],
                                                       ALU.mult, ALU.mult)
                        if t == NT - 1:
                            emptied(ins, "norm")
                if kind == "unit":
                    _, u, name, i = s
                    if u + AHEAD < len(UNITS):
                        if name in NODE_MAJOR and (name, (i + 1) / NODE_MAJOR[name][1] - 1) in STAGGERED:
                            late.append(u + AHEAD)
                        else:
                            split_up_to(u + AHEAD)
                    if name in ("v1", "q1", "k1"):
                        chunk_lo(name, i, f"{name}.{i}", COLS[name] + i)
                    if name in ("q2", "k2"):
                        hi[0] += 2
                        dve.wait_ge(act_hi, hi[0])
                        for r in range(2):
                            own, other = slice(64 * r, 64 * r + 64), slice(64 - 64 * r, 128 - 64 * r)
                            src, high, low = ((qcat[own, i % 2, r], qcat[other, i % 2, r]) if name == "q2" else
                                              (kcat[own, r, 0], kcat[own, r, 1])), None, None
                            high, low = src
                            ins = dve.scalar_tensor_tensor(low, out_of(f"{name}.{i}")[own, 0:N],
                                                           bias[own, COLS[name] + i:COLS[name] + i + 1], f(high),
                                                           ALU.add, ALU.subtract)
                            if r:
                                emptied(ins, f"{name}.{i}")
                    if name == "mk":
                        wait_full(dve, f"mk.{i}")
                        dve.tensor_reduce(mk_s[:, 0, i:i + 1], out_of(f"mk.{i}")[:, 0:N], X, ALU.max,
                                          negate=True).then_inc(mk_max, 1)
                    if name in NODE_MAJOR and i % NODE_MAJOR[name][1] == NODE_MAJOR[name][1] - 1:
                        c = i // NODE_MAJOR[name][1]
                        sl = slice(c * HALF, (c + 1) * HALF)
                        if name in ("v2", "v"):
                            full_t, rw = (v2f, "biv") if name == "v2" else (kf, "bv")
                            wait_row(dve, rw)
                            if (name, c) == ("v", 0):
                                dve.wait_ge(node_split, 4 * NT)
                                dve.tensor_copy(v_hi[:, :, :, P:P + 2].rearrange("p t j c -> p (t j) c"),
                                                ones[:, 0:2 * NT * KD].rearrange("p (j c) -> p j c", c=2)).then_inc(v_ones, 1)
                            for t in range(NT):
                                pr = f"{name}.{c}.{t}"
                                wait_full(dve, pr)
                                emptied(dve.tensor_tensor(full_t[:, t, sl], out_of(pr)[:], row(rw, c * HALF, (c + 1) * HALF),
                                                          ALU.add), pr)
                            for t in range(NT):
                                wait_emptied(dve, f"{name}.{c}.{t}")
                                if name == "v2":
                                    low, high, src = v2[:, 1, t, sl], v2[:, 0, t, sl], v2f[:, t, sl]
                                else:
                                    low, high = v_lo[:, t, 4 * c:4 * c + 4], v_hi[:, t, 4 * c:4 * c + 4, 0:P]
                                    src = kf[:, t, sl].rearrange("p (j c) -> p j c", c=P)
                                lo_part(low, src, high).then_inc(node_split, 1)
                        if name == "mv":
                            for t in range(NT):
                                lo_part(mvn[:, 1, t], out_of(f"mv.0.{t}")[:], mvn[:, 0, t], f"mv.0.{t}")
                        if name in ("mq", "k") or (name, c) == ("q", 0):
                            softmax(name, c)
                            if name == "k":
                                for t in range(NT):
                                    dve.wait_ge(q_ready, sub_no(name, c, t))
                                    lo_part(k2n[:, 1, t, sl], kf[:, t, sl], k2n[:, 0, t, sl]).then_inc(node_split, 1)
                        if name == "wo":
                            for t in range(NT):
                                dve.wait_ge(base1_ready, t + 1)
                                wait_full(dve, f"wo.{c}.{t}")
                                pr = f"wo.{c}.{t}"
                                emptied(dve.tensor_tensor_reduce(out=base1[:, t, sl], in0=out_of(pr)[:], in1=base1[:, t, sl],
                                                                 scale=1.0, scalar=-3.0e38, op0=ALU.add, op1=ALU.max,
                                                                 accum_out=span[:, 0, c, t:t + 1]), pr)
                                wait_emptied(dve, pr)
                                half_stats(base1, t, c)
                                note(dve.tensor_reduce(span[:, 1, c, t:t + 1], base1[:, t, sl], X, ALU.min))
                        if name == "g1":
                            wait_row(dve, "gnn_b1")
                            for t in range(NT):
                                wait_full(dve, f"g1.0.{t}")
                                emptied(dve.tensor_tensor(g[:, t], out_of(f"g1.0.{t}")[:], row("gnn_b1"), ALU.add), f"g1.0.{t}")
                            for t in range(NT):
                                wait_emptied(dve, f"g1.0.{t}")
                                lo_part(g2[:, 1, t], g[:, t], g2[:, 0, t]).then_inc(g_ready, 1)
                        if name == "wp":
                            for t in range(NT):
                                dve.wait_ge(base3_ready, t + 1)
                                wait_full(dve, f"wp.{c}.{t}")
                                emptied(dve.tensor_tensor(x_sb[:, t, sl], x_sb[:, t, sl], out_of(f"wp.{c}.{t}")[:], ALU.add),
                                        f"wp.{c}.{t}")
                                wait_emptied(dve, f"wp.{c}.{t}")
                                half_stats(x_sb, t, c)
                                if c == 1:
                                    tile_stats(t)
                                    if t:
                                        layer_norm(x_sb, xn4, t - 1)
                            if c == 1:
                                layer_norm(x_sb, xn4, NT - 1)
                                split_up_to(late.pop())
                        if name == "e2":
                            for t in range(NT):
                                dve.wait_ge(base4_ready, 2 * NT)
                                wait_full(dve, f"e2.{c}.{t}")
                                dve.tensor_tensor(x_sb[:, t, sl], x_sb[:, t, sl], out_of(f"e2.{c}.{t}")[:],
                                                  ALU.add).then_inc(out_ready, 1)
                    if name == "e1" and i >= LATE:
                        expert_split(i)
                if kind == "mix0_kT":
                    for t in s[1]:
                        lo_part(mkn[:, 1, t], out_of(f"kn.{t}")[:], mkn[:, 0, t], f"kn.{t}")
                if kind == "mix0_context":
                    wait_emptied(dve, "mk.3")
                    link(dve.reciprocal(mk_s[:, 2], mk_s[:, 1]))
                    wait_full(dve, "mix_context")
                    emptied(dve.tensor_tensor(mctx[:], out_of("mix_context")[:].rearrange("p (j c) -> p j c", c=P),
                                              bcast(mk_s[:, 2], [P, KH, P]), ALU.mult), "mix_context")
                    wait_emptied(dve, "mix_context")
                    dve.memset(f(mctx2[:]), 0.0).then_inc(mctx_f, 1)
                    dve.wait_ge(mctx_f, 1)
                    for r in range(2):
                        hs = slice(64 * r, 64 * r + 64)
                        lo_part(mctx2[hs, 1, :, hs], mctx[hs, :, hs], mctx2[hs, 0, :, hs]).then_inc(mctx_ready, 1)
                if kind == "mix0_qT":
                    for j in s[1]:
                        lo_part(mqT[:, 1, j], out_of(f"qT.{j}")[:, 0:N], mqT[:, 0, j], f"qT.{j}")
                if kind == "mix0_out":
                    for j in s[1]:
                        chunk_lo("mixo", j, f"mixo.{j}")
                if kind == "scores":
                    h = s[1]
                    b = h % 2
                    if h == 0:
                        dve.wait_ge(mask_ready, 1)
                        wait_full(dve, "mixo.3")
                    if h >= 1:
                        dve.wait_ge(s_max, h)
                    if h >= 2:
                        wait_full(dve, f"pT.{h - 2}.2")
                    for t in range(NT):
                        pr = f"scores.{h}.{t}"
                        wait_full(dve, pr)
                        emptied(dve.tensor_tensor_reduce(out=prob[:, b, t], in0=out_of(pr)[:, 0:N], in1=mask[:, t], scale=1.0,
                                                         scalar=-3.0e38, op0=ALU.add, op1=ALU.max,
                                                         accum_out=top1[:, 0, t:t + 1]), pr)
                    for t in range(NT):
                        wait_emptied(dve, f"scores.{h}.{t}")
                    dve.tensor_scalar(nmax[:, b], top1[:, 0], -0.125, None, ALU.mult).then_inc(s_max, 1)
                if kind == "probs":
                    h = s[1]
                    b = h % 2
                    for m in range(NT):
                        lo_part(probT[:, 1, m], out_of(f"pT.{h}.{m}")[:, 0:N], probT[:, 0, m], f"pT.{h}.{m}")
                if kind == "normalise":
                    h = s[1]
                    dve.wait_ge(s_exp, NT * (h + 1))
                    link(dve.reciprocal(rsum[:, h % 2], rsum[:, h % 2]))
                    for t in range(NT):
                        dve.tensor_scalar(prob[:, h % 2, t], prob[:, h % 2, t], rsum[:, h % 2, t:t + 1], None,
                                          ALU.mult).then_inc(p_ready, 1)
                if kind == "attend":
                    h = s[1]
                    hs = slice(64 * (h % 2), 64 * (h % 2) + 64)
                    lo_part(TT["o"][hs, 1, h // 2], out_of(f"attend.{h}")[hs, 0:N], TT["o"][hs, 0, h // 2], f"attend.{h}")
                if kind == "ffn_mean":
                    w = s[1]
                    pr = f"w_sum.{w}"
                    wait_full(dve, pr)
                    emptied(dve.tensor_scalar(w_s[:, 1, w:w + 1], out_of(pr)[:, 0:1], 1.0 / (D * HID), CLIP, ALU.mult, ALU.max), pr)
                    wait_emptied(dve, pr)
                    link(dve.reciprocal(w_s[:, 0, w:w + 1], w_s[:, 1, w:w + 1]))
                    raw_w = (w1r, w2r)[w]
                    link(dve.tensor_scalar(raw_w[:], raw_w[:], w_s[:, 0, w:w + 1], 1.0, ALU.mult, ALU.min))
                    ins = dve.tensor_scalar(raw_w[:], raw_w[:], -1.0, ROUND, ALU.max, ALU.add)
                    if w == 1:
                        link(ins)
                        dve.tensor_scalar(w2q[:].rearrange("p a b -> p (a b)"), w2r[:], ROUND, None, ALU.subtract).then_inc(w2_quant, 1)
                    else:
                        ins.then_inc(w1_unit, 1)
                if kind == "ffn":
                    norm_quant()
                    split_up_to(late.pop())
                    for k in range(KD // 2):
                        pr = f"xqT.{k}"
                        wait_full(dve, pr)
                        emptied(dve.tensor_scalar(xqT[:, 2 * k:2 * k + 2], out_of(pr)[:].bitcast(BF16)[:, 0:2 * N].rearrange(
                            "p (a n) -> p a n", a=2), 127.0, -128.0, ALU.min, ALU.max), pr)
                    wait_row(dve, "ffn_b1")
                    for t in range(NT):
                        wait_full(dve, f"ffn_h.{t}")
                        emptied(dve.scalar_tensor_tensor(hn[:, t], out_of(f"ffn_h.{t}")[:], q_s[:, 6, t:t + 1], row("ffn_b1"),
                                                         ALU.mult, ALU.add), f"ffn_h.{t}")
                    hidden_quant()
                    for k in range(KH // 2):
                        pr = f"hqT.{k}"
                        wait_full(dve, pr)
                        emptied(dve.tensor_scalar(hqT[:, 2 * k:2 * k + 2], out_of(pr)[:].bitcast(BF16)[:, 0:2 * N].rearrange(
                            "p (a n) -> p a n", a=2), 127.0, -128.0, ALU.min, ALU.max), pr)
                    for t in range(NT):
                        dve.wait_ge(base2_ready, t + 1)
                        for c in range(2):
                            pr = f"ffn_o.{t}.{c}"
                            sl = slice(c * HALF, (c + 1) * HALF)
                            wait_full(dve, pr)
                            emptied(dve.scalar_tensor_tensor(x_sb[:, t, sl], out_of(pr)[:], q_s[:, 7, t:t + 1], base2[:, t, sl],
                                                             ALU.mult, ALU.add), pr)
                            wait_emptied(dve, pr)
                            half_stats(x_sb, t, c)
                        tile_stats(t)
                        if t:
                            layer_norm(x_sb, xn3, t - 1)
                    layer_norm(x_sb, xn3, NT - 1)
                if kind == "hop_dot":
                    n = s[1]
                    for t in range(NT):
                        wait_emptied(dve, f"hop.{n - 1}.{t}" if n else f"g1.0.{t}")
                    wait_row(dve, f"wg{n}")
                    for t in range(NT):
                        for j in range(2):
                            dve.wait_ge(v_chain, vn[0] - (t + j > 0))
                            note(dve.tensor_tensor_reduce(out=gjunk[:, j], in0=g[:, t], in1=row(f"wg{n}", j * HID, (j + 1) * HID),
                                                          scale=1.0, scalar=0.0, op0=ALU.mult, op1=ALU.add,
                                                          accum_out=aij[:, j, t:t + 1]))
                    noted()
                    dve.tensor_scalar(aij[:, 1], aij[:, 1], tiny_sb[:, 4 + n:5 + n], None, ALU.add).then_inc(aij_ready, 1)
                if kind == "hop_msg":
                    n = s[1]
                    wait_emptied(dve, f"ai.{n}")
                    dve.wait_ge(msg_f, n + 1)
                    lo_part(msg2[:, 1], msg[:], msg2[:, 0]).then_inc(msg_ready, 1)
                if kind == "hop_sum":
                    n = s[1]
                    for t in range(NT):
                        pr = f"hop.{n}.{t}"
                        if n == 0:
                            dve.wait_ge(base4_ready, t + 1)
                        wait_full(dve, pr)
                        emptied(dve.tensor_tensor(g[:, t], g[:, t], out_of(pr)[:], ALU.add), pr)
                    if n < HOPS - 1:
                        for t in range(NT):
                            wait_emptied(dve, f"hop.{n}.{t}")
                            lo_part(g2[:, 1, t], g[:, t], g2[:, 0, t]).then_inc(g_ready, 1)
                if kind == "context":
                    dve.memset(f(ctx1[:]), 0.0).then_inc(ctx_f, 1)
                    dve.wait_ge(ctx_f, 1)
                    for b in range(3):
                        np_ = min(3, KD - 3 * b)
                        src = out_of(f"context.{b}")[:, 0:130 * np_].rearrange("p (j c) -> p j c", c=130)
                        hi[0] += 4
                        dve.wait_ge(act_hi, hi[0])
                        for r in range(2):
                            hs = slice(64 * r, 64 * r + 64)
                            js = slice(3 * b, 3 * b + np_)
                            note(dve.tensor_tensor(ctx1[hs, 1, js, hs], src[hs, :, hs], f(ctx1[hs, 0, js, hs]), ALU.subtract))
                            ins = dve.tensor_tensor(ctx1[hs, 1, js, P + r], src[hs, :, P], f(ctx1[hs, 0, js, P + r]),
                                                    ALU.subtract)
                            if r == 1:
                                emptied(ins, f"context.{b}")
                            else:
                                note(ins)
                if kind == "queries":
                    for j in range(2 * s[1], 2 * s[1] + 2):
                        chunk_lo("q1T", j, f"q1T.{j}")
                if kind == "y":
                    for b in range(NT + 1):
                        pr = f"yn.{s[1]}.{b}"
                        wait_full(dve, pr)
                        src = out_of(pr)[:, 0:390].rearrange("p (j c) -> p j c", c=130)
                        if b < NT:
                            qs = qf[:, b, HALF * s[1]:HALF * s[1] + 3 * P].rearrange("p (j c) -> p j c", c=P)
                        else:
                            qs = qf[:, :, HALF * s[1] + 3 * P:HALF * s[1] + 4 * P]
                        link(dve.reciprocal(den[:].rearrange("p (j r) -> p j r", r=2), src[:, :, P:P + 2]))
                        emptied(dve.tensor_tensor(ytmp[:].rearrange("p (j r d) -> p j r d", r=2, d=DH),
                                                  src[:, :, 0:P].rearrange("p j (r d) -> p j r d", r=2),
                                                  den[:].rearrange("p (j r) -> p j r", r=2).unsqueeze(3).to_broadcast([P, 3, 2, DH]),
                                                  ALU.mult), pr)
                        wait_emptied(dve, pr)
                        dve.tensor_tensor(qs, qs, ytmp[:].rearrange("p (j c) -> p j c", c=P), ALU.add).then_inc(y_ready, 1)
                        dve.wait_ge(y_ready, (NT + 1) * s[1] + b + 1)
                if kind == "gate_weights":
                    dve.wait_ge(gate_hi, 1)
                    dve.tensor_tensor(gate2[:, 1, :, 0:EXPERTS], gate[:].rearrange("p (k e) -> p k e", e=EXPERTS),
                                      f(gate2[:, 0, :, 0:EXPERTS]), ALU.subtract).then_inc(gate_ready, 1)
                if kind == "gate":
                    wait_full(dve, "logitsT")
                    emptied(dve.tensor_copy(lgT[:], out_of("logitsT")[:, 0:N]), "logitsT")
                if kind == "gate_pick":
                    link(dve.memset(cw[:], 0.0))
                    dve.wait_ge(consts, 8)
                    wait_full(dve, "logits")
                    logits = out_of("logits")[:, 0:N].rearrange("p (t c) -> p t c", c=P)[:, :, 0:EXPERTS]
                    link(dve.tensor_reduce(gsum[:, 0], logits, X, ALU.max, negate=True))
                    emptied(dve.tensor_tensor(lg[:], logits, bcast(gsum[:, 0], [P, NT, EXPERTS]), ALU.add), "logits")
                    for t in range(NT):
                        dve.wait_ge(lg_exp, t + 1)
                        link(dve.tensor_reduce(gsum[:, 1, t:t + 1], lg[:, t], X, ALU.add))
                        link(dve.reciprocal(gsum[:, 1, t:t + 1], gsum[:, 1, t:t + 1]))
                        link(dve.tensor_scalar(lg[:, t], lg[:, t], gsum[:, 1, t:t + 1], None, ALU.mult))
                        link(dve.max(top[:, t], lg[:, t]))
                        link(dve.max_index(top_at[:, t], top[:, t], lg[:, t]))
                        link(dve.tensor_copy(top_f[:, t], top_at[:, t]))
                        link(dve.scalar_tensor_tensor(gsum[:, 2, t:t + 1], top[:, t, 0:1], 1e-8, top[:, t, 1:2], ALU.add, ALU.add))
                        link(dve.reciprocal(gsum[:, 2, t:t + 1], gsum[:, 2, t:t + 1]))
                        link(dve.tensor_scalar(top[:, t, 0:2], top[:, t, 0:2], gsum[:, 2, t:t + 1], None, ALU.mult))
                        for j in range(2):
                            link(dve.tensor_scalar(pick[:, j], expert[:], top_f[:, t, j:j + 1], top[:, t, j:j + 1],
                                                   ALU.is_equal, ALU.mult))
                        link(dve.tensor_tensor(cw[:, t, 0:EXPERTS], pick[:, 0], pick[:, 1], ALU.add))
                        dve.tensor_copy(cw[:, t, 32:96].rearrange("p (j c) -> p j c", c=32)[:, :, 0:EXPERTS],
                                        cw[:, t, 0:EXPERTS].unsqueeze(1).to_broadcast([P, 2, EXPERTS])).then_inc(cw_ready, 1)
                        dve.wait_ge(cw_ready, t + 1)
                if kind == "gate_rows":
                    low = slice(64, 96)
                    lo_part(cwT[low], out_of("cwT")[low, 0:N], cwT[low], "cwT")
                    dve.wait_ge(eb2_hi, 1)
                    low = slice(32, 64)
                    dve.tensor_tensor(eb2_parts[low], eb2[low], f(eb2_parts[low]), ALU.subtract).then_inc(eb2_ready, 1)
                    for i in range(LATE):
                        expert_split(i)

        @block.tensor
        def _(pe):
            HI, LO = 0, 1
            PASSES = ((HI, HI), (HI, LO), (LO, HI))

            def products(dst, terms):
                last = None
                for n, (a, b) in enumerate(terms):
                    for m, (pa, pb) in enumerate(PASSES):
                        last = pe.matmul(dst, a(pa), b(pb), start=(n == 0 and m == 0),
                                         stop=(n == len(terms) - 1 and m == 2))
                return last

            def transposes(name, srcs):
                wait_bank(pe, name)
                for n, src in enumerate(srcs):
                    last = pe.transpose(out_of(name)[:, n * P:(n + 1) * P], src, ident[:])
                full(last, name)

            def spread(name, col):
                wait_bank(pe, name)
                for t in range(NT):
                    last = pe.matmul(out_of(name)[:, t * P:(t + 1) * P], col(t).to_broadcast([P, P]), ident[:],
                                     start=True, stop=True)
                full(last, name)

            pe.wait_ge(consts, 4)
            pe.wait_ge(key_ready, 1)
            nats = {"xn1": (xn1, 0), "xn3": (xn3, NT), "xn4": (xn4, 2 * NT)}

            def keys(q):
                pr = f"keys.{q}"
                wait_bank(pe, pr)
                for j in range(4):
                    c = 4 * q + j
                    for h in range(2):
                        last = pe.matmul(out_of(pr)[:, j * P:(j + 1) * P], key_part[:, h, c:c + 1].to_broadcast([P, P]),
                                         ident_h[:], start=(h == 0), stop=(h == 1))
                full(last, pr)

            for s in STEPS:
                kind = s[0]
                if kind == "graph":
                    if s[1] == 0:
                        for k in range(1, KD - 1):
                            wait_emptied(pe, f"xn1.{k}")
                        pe.wait_ge(consts, 7)
                        for t in range(NT):
                            pe.matmul(bank[t][:, 0:N], ident_b[:], diag[:, (2 - t) * P:(2 - t) * P + N], start=True, stop=False)
                    if s[1] + 1 < GROUPS:
                        keys(s[1] + 1)
                    for c in range(4 * s[1], 4 * s[1] + 4):
                        pe.wait_ge(onehots, c + 1)
                        for t in range(NT):
                            src = onehot[:, c % 8, 0, t * P:(t + 1) * P]
                            a = pe.matmul(bank[t][:, 0:N], src, onehot[:, c % 8, 2], start=False, stop=(c == EC - 1))
                            b = pe.matmul(bank[3 + t][:, 0:N], src, onehot[:, c % 8, 1], start=(c == 0), stop=(c == EC - 1))
                            if c == EC - 1:
                                full(a, f"last_edge.{t}")
                                full(b, f"count.{t}")
                        if c < EC - 1:
                            b.then_inc(onehots_used, 1)
                if kind == "transpose":
                    src, n = nats[s[1]]
                    if s[1] == "xn1":
                        keys(0)
                    for t, k in [(t, k) for t in range(NT) for k in range(KD - 1)] + [(t, KD - 1) for t in range(NT)]:
                        if k == 0:
                            pe.wait_ge(nat_ready, n + t + 1)
                        pr = f"{s[1]}.{k}"
                        if t == 0:
                            wait_bank(pe, pr)
                        last = pe.transpose(out_of(pr)[:, t * P:(t + 1) * P], src[:, t, k * P:(k + 1) * P], ident[:])
                        if t == NT - 1:
                            full(last, pr)
                if kind == "transpose_y":
                    pe.wait_ge(y_ready, (NT + 1) * (s[1] // 2 + 1))
                    for k in range(2 * s[1], 2 * s[1] + 2):
                        transposes(f"y.{k}", [qf[:, t, k * P:(k + 1) * P] for t in range(NT)])
                if kind == "degree":
                    wait_emptied(pe, "count.2")
                    wait_bank(pe, "degree")
                    for c in range(NT):
                        for r in range(NT):
                            last = pe.matmul(out_of("degree")[:, 2 * c:2 * c + 2], count[:, r, c * P:(c + 1) * P], ones[:, 0:2],
                                             start=(r == 0), stop=(r == NT - 1))
                    full(last, "degree")
                if kind == "norm":
                    pe.wait_ge(dis_ready, 1)
                    spread("norm", lambda t: dis[:, 1, t:t + 1])
                if kind == "unit":
                    _, u, name, i = s
                    wait_split(pe, u)
                    w = (w_hi, w_lo)
                    slot = u % RING
                    if name in FEATURE_MAJOR:
                        src = FEATURE_MAJOR[name]
                        pr = f"{name}.{i}"
                        wait_bank(pe, pr)
                        for k in range(KD):
                            if i == 0 and name in ("v1", "q2", "k2", "e1"):
                                wait_emptied(pe, f"{src}.{k}")
                            for m, (pa, pb) in enumerate(PASSES):
                                last = pe.matmul(out_of(pr)[:, 0:N], w[pa][:, slot, k * P:(k + 1) * P], TT[src][:, pb, k],
                                                 start=(k == 0 and m == 0), stop=(k == KD - 1 and m == 2))
                        last.then_inc(unit_done, 1)
                    else:
                        src, per = NODE_MAJOR[name]
                        c = i // per
                        here = [i]
                        if (name, c) in STAGGERED and i % per >= per - 2:
                            if i % per == per - 2:
                                continue
                            here = [i - 1, i]
                        for kk in [n % per for n in here]:
                            if name == "e2":
                                if c == 0:
                                    pe.wait_ge(h_scaled, 2 * (2 * kk + 2))
                                if i == 0:
                                    pe.wait_ge(eb2_ready, 1)
                                    wait_emptied(pe, "cwT")
                            elif name == "wo":
                                if i == 0:
                                    wait_emptied(pe, "mixo.2")
                                    wait_emptied(pe, "mixo.3")
                                if c == 0 and kk >= 2:
                                    wait_emptied(pe, f"attend.{4 * kk - 5}")
                            elif c == 0 and name in ("v2", "g1") or name == "wp":
                                wait_emptied(pe, f"{src}.{2 * kk}")
                                wait_emptied(pe, f"{src}.{2 * kk + 1}")
                        for t in range(NT):
                            pr = f"{name}.{c}.{t}"
                            ts = slice(t * P, (t + 1) * P)
                            if i % per == 0:
                                wait_bank(pe, pr)
                                if name == "e2":
                                    pe.matmul(out_of(pr)[:], cwT[:, ts], eb2_parts[:, c * HALF:(c + 1) * HALF],
                                              start=True, stop=False)
                            for n in here:
                                kk, at_ = n % per, (u - (i - n)) % RING
                                for j in range(2):
                                    k = 2 * kk + j
                                    if name == "e2":
                                        tile = TT["h_a"] if k < KD else TT["h_b"]
                                        k = k % KD
                                    elif name == "wo":
                                        tile, k = (TT["mixo"], k) if k < KH else (TT["o"], k - KH)
                                    else:
                                        tile = TT[src]
                                    for m, (pa, pb) in enumerate(PASSES):
                                        last = pe.matmul(out_of(pr)[:], tile[:, pa, k, ts], w[pb][:, at_, j * HALF:(j + 1) * HALF],
                                                         start=(kk == 0 and j == 0 and m == 0 and name != "e2"),
                                                         stop=(kk == per - 1 and j == 1 and m == 2))
                                if t == NT - 1:
                                    last.then_inc(unit_done, 1)
                                elif kk == per - 1:
                                    full(last, pr)
                if kind == "mix0_kT":
                    wait_emptied(pe, "mk.3")
                    for t in s[1]:
                        transposes(f"kn.{t}", [ekT[:, j, t * P:(t + 1) * P] for j in range(KH)])
                if kind == "mix0_context":
                    pr = "mix_context"
                    wait_emptied(pe, "kn.2")
                    wait_emptied(pe, "kn.1")
                    wait_emptied(pe, "mv.0.2")
                    wait_bank(pe, pr)
                    for j in range(KH):
                        js = slice(j * P, (j + 1) * P)
                        last = products(out_of(pr)[:, js], [(lambda p, t=t: mkn[:, p, t, js], lambda p, t=t: mvn[:, p, t, js])
                                                            for t in range(NT)])
                    full(last, pr)
                if kind == "mix0_qT":
                    pe.wait_ge(q_ready, sub_no("mq", 0, NT - 1))
                    for j in s[1]:
                        transposes(f"qT.{j}", [mqn[:, t, j * P:(j + 1) * P] for t in range(NT)])
                if kind == "mix0_out":
                    pe.wait_ge(mctx_ready, 2)
                    for j in s[1]:
                        pr = f"mixo.{j}"
                        wait_emptied(pe, f"qT.{j}")
                        wait_bank(pe, pr)
                        full(products(out_of(pr)[:, 0:N], [(lambda p: mctx2[:, p, j], lambda p: mqT[:, p, j])]), pr)
                if kind == "scores":
                    h = s[1]
                    j, r = h // 2, h % 2
                    wait_emptied(pe, f"q2.{j}")
                    pe.wait_ge(k_twice, 32 * (j + 1))
                    for t in range(NT):
                        pr = f"scores.{h}.{t}"
                        wait_bank(pe, pr)
                        for p in (HI, LO):
                            last = pe.matmul(out_of(pr)[:, 0:N], qcat[:, j % 2, r, t * P:(t + 1) * P], kcat[:, r, p],
                                             start=(p == HI), stop=(p == LO))
                        full(last, pr)
                if kind == "probs":
                    h = s[1]
                    pe.wait_ge(p_ready, NT * (h + 1))
                    for m in range(NT):
                        transposes(f"pT.{h}.{m}", [prob[:, h % 2, t, m * P:(m + 1) * P] for t in range(NT)])
                if kind == "attend":
                    h = s[1]
                    pr = f"attend.{h}"
                    if h == 0:
                        pe.wait_ge(node_split, 2 * NT)
                    wait_emptied(pe, f"pT.{h}.2")
                    wait_emptied(pe, f"pT.{h}.1")
                    wait_emptied(pe, f"pT.{h}.0")
                    wait_bank(pe, pr)
                    js = slice(h // 2 * P, (h // 2 + 1) * P)
                    full(products(out_of(pr)[:, 0:N], [(lambda p, m=m: v2[:, p, m, js], lambda p, m=m: probT[:, p, m])
                                                       for m in range(NT)]), pr)
                if kind == "ffn_mean":
                    w = s[1]
                    pe.wait_ge(w_abs, 2 - w)
                    wait_bank(pe, f"w_sum.{w}")
                    full(pe.matmul(out_of(f"w_sum.{w}")[:, 0:1], ones[:], w_s[:, 0, w:w + 1], start=True, stop=True), f"w_sum.{w}")
                if kind == "ffn":
                    def bf16_transposes(name, src, ready, pairs):
                        for t in range(NT):
                            pe.wait_ge(quant_ready, ready + t + 1)
                            for k in range(pairs):
                                pr = f"{name}.{k}"
                                if t == 0:
                                    wait_bank(pe, pr)
                                view = out_of(pr)[:].bitcast(BF16)
                                for a in range(2):
                                    last = pe.transpose(view[:, (a * NT + t) * P:(a * NT + t + 1) * P],
                                                        src[:, t, (2 * k + a) * P:(2 * k + a + 1) * P], ident_b[:])
                                if t == NT - 1:
                                    full(last, pr)

                    bf16_transposes("xqT", xq, 0, KD // 2)
                    pe.wait_ge(w1_quant, 1)
                    for t in range(NT):
                        pr = f"ffn_h.{t}"
                        wait_bank(pe, pr)
                        for k in range(KD):
                            if t == 0 and k % 2 == 0:
                                wait_emptied(pe, f"xqT.{k // 2}")
                            last = pe.matmul(out_of(pr)[:], xqT[:, k, t * P:(t + 1) * P], w1q[:, k], start=(k == 0), stop=(k == KD - 1))
                        full(last, pr)
                    pe.wait_ge(w2_quant, 1)
                    bf16_transposes("hqT", hq, NT, KH // 2)
                    wait_emptied(pe, "hqT.0")
                    wait_emptied(pe, "hqT.1")
                    for t in range(NT):
                        for c in range(2):
                            pr = f"ffn_o.{t}.{c}"
                            wait_bank(pe, pr)
                            for k in range(KH):
                                last = pe.matmul(out_of(pr)[:], hqT[:, k, t * P:(t + 1) * P], w2q[:, k, c * HALF:(c + 1) * HALF],
                                                 start=(k == 0), stop=(k == KH - 1))
                            full(last, pr)
                if kind == "hop_row":
                    n = s[1]
                    pe.wait_ge(aij_ready, n + 1)
                    spread(f"ai.{n}", lambda t: aij[:, 0, t:t + 1])
                if kind == "hop_sum":
                    n = s[1]
                    pe.wait_ge(msg_ready, n + 1)
                    pe.wait_ge(g_ready, NT * (n + 1))
                    for c in range(NT):
                        pr = f"hop.{n}.{c}"
                        wait_bank(pe, pr)
                        cs = slice(c * P, (c + 1) * P)
                        full(products(out_of(pr)[:], [(lambda p, r=r: msg2[:, p, r, cs], lambda p, r=r: g2[:, p, r])
                                                      for r in range(NT)]), pr)
                if kind == "context":
                    pe.wait_ge(node_split, 6 * NT)
                    pe.wait_ge(v_ones, 1)
                    for b in range(3):
                        pr = f"context.{b}"
                        wait_bank(pe, pr)
                        for j in range(3 * b, min(3 * b + 3, KD)):
                            js = slice(j * P, (j + 1) * P)
                            o = out_of(pr)[:, 130 * (j % 3):130 * (j % 3) + 130]
                            for t in range(NT):
                                pe.matmul(o, k2n[:, HI, t, js], v_hi[:, t, j], start=(t == 0), stop=False)
                                pe.matmul(o[:, 0:P], k2n[:, HI, t, js], v_lo[:, t, j], start=False, stop=False)
                                last = pe.matmul(o, k2n[:, LO, t, js], v_hi[:, t, j], start=False, stop=(t == NT - 1))
                        full(last, pr)
                if kind == "queries":
                    pe.wait_ge(q_ready, sub_no("q", s[1] // 2, NT - 1))
                    for j in range(2 * s[1], 2 * s[1] + 2):
                        transposes(f"q1T.{j}", [qf[:, t, j * P:(j + 1) * P] for t in range(NT)])
                if kind == "y":
                    c = s[1]
                    for b in range(3):
                        wait_emptied(pe, f"context.{b}")
                    wait_emptied(pe, f"q1T.{4 * c + 2}")
                    wait_emptied(pe, f"q1T.{4 * c + 3}")
                    for b in range(NT + 1):
                        pr = f"yn.{c}.{b}"
                        wait_bank(pe, pr)
                        for n in range(3):
                            t, j = (b, 4 * c + n) if b < NT else (n, 4 * c + 3)
                            last = products(out_of(pr)[:, 130 * n:130 * n + 130],
                                            [(lambda p: TT["q1T"][:, p, j, t * P:(t + 1) * P], lambda p: ctx1[:, p, j])])
                        full(last, pr)
                if kind == "gate":
                    pe.wait_ge(gate_ready, 1)
                    wait_bank(pe, "logitsT")
                    full(products(out_of("logitsT")[:, 0:N], [(lambda p, k=k: gate2[:, p, k],
                                                               lambda p, k=k: TT["xn4"][:, p, k]) for k in range(KD)]), "logitsT")
                if kind == "gate_pick":
                    wait_emptied(pe, "logitsT")
                    transposes("logits", [lgT[:, t * P:(t + 1) * P] for t in range(NT)])
                if kind == "gate_rows":
                    pe.wait_ge(cw_ready, NT)
                    transposes("cwT", [cw[:, t] for t in range(NT)])
                    for e in range(EXPERTS):
                        spread(f"cw.{e}", lambda t: cw[:, t, e:e + 1])


def kernel(**inputs):
    import numpy as np
    import concourse.bacc as bacc
    from concourse.bass_utils import run_bass_kernel_spmd

    a = {k: np.asarray(v) for k, v in inputs.items()}

    def feature_major(w):
        k, m = w.shape
        return w.reshape(k // P, P, m // P, P).transpose(2, 1, 0, 3).reshape(-1, P, D)

    def node_major(w):
        k, m = w.shape
        return w.reshape(k // (2 * P), 2, P, m // HALF, HALF).transpose(3, 0, 2, 1, 4).reshape(m // HALF, k // (2 * P), P, D)

    packs = {"v1": feature_major(a["L0_gnn_wv"].T), "v2": node_major(a["L0_gnn_wiv"].T).reshape(-1, P, D),
             "mk": feature_major(a["L0_mix_Wk"]), "mv": node_major(a["L0_mix_Wv"])[0], "mq": node_major(a["L0_mix_Wq"])[0],
             "q1": feature_major(a["L0_gnn_wq"].T), "k1": feature_major(a["L0_gnn_wk"].T),
             "q2": feature_major(a["L0_gnn_wiq"].T), "k2": feature_major(a["L0_gnn_wik"].T),
             "wo": np.concatenate([node_major(a["L0_mix_Wo"]), node_major(a["L0_gnn_wo"].T)], axis=1).reshape(-1, P, D),
             "g1": node_major(a["L1_gnn_W1"])[0]}
    for n in "kvq":
        packs[n] = node_major(a[f"L1_mix_W{n}"]).reshape(-1, P, D)
    packs["wp"] = node_major(a["L1_mix_Wp"]).reshape(-1, P, D)
    packs["e1"] = np.concatenate([feature_major(a["L1_ffn_W1"][e]) for e in range(EXPERTS)])
    packs["e2"] = node_major(a["L1_ffn_W2"].reshape(EXPERTS * EHID, D)).reshape(-1, P, D)
    rows = {"biv": a["L0_gnn_biv"], "bo": a["L0_gnn_bo"], "mix_bo": a["L0_mix_bo"], "ffn_b1": a["L0_ffn_b1"],
            "ffn_b2": a["L0_ffn_b2"], "gnn_b1": a["L1_gnn_b1"], "bk": a["L1_mix_bk"], "bv": a["L1_mix_bv"],
            "bq": a["L1_mix_bq"], "bp": a["L1_mix_bp"]} | {f"wg{n}": a["L1_gnn_Wg"][n, :, 0] for n in range(HOPS)}
    arrays = {
        "weights": np.stack([packs[n][i] for n, i in UNITS]),
        "x_in": np.ascontiguousarray(a["x"]),
        "edges": np.ascontiguousarray(np.stack([a["src"], a["dst"], a["edge_type_5"]]).reshape(3, EC, P).transpose(2, 0, 1)),
        "rows": np.concatenate([rows[n] for n in ROW_ORDER]),
        "cols": np.ascontiguousarray(np.concatenate(
            [a[f"L0_gnn_{n}"].reshape(KD, P) for n in ("bv", "bq", "bk", "biq", "bik")]
            + [a["L1_ffn_b1"].reshape(EXPERTS * 2, P)]).T),
        "tiny": np.concatenate([a["L0_gnn_edge_type_weights"], a["L1_gnn_bg"][:, 0]]),
        "w1_in": np.ascontiguousarray(a["L0_ffn_w1"].T.reshape(KD, P, HID).transpose(1, 0, 2).reshape(P, -1)),
        "w2_in": np.ascontiguousarray(a["L0_ffn_w2"].T.reshape(KH, P, D).transpose(1, 0, 2).reshape(P, -1)),
        "gate_in": np.ascontiguousarray(a["L1_ffn_gate_W"].reshape(KD, P, EXPERTS).transpose(1, 0, 2).reshape(P, -1)),
        "eb2_in": np.ascontiguousarray(a["L1_ffn_b2"]),
    }
    nc = bacc.Bacc("TRN2", target_bir_lowering=False, num_devices=1)
    args = [nc.dram_tensor(n, v.shape, mybir.dt.from_np(v.dtype), kind="ExternalInput").ap() for n, v in arrays.items()]
    args.append(nc.dram_tensor("out", (N, D), F32, kind="ExternalOutput").ap())
    gps_kernel(nc, *args)
    return run_bass_kernel_spmd(nc, [arrays], core_ids=[0]).results[0]["out"]
```
